# Optimizing a Trainium2 kernel written in Bass

```python
import numpy as np
import jax
import jax.numpy as jnp

def _softmax(x, axis=-1):
    return jax.nn.softmax(x, axis=axis)

def _gelu(x):
    return jax.nn.gelu(x, approximate=True)

def _silu(x):
    return jax.nn.silu(x)

def _sigmoid(x):
    return jax.nn.sigmoid(x)

def _layernorm(x, axis=-1, eps=1e-05):
    m = jnp.mean(x, axis=axis, keepdims=True)
    v = jnp.var(x, axis=axis, keepdims=True)
    return (x - m) / jnp.sqrt(v + eps)

def _scatter_add(tgt, idx, src, axis=0):
    return tgt.at[idx].add(src)

def _segment_sum(src, seg, n):
    return jax.ops.segment_sum(src, seg, n)
kernel_name = 'mk_flamingo_gated_d4_seqx_r8_05b618'

def setup_inputs(seed: int=0):
    np.random.seed(seed)
    _w = jnp.asarray

    def _rec_inputs():
        import jax
        import jax.numpy as jnp
        _rk = jax.random.key(seed)
        x = 7.22e-05 + 1 * jax.random.normal(jax.random.fold_in(_rk, 1), (8, 128, 128), jnp.float32)
        _lenS = 128 - jax.random.randint(jax.random.fold_in(_rk, 7), (8,), 0, max(1, 128 // 4) + 1, jnp.int32)
        _lenS2 = 77 - jax.random.randint(jax.random.fold_in(_rk, 8), (8,), 0, max(1, 77 // 4) + 1, jnp.int32)
        _ctx_1024P = jax.random.normal(jax.random.fold_in(_rk, 11), (8, 16, 128), jnp.float32)
        _ctx_1024c = jax.random.dirichlet(jax.random.fold_in(_rk, 511), 0.3 * jnp.ones((16,), jnp.float32), (8, 77))
        _ctx_1024t = jnp.einsum('bsk,bkd->bsd', _ctx_1024c, _ctx_1024P)
        _ctx_1024t = _ctx_1024t * jax.lax.rsqrt(jnp.mean(jnp.square(_ctx_1024t)) + 1e-12) * 0.953939
        ctx_1024 = 4.13588e-05 + 0.999923 * (_ctx_1024t + 0.3 * jax.random.normal(jax.random.fold_in(_rk, 611), (8, 77, 128), jnp.float32))
        _validS = jnp.arange(128)[None, :] < _lenS[:, None]
        _validS2 = jnp.arange(77)[None, :] < _lenS2[:, None]
        _causal = jnp.tril(jnp.ones((128, 128), dtype=bool))
        mask_BxSxS2_ik0 = jnp.where(jnp.broadcast_to(_validS2[:, None, :], (8, 128, 77)), 0, 1).astype(jnp.int32)
        mask_BxS2_if1 = jnp.where(jnp.ones((8, 77), dtype=bool), 1, 0).astype(jnp.int32)
        _g = jax.random.normal(jax.random.fold_in(_rk, 9001), (2, 4), jnp.float32)
        _g = jnp.sign(_g) * jnp.maximum(jnp.abs(_g), 1.0) + (_g == 0) * 1.0
        g_xattn = _g[0]
        g_ffn = _g[1]
        return (x, ctx_1024, mask_BxSxS2_ik0, mask_BxS2_if1, g_xattn, g_ffn)
    x, ctx_1024, mask_BxSxS2_ik0, mask_BxS2_if1, g_xattn, g_ffn = _rec_inputs()

    def _L0_xattn_setup():
        import jax, jax.numpy as jnp
        import numpy as np
        INF = 1000000000.0
        N_HEAD, QK_DIM, V_DIM, D_MODEL = (16, 64, 64, 128)
        B, S = (4, 256)

        def rope(x):
            b, s, h, d = x.shape
            inv_freq = 1.0 / 10000.0 ** (jnp.arange(0, d, 2, dtype=jnp.float32) / d)
            ang = jnp.arange(s, dtype=jnp.float32)[:, None] * inv_freq
            cos = jnp.cos(ang)[None, :, None, :]
            sin = jnp.sin(ang)[None, :, None, :]
            x1, x2 = (x[..., 0::2], x[..., 1::2])
            out_even = x1 * cos - x2 * sin
            out_odd = x1 * sin + x2 * cos
            return jnp.stack([out_even, out_odd], axis=-1).reshape(x.shape)
        key = jax.random.key(seed)
        ks = jax.random.split(key, 8)
        q = jax.random.normal(ks[0], (B, S, D_MODEL), dtype=jnp.float32)
        k = jax.random.normal(ks[1], (B, S, D_MODEL), dtype=jnp.float32)
        v = jax.random.normal(ks[2], (B, S, D_MODEL), dtype=jnp.float32)
        sd = 1.0 / np.sqrt(D_MODEL)
        Wq = jax.random.normal(ks[3], (D_MODEL, N_HEAD * QK_DIM), dtype=jnp.float32) * sd
        Wk = jax.random.normal(ks[4], (D_MODEL, N_HEAD * QK_DIM), dtype=jnp.float32) * sd
        Wv = jax.random.normal(ks[5], (D_MODEL, N_HEAD * V_DIM), dtype=jnp.float32) * sd
        Wo = jax.random.normal(ks[6], (N_HEAD * V_DIM, D_MODEL), dtype=jnp.float32) * (1.0 / np.sqrt(N_HEAD * V_DIM))
        mask = jnp.broadcast_to(jnp.tril(jnp.ones((S, S), dtype=jnp.int32)), (B, S, S))
        return {'q': q, 'k': k, 'v': v, 'Wq': Wq, 'Wk': Wk, 'Wv': Wv, 'Wo': Wo, 'mask': mask}
    _L0_xattn_all = _L0_xattn_setup()
    _L0_xattn_in = {k: v for k, v in _L0_xattn_all.items() if k in ('Wq', 'Wk', 'Wv', 'Wo')}
    del _L0_xattn_all

    def _L0_ffn_setup():
        import math
        import jax, jax.numpy as jnp
        import numpy as np
        D_MODEL = 128
        D_HIDDEN = 256
        N_EXPERTS = 8
        TOP_K = 2
        CAPACITY_FACTOR = 1.25

        def _moe_forward(x, w_router, w_gate, w_down):
            B, T, D = x.shape
            N = B * T
            xf = x.reshape(N, D)
            logits = xf.astype(jnp.float32) @ w_router.T
            gates = jax.nn.softmax(logits, axis=-1)
            topk_gates, topk_idx = jax.lax.top_k(gates, TOP_K)
            expert_mask = jax.nn.one_hot(topk_idx, N_EXPERTS, dtype=jnp.int32).sum(axis=1)
            capacity = math.ceil(N / N_EXPERTS * CAPACITY_FACTOR)
            position_in_expert = jnp.cumsum(expert_mask, axis=0) - 1
            expert_mask = expert_mask * (position_in_expert < capacity)
            keep = jnp.take_along_axis(expert_mask, topk_idx, axis=1) > 0
            topk_gates = topk_gates * keep
            topk_gates = topk_gates / (topk_gates.sum(axis=-1, keepdims=True) + 1e-06)
            hidden = jax.nn.silu(xf @ w_gate.T)
            combine = (topk_gates[:, :, None] * jax.nn.one_hot(topk_idx, N_EXPERTS, dtype=topk_gates.dtype)).sum(axis=1)
            y = jnp.zeros((N, D), dtype=x.dtype)
            for e in range(N_EXPERTS):
                y = y + combine[:, e:e + 1] * (hidden @ w_down[e].T)
            return y.reshape(B, T, D)
        key = jax.random.key(seed)
        k0, k1, k2, k3 = jax.random.split(key, 4)
        B, T = (2, 256)
        x = jax.random.normal(k0, (B, T, D_MODEL), dtype=jnp.float32)
        w_router = jax.random.normal(k1, (N_EXPERTS, D_MODEL), dtype=jnp.float32) * 0.02
        w_gate = jax.random.normal(k2, (D_HIDDEN, D_MODEL), dtype=jnp.float32) * 0.02
        w_down = jax.random.normal(k3, (N_EXPERTS, D_MODEL, D_HIDDEN), dtype=jnp.float32) * 0.02
        return {'x': x, 'w_router': w_router, 'w_gate': w_gate, 'w_down': w_down}
    _L0_ffn_all = _L0_ffn_setup()
    _L0_ffn_in = {k: v for k, v in _L0_ffn_all.items() if k in ('w_router', 'w_gate', 'w_down')}
    del _L0_ffn_all

    def _L1_xattn_setup():
        import jax, jax.numpy as jnp
        import numpy as np
        DIM = 128
        HEADS = 16
        HEAD_DIM = 64
        INNER = HEADS * HEAD_DIM

        def _split_heads(t):
            b, n, _ = t.shape
            return t.reshape(b, n, HEADS, HEAD_DIM).transpose(0, 2, 1, 3)
        key = jax.random.key(seed)
        ks = jax.random.split(key, 7)
        b, n, m = (2, 256, 256)
        s = 0.02
        return {'x': jax.random.normal(ks[0], (b, n, DIM), dtype=jnp.float32), 'context': jax.random.normal(ks[1], (b, m, DIM), dtype=jnp.float32), 'w_kv': jax.random.normal(ks[2], (DIM, 2 * INNER), dtype=jnp.float32) * s, 'w_q': jax.random.normal(ks[3], (DIM, INNER), dtype=jnp.float32) * s, 'w_out1': jax.random.normal(ks[4], (INNER, DIM), dtype=jnp.float32) * s, 'w_out2': jax.random.normal(ks[5], (DIM, DIM), dtype=jnp.float32) * s, 'gamma': jnp.ones((DIM,), dtype=jnp.float32)}
    _L1_xattn_all = _L1_xattn_setup()
    _L1_xattn_in = {k: v for k, v in _L1_xattn_all.items() if k in ('w_kv', 'w_q', 'w_out1', 'w_out2', 'gamma')}
    del _L1_xattn_all

    def _L1_ffn_setup():
        import jax, jax.numpy as jnp
        import numpy as np
        D_MODEL = 128
        NUM_EXPERTS = 8
        TOP_K = 2
        B, S = (4, 256)
        key = jax.random.key(seed)
        ks = jax.random.split(key, 7)
        scale_in = 1.0 / np.sqrt(D_MODEL)
        scale_hid = 1.0 / np.sqrt(2 * D_MODEL)
        return {'x': jax.random.normal(ks[0], (B, S, D_MODEL), dtype=jnp.float32), 'Wg': jax.random.normal(ks[1], (D_MODEL, NUM_EXPERTS), dtype=jnp.float32) * scale_in, 'bg': jnp.zeros((NUM_EXPERTS,), dtype=jnp.float32), 'W1': jax.random.normal(ks[2], (NUM_EXPERTS, D_MODEL, 2 * D_MODEL), dtype=jnp.float32) * scale_in, 'b1': jnp.zeros((NUM_EXPERTS, 2 * D_MODEL), dtype=jnp.float32), 'W2': jax.random.normal(ks[3], (NUM_EXPERTS, 2 * D_MODEL, D_MODEL), dtype=jnp.float32) * scale_hid, 'b2': jnp.zeros((NUM_EXPERTS, D_MODEL), dtype=jnp.float32)}
    _L1_ffn_all = _L1_ffn_setup()
    _L1_ffn_in = {k: v for k, v in _L1_ffn_all.items() if k in ('Wg', 'bg', 'W1', 'b1', 'W2', 'b2')}
    del _L1_ffn_all

    def _L2_xattn_setup():
        import jax, jax.numpy as jnp
        import numpy as np
        B, L_ENC, L_DEC, D = (16, 64, 128, 128)
        key = jax.random.key(seed)
        k1, k2, k3, k4, k5, k6 = jax.random.split(key, 6)
        encoder_hc = jax.random.normal(k1, (B, L_ENC, D), dtype=jnp.float32)
        decoder_hq = jax.random.normal(k2, (B, L_DEC, D), dtype=jnp.float32)
        w_sim = jax.random.normal(k3, (3 * D,), dtype=jnp.float32) * 0.02
        b_sim = jax.random.normal(k4, (1,), dtype=jnp.float32) * 0.02
        W_qv = jax.random.normal(k5, (4 * D, D), dtype=jnp.float32) * 0.02
        b_qv = jax.random.normal(k6, (D,), dtype=jnp.float32) * 0.02
        return {'encoder_hc': encoder_hc, 'decoder_hq': decoder_hq, 'w_sim': w_sim, 'b_sim': b_sim, 'W_qv': W_qv, 'b_qv': b_qv}
    _L2_xattn_all = _L2_xattn_setup()
    _L2_xattn_in = {k: v for k, v in _L2_xattn_all.items() if k in ('w_sim', 'b_sim', 'W_qv', 'b_qv')}
    del _L2_xattn_all

    def _L2_ffn_setup():
        import jax, jax.numpy as jnp
        import numpy as np
        NUM_EXPERTS = 8
        TOP_K = 2
        D = 128
        H = 4 * D
        B, S = (4, 256)
        key = jax.random.key(seed)
        ks = jax.random.split(key, 8)
        s = 0.02
        return {'x': jax.random.normal(ks[0], (B, S, D), dtype=jnp.float32), 'gate_w': jax.random.normal(ks[1], (NUM_EXPERTS, D), dtype=jnp.float32) * s, 'gate_b': jnp.zeros((NUM_EXPERTS,), dtype=jnp.float32), 'w1': jax.random.normal(ks[2], (NUM_EXPERTS, D, H), dtype=jnp.float32) * s, 'b1': jnp.zeros((NUM_EXPERTS, H), dtype=jnp.float32), 'w2': jax.random.normal(ks[3], (NUM_EXPERTS, H, D), dtype=jnp.float32) * s, 'b2': jnp.zeros((NUM_EXPERTS, D), dtype=jnp.float32)}
    _L2_ffn_all = _L2_ffn_setup()
    _L2_ffn_in = {k: v for k, v in _L2_ffn_all.items() if k in ('gate_w', 'gate_b', 'w1', 'b1', 'w2', 'b2')}
    del _L2_ffn_all

    def _L3_xattn_setup():
        import jax, jax.numpy as jnp
        import numpy as np
        D_MODEL = 128
        N_HEADS = 16
        D_HEAD = D_MODEL // N_HEADS
        NEG_INF = jnp.float32(-1e+30)
        key = jax.random.key(seed)
        kq, kk, kv, kwq, kwk, kwv, kwo = jax.random.split(key, 7)
        B, L = (4, 256)
        s = 1.0 / np.sqrt(D_MODEL)
        return {'query': jax.random.normal(kq, (B, L, D_MODEL), jnp.float32), 'key': jax.random.normal(kk, (B, L, D_MODEL), jnp.float32), 'value': jax.random.normal(kv, (B, L, D_MODEL), jnp.float32), 'attention_mask': jnp.ones((B, L), jnp.int32), 'Wq': jax.random.normal(kwq, (D_MODEL, D_MODEL), jnp.float32) * s, 'Wk': jax.random.normal(kwk, (D_MODEL, D_MODEL), jnp.float32) * s, 'Wv': jax.random.normal(kwv, (D_MODEL, D_MODEL), jnp.float32) * s, 'Wo': jax.random.normal(kwo, (D_MODEL, D_MODEL), jnp.float32) * s}
    _L3_xattn_all = _L3_xattn_setup()
    _L3_xattn_in = {k: v for k, v in _L3_xattn_all.items() if k in ('Wq', 'Wk', 'Wv', 'Wo')}
    del _L3_xattn_all

    def _L3_ffn_setup():
        import jax, jax.numpy as jnp
        import numpy as np
        B, S, D, F, E = (4, 256, 128, 512, 8)
        LN_EPS = 1e-05
        key = jax.random.key(seed)
        ks = jax.random.split(key, 6)
        sc = 0.02
        return {'x': jax.random.normal(ks[0], (B, S, D), dtype=jnp.float32), 'Wr': jax.random.normal(ks[1], (D, E), dtype=jnp.float32) * sc, 'br': jnp.zeros((E,), jnp.float32), 'ln_g': jnp.ones((D,), jnp.float32), 'ln_b': jnp.zeros((D,), jnp.float32), 'W1': jax.random.normal(ks[2], (E, D, F), dtype=jnp.float32) * sc, 'b1': jnp.zeros((E, F), jnp.float32), 'W2': jax.random.normal(ks[3], (E, F, D), dtype=jnp.float32) * sc, 'b2': jnp.zeros((E, D), jnp.float32)}
    _L3_ffn_all = _L3_ffn_setup()
    _L3_ffn_in = {k: v for k, v in _L3_ffn_all.items() if k in ('Wr', 'br', 'ln_g', 'ln_b', 'W1', 'b1', 'W2', 'b2')}
    del _L3_ffn_all
    return {'x': x, 'ctx_1024': ctx_1024, 'mask_BxSxS2_ik0': mask_BxSxS2_ik0, 'mask_BxS2_if1': mask_BxS2_if1, 'g_xattn': g_xattn, 'g_ffn': g_ffn, 'L0_xattn_Wq': _L0_xattn_in['Wq'], 'L0_xattn_Wk': _L0_xattn_in['Wk'], 'L0_xattn_Wv': _L0_xattn_in['Wv'], 'L0_xattn_Wo': _L0_xattn_in['Wo'], 'L0_ffn_w_router': _L0_ffn_in['w_router'], 'L0_ffn_w_gate': _L0_ffn_in['w_gate'], 'L0_ffn_w_down': _L0_ffn_in['w_down'], 'L1_xattn_w_kv': _L1_xattn_in['w_kv'], 'L1_xattn_w_q': _L1_xattn_in['w_q'], 'L1_xattn_w_out1': _L1_xattn_in['w_out1'], 'L1_xattn_w_out2': _L1_xattn_in['w_out2'], 'L1_xattn_gamma': _L1_xattn_in['gamma'], 'L1_ffn_Wg': _L1_ffn_in['Wg'], 'L1_ffn_bg': _L1_ffn_in['bg'], 'L1_ffn_W1': _L1_ffn_in['W1'], 'L1_ffn_b1': _L1_ffn_in['b1'], 'L1_ffn_W2': _L1_ffn_in['W2'], 'L1_ffn_b2': _L1_ffn_in['b2'], 'L2_xattn_w_sim': _L2_xattn_in['w_sim'], 'L2_xattn_b_sim': _L2_xattn_in['b_sim'], 'L2_xattn_W_qv': _L2_xattn_in['W_qv'], 'L2_xattn_b_qv': _L2_xattn_in['b_qv'], 'L2_ffn_gate_w': _L2_ffn_in['gate_w'], 'L2_ffn_gate_b': _L2_ffn_in['gate_b'], 'L2_ffn_w1': _L2_ffn_in['w1'], 'L2_ffn_b1': _L2_ffn_in['b1'], 'L2_ffn_w2': _L2_ffn_in['w2'], 'L2_ffn_b2': _L2_ffn_in['b2'], 'L3_xattn_Wq': _L3_xattn_in['Wq'], 'L3_xattn_Wk': _L3_xattn_in['Wk'], 'L3_xattn_Wv': _L3_xattn_in['Wv'], 'L3_xattn_Wo': _L3_xattn_in['Wo'], 'L3_ffn_Wr': _L3_ffn_in['Wr'], 'L3_ffn_br': _L3_ffn_in['br'], 'L3_ffn_ln_g': _L3_ffn_in['ln_g'], 'L3_ffn_ln_b': _L3_ffn_in['ln_b'], 'L3_ffn_W1': _L3_ffn_in['W1'], 'L3_ffn_b1': _L3_ffn_in['b1'], 'L3_ffn_W2': _L3_ffn_in['W2'], 'L3_ffn_b2': _L3_ffn_in['b2']}

def reference(x, ctx_1024, mask_BxSxS2_ik0, mask_BxS2_if1, g_xattn, g_ffn, L0_xattn_Wq, L0_xattn_Wk, L0_xattn_Wv, L0_xattn_Wo, L0_ffn_w_router, L0_ffn_w_gate, L0_ffn_w_down, L1_xattn_w_kv, L1_xattn_w_q, L1_xattn_w_out1, L1_xattn_w_out2, L1_xattn_gamma, L1_ffn_Wg, L1_ffn_bg, L1_ffn_W1, L1_ffn_b1, L1_ffn_W2, L1_ffn_b2, L2_xattn_w_sim, L2_xattn_b_sim, L2_xattn_W_qv, L2_xattn_b_qv, L2_ffn_gate_w, L2_ffn_gate_b, L2_ffn_w1, L2_ffn_b1, L2_ffn_w2, L2_ffn_b2, L3_xattn_Wq, L3_xattn_Wk, L3_xattn_Wv, L3_xattn_Wo, L3_ffn_Wr, L3_ffn_br, L3_ffn_ln_g, L3_ffn_ln_b, L3_ffn_W1, L3_ffn_b1, L3_ffn_W2, L3_ffn_b2):
    import jax
    import jax.numpy as jnp

    def _L0_xattn_ref(q, k, v, Wq, Wk, Wv, Wo, mask):
        import jax, jax.numpy as jnp
        import numpy as np
        INF = 1000000000.0
        N_HEAD, QK_DIM, V_DIM, D_MODEL = (16, 64, 64, 128)
        B, S = (4, 256)

        def rope(x):
            b, s, h, d = x.shape
            inv_freq = 1.0 / 10000.0 ** (jnp.arange(0, d, 2, dtype=jnp.float32) / d)
            ang = jnp.arange(s, dtype=jnp.float32)[:, None] * inv_freq
            cos = jnp.cos(ang)[None, :, None, :]
            sin = jnp.sin(ang)[None, :, None, :]
            x1, x2 = (x[..., 0::2], x[..., 1::2])
            out_even = x1 * cos - x2 * sin
            out_odd = x1 * sin + x2 * cos
            return jnp.stack([out_even, out_odd], axis=-1).reshape(x.shape)
        b, ql, _ = q.shape
        kl = k.shape[1]
        Q = (q @ Wq).reshape(b, ql, N_HEAD, QK_DIM)
        K = (k @ Wk).reshape(b, kl, N_HEAD, QK_DIM)
        V = (v @ Wv).reshape(b, kl, N_HEAD, V_DIM)
        Q, K = (rope(Q), rope(K))
        scale = QK_DIM ** 0.5
        attn = jnp.einsum('bqhd,bkhd->bhqk', Q / scale, K)
        attn = jnp.where(mask[:, None, :, :] == 0, -INF, attn)
        attn = jax.nn.softmax(attn, axis=-1)
        out = jnp.einsum('bhqk,bkhd->bqhd', attn, V).reshape(b, ql, N_HEAD * V_DIM)
        return out @ Wo

    def _L0_ffn_ref(x, w_router, w_gate, w_down):
        import math
        import jax, jax.numpy as jnp
        import numpy as np
        D_MODEL = 128
        D_HIDDEN = 256
        N_EXPERTS = 8
        TOP_K = 2
        CAPACITY_FACTOR = 1.25

        def _moe_forward(x, w_router, w_gate, w_down):
            B, T, D = x.shape
            N = B * T
            xf = x.reshape(N, D)
            logits = xf.astype(jnp.float32) @ w_router.T
            gates = jax.nn.softmax(logits, axis=-1)
            topk_gates, topk_idx = jax.lax.top_k(gates, TOP_K)
            expert_mask = jax.nn.one_hot(topk_idx, N_EXPERTS, dtype=jnp.int32).sum(axis=1)
            capacity = math.ceil(N / N_EXPERTS * CAPACITY_FACTOR)
            position_in_expert = jnp.cumsum(expert_mask, axis=0) - 1
            expert_mask = expert_mask * (position_in_expert < capacity)
            keep = jnp.take_along_axis(expert_mask, topk_idx, axis=1) > 0
            topk_gates = topk_gates * keep
            topk_gates = topk_gates / (topk_gates.sum(axis=-1, keepdims=True) + 1e-06)
            hidden = jax.nn.silu(xf @ w_gate.T)
            combine = (topk_gates[:, :, None] * jax.nn.one_hot(topk_idx, N_EXPERTS, dtype=topk_gates.dtype)).sum(axis=1)
            y = jnp.zeros((N, D), dtype=x.dtype)
            for e in range(N_EXPERTS):
                y = y + combine[:, e:e + 1] * (hidden @ w_down[e].T)
            return y.reshape(B, T, D)
        return _moe_forward(x, w_router, w_gate, w_down)

    def _L1_xattn_ref(x, context, w_kv, w_q, w_out1, w_out2, gamma):
        import jax, jax.numpy as jnp
        import numpy as np
        DIM = 128
        HEADS = 16
        HEAD_DIM = 64
        INNER = HEADS * HEAD_DIM

        def _split_heads(t):
            b, n, _ = t.shape
            return t.reshape(b, n, HEADS, HEAD_DIM).transpose(0, 2, 1, 3)
        scale = HEAD_DIM ** (-0.5)
        kv = context @ w_kv
        k, v = jnp.split(kv, 2, axis=-1)
        q = _split_heads(x @ w_q)
        k = _split_heads(k)
        v = _split_heads(v)
        dots = jnp.einsum('bhid,bhjd->bhij', q, k) * scale
        attn = jax.nn.softmax(dots, axis=-1)
        out = jnp.einsum('bhij,bhjd->bhid', attn, v)
        b, h, n, d = out.shape
        out = out.transpose(0, 2, 1, 3).reshape(b, n, h * d)
        out = jax.nn.relu(out @ w_out1) @ w_out2
        mean = jnp.mean(out, axis=-1, keepdims=True)
        var = jnp.var(out, axis=-1, keepdims=True)
        return (out - mean) * jax.lax.rsqrt(var + 1e-05) * gamma

    def _L1_ffn_ref(x, Wg, bg, W1, b1, W2, b2):
        import jax, jax.numpy as jnp
        import numpy as np
        D_MODEL = 128
        NUM_EXPERTS = 8
        TOP_K = 2
        B, S = (4, 256)
        Bb, Ss, D = x.shape
        E = Wg.shape[1]
        xf = x.reshape(-1, D)
        logits = xf @ Wg + bg
        probs = jax.nn.softmax(logits, axis=-1)
        w, idx = jax.lax.top_k(probs, TOP_K)
        w = w / jnp.sum(w, axis=-1, keepdims=True)
        comb = jnp.sum(jax.nn.one_hot(idx, E, dtype=xf.dtype) * w[..., None], axis=1)
        h = jax.nn.relu(jnp.einsum('nd,edh->enh', xf, W1) + b1[:, None, :])
        y = jnp.einsum('enh,ehd->end', h, W2) + b2[:, None, :]
        out = jnp.einsum('end,ne->nd', y, comb)
        return out.reshape(Bb, Ss, D)

    def _L2_xattn_ref(encoder_hc, decoder_hq, w_sim, b_sim, W_qv, b_qv):
        import jax, jax.numpy as jnp
        import numpy as np
        B, L_ENC, L_DEC, D = (16, 64, 128, 128)
        d = encoder_hc.shape[-1]
        w1, w2, w3 = (w_sim[:d], w_sim[d:2 * d], w_sim[2 * d:])
        Sim = (encoder_hc @ w1)[:, :, None] + (decoder_hq @ w2)[:, None, :] + jnp.einsum('bid,bjd->bij', encoder_hc * w3, decoder_hq) + b_sim[0]
        A = jax.nn.softmax(Sim, axis=2)
        hq_hat = jnp.einsum('bij,bjd->bid', A, decoder_hq)
        Batt = jax.nn.softmax(jnp.max(Sim, axis=2), axis=1)
        hc_bar = jnp.einsum('bi,bid->bd', Batt, encoder_hc)[:, None, :]
        hc_hat = jnp.broadcast_to(hc_bar, encoder_hc.shape)
        feats = jnp.concatenate([encoder_hc, hq_hat, encoder_hc * hq_hat, encoder_hc * hc_hat], axis=-1)
        hcq = feats @ W_qv + b_qv
        return hcq

    def _L2_ffn_ref(x, gate_w, gate_b, w1, b1, w2, b2):
        import jax, jax.numpy as jnp
        import numpy as np
        NUM_EXPERTS = 8
        TOP_K = 2
        D = 128
        H = 4 * D
        B, S = (4, 256)
        orig_shape = x.shape
        xf = x.reshape(-1, orig_shape[-1])
        gates = xf @ gate_w.T + gate_b
        weights, indices = jax.lax.top_k(gates, TOP_K)
        weights = jax.nn.softmax(weights, axis=-1)
        out = jnp.zeros_like(xf)
        for e in range(NUM_EXPERTS):
            w_e = jnp.sum(weights * (indices == e), axis=-1, keepdims=True)
            h = jax.nn.gelu(xf @ w1[e] + b1[e], approximate=False)
            out = out + w_e * (h @ w2[e] + b2[e])
        return out.reshape(orig_shape)

    def _L3_xattn_ref(query, key, value, attention_mask, Wq, Wk, Wv, Wo):
        import jax, jax.numpy as jnp
        import numpy as np
        D_MODEL = 128
        N_HEADS = 16
        D_HEAD = D_MODEL // N_HEADS
        NEG_INF = jnp.float32(-1e+30)
        B, Lq, D = query.shape
        Lk = key.shape[1]

        def split_heads(x, W, L):
            return (x @ W.T).reshape(B, L, N_HEADS, D_HEAD).transpose(0, 2, 1, 3)
        q = split_heads(query, Wq, Lq)
        k = split_heads(key, Wk, Lk)
        v = split_heads(value, Wv, Lk)
        scores = jnp.einsum('bhqd,bhkd->bhqk', q, k) / jnp.sqrt(jnp.float32(D_HEAD))
        causal = jnp.triu(jnp.ones((Lq, Lk), bool), k=1)
        scores = jnp.where(causal[None, None], NEG_INF, scores)
        key_valid = attention_mask.astype(bool)[:, None, None, :]
        scores = jnp.where(key_valid, scores, NEG_INF)
        attn = jax.nn.softmax(scores, axis=-1)
        ctx = jnp.einsum('bhqk,bhkd->bhqd', attn, v)
        ctx = ctx.transpose(0, 2, 1, 3).reshape(B, Lq, D)
        return ctx @ Wo.T

    def _L3_ffn_ref(x, Wr, br, ln_g, ln_b, W1, b1, W2, b2):
        import jax, jax.numpy as jnp
        import numpy as np
        B, S, D, F, E = (4, 256, 128, 512, 8)
        LN_EPS = 1e-05
        tokens_shape = x.shape[:-1]
        xt = x.reshape(-1, x.shape[-1])
        router_logits = xt @ Wr + br
        router_probs = jax.nn.softmax(router_logits, axis=-1)
        gates = jnp.max(router_probs, axis=-1, keepdims=True)
        idx = jnp.argmax(router_probs, axis=-1)
        onehot = jax.nn.one_hot(idx, E, dtype=xt.dtype)
        mu = jnp.mean(xt, axis=-1, keepdims=True)
        var = jnp.mean(jnp.square(xt - mu), axis=-1, keepdims=True)
        xn = (xt - mu) * jax.lax.rsqrt(var + LN_EPS) * ln_g + ln_b
        h = jnp.einsum('te,td,edf->tf', onehot, xn, W1) + b1[idx]
        h = jax.nn.relu(h)
        y = jnp.einsum('te,tf,efd->td', onehot, h, W2) + b2[idx]
        y = y * gates
        return y.reshape(tokens_shape + (y.shape[-1],))
    x = x + jnp.tanh(g_xattn[0]) * _L0_xattn_ref(_layernorm(x, axis=-1), ctx_1024, ctx_1024, L0_xattn_Wq, L0_xattn_Wk, L0_xattn_Wv, L0_xattn_Wo, mask_BxSxS2_ik0)
    x = x + jnp.tanh(g_ffn[0]) * _L0_ffn_ref(_layernorm(x, axis=-1), L0_ffn_w_router, L0_ffn_w_gate, L0_ffn_w_down)
    x = x + jnp.tanh(g_xattn[1]) * _L1_xattn_ref(_layernorm(x, axis=-1), ctx_1024, L1_xattn_w_kv, L1_xattn_w_q, L1_xattn_w_out1, L1_xattn_w_out2, L1_xattn_gamma)
    x = x + jnp.tanh(g_ffn[1]) * _L1_ffn_ref(_layernorm(x, axis=-1), L1_ffn_Wg, L1_ffn_bg, L1_ffn_W1, L1_ffn_b1, L1_ffn_W2, L1_ffn_b2)
    x = x + jnp.tanh(g_xattn[2]) * _L2_xattn_ref(_layernorm(x, axis=-1), ctx_1024, L2_xattn_w_sim, L2_xattn_b_sim, L2_xattn_W_qv, L2_xattn_b_qv)
    x = x + jnp.tanh(g_ffn[2]) * _L2_ffn_ref(_layernorm(x, axis=-1), L2_ffn_gate_w, L2_ffn_gate_b, L2_ffn_w1, L2_ffn_b1, L2_ffn_w2, L2_ffn_b2)
    x = x + jnp.tanh(g_xattn[3]) * _L3_xattn_ref(_layernorm(x, axis=-1), ctx_1024, ctx_1024, mask_BxS2_if1, L3_xattn_Wq, L3_xattn_Wk, L3_xattn_Wv, L3_xattn_Wo)
    x = x + jnp.tanh(g_ffn[3]) * _L3_ffn_ref(_layernorm(x, axis=-1), L3_ffn_Wr, L3_ffn_br, L3_ffn_ln_g, L3_ffn_ln_b, L3_ffn_W1, L3_ffn_b1, L3_ffn_W2, L3_ffn_b2)
    return x

_drawn_inputs = setup_inputs


def setup_inputs(seed=0):
    import zlib

    import numpy as np

    out = dict(_drawn_inputs(seed))
    spreads = {'L1_xattn_gamma': (1.0, 0.2),
     'L1_ffn_bg': (0.0, 0.1),
     'L1_ffn_b1': (0.0, 0.1),
     'L1_ffn_b2': (0.0, 0.1),
     'L2_ffn_gate_b': (0.0, 0.1),
     'L2_ffn_b1': (0.0, 0.8),
     'L2_ffn_b2': (0.0, 0.1),
     'L3_ffn_br': (0.0, 0.8),
     'L3_ffn_ln_g': (1.0, 0.6),
     'L3_ffn_ln_b': (0.0, 0.8),
     'L3_ffn_b1': (0.0, 0.8),
     'L3_ffn_b2': (0.0, 0.8)}
    factors = {'g_ffn': 36.368,
     'L0_ffn_w_router': 2.921,
     'L2_xattn_w_sim': 4.646,
     'L2_xattn_b_qv': 4.935,
     'L2_ffn_w1': 3.246,
     'L2_ffn_w2': 2.994,
     'L3_ffn_Wr': 5.059,
     'L3_ffn_W1': 8.0,
     'L3_ffn_W2': 7.336}
    for name, (base, spread) in spreads.items():
        noise = np.random.default_rng([zlib.crc32(name.encode()), seed]).standard_normal(out[name].shape)
        drawn = base * np.exp(spread * noise) if base else spread * noise
        out[name] = jnp.asarray(drawn.astype(out[name].dtype))
    for name, factor in factors.items():
        out[name] = (out[name] * factor).astype(out[name].dtype)
    return out
```

```python
from contextlib import ExitStack

import concourse.bass as bass
from concourse import mybir

F32 = mybir.dt.float32
I32 = mybir.dt.int32
ALU = mybir.AluOpType
ACT = mybir.ActivationFunctionType
AX_X = mybir.AxisListType.X

B = 8
S = 128
D = 128
K = 77
H = 16
G = 4
NG = H // G
E = 8
HALF = 4 * S
UNITS = 2 * E
CAPACITY = 160
NEG = -1.0e30
EPS = 1e-5
LAYERS = 4


class Chain:

    def __init__(self, eng, sem):
        self.eng, self.sem, self.base, self.n = eng, sem, 0, 0

    def at(self, base):
        self.base, self.n = base, 0

    def __call__(self, instruction):
        instruction.then_inc(self.sem, 1)
        self.n += 1
        self.eng.wait_ge(self.sem, self.base + self.n)


def positive(value):
    return not isinstance(value, int) or value > 0


class Attention:

    BANK = {"S": (0, 1), "T": (2, 3), "A": (4, 5), "F": (6, 7), "R": (6, 7), "Z": (5, 5), "Y": (4, 4)}

    def __init__(self, fills, dh, scale, masked, hidden, start):
        self.fills, self.dh, self.scale, self.masked = fills, dh, scale, masked
        self.wide = dh == 64
        order = "S0 F S1 F T0 F A0 S2 F T1 F A1 S3 F T2 F A2 R0 T3 F A3 F R1 Z0 Y0".split()
        if not self.wide:
            order.remove("R1")
            order.remove("R0")
            order.insert(-2, "R0")
        if not hidden:
            order.remove("Z0")
        left, places = list(range(len(fills))), order.count("F")
        self.slots = []
        for name in order:
            if name == "F":
                share = -(-len(left) // places) if len(left) > places else min(1, len(left))
                self.slots += [("F", left.pop(0)) for _ in range(share)]
                places -= 1
            else:
                self.slots.append((name[0], int(name[1])))
        self.start = list(start)
        self.first = [sum(self.bank(("F", f)) == k for f in range(len(fills))) for k in range(8)]
        self.each = [sum(self.bank(s) == k for s in self.slots) for k in range(8)]

    def bank(self, slot):
        return self.BANK[slot[0]][slot[1] % 2]

    def use(self, slot, b, more=True):
        bank = self.bank(slot)
        earlier = [s for s in self.slots[:self.slots.index(slot)] if self.bank(s) == bank and (more or s[0] != "F")]
        return bank, b * self.each[bank] + self.start[bank] + self.first[bank] + len(earlier)

    def projection(self, f, b):
        bank = self.bank(("F", f))
        if isinstance(b, int) and b == 0:
            return bank, self.start[bank] + f // 2
        return self.use(("F", f), b - 1)

    def end(self):
        last = [sum(self.bank(s) == k for s in self.slots if s[0] != "F") for k in range(8)]
        return [self.start[k] + self.first[k] + (B - 1) * self.each[k] + last[k] for k in range(8)]


PROJECTIONS = {
    0: [("v", 0), ("q", 0), ("qs", 0), ("k", 0), ("ks", 0), ("q", 1), ("qs", 1), ("k", 1), ("ks", 1), ("v", 1)],
    1: [("v", 0), ("q", 0), ("k", 0), ("q", 1), ("k", 1), ("v", 1)],
    3: [("qk", 0), ("v", 0)],
}
HIDDEN_BLOCKS = {0: 2, 1: 2, 2: 4, 3: 4}
SHARED = 0


def build(nc, A, out):
    ctx = ExitStack()
    with ctx:
        def sb(name, shape, dt=F32):
            return ctx.enter_context(nc.sbuf_tensor(name, shape, dt))

        sems = {}

        def sem(name):
            if name not in sems:
                sems[name] = ctx.enter_context(nc.semaphore(name))
            return sems[name]

        P = [ctx.enter_context(nc.psum_tensor(f"bank{i}", [128, 512], F32)) for i in range(8)]

        x = sb("x", [S, B, D])
        xn = sb("xn", [S, B, D])
        xnT = sb("xnT", [D, B, S])
        cx = sb("cx", [K, B, D])
        cxT = sb("cxT", [D, B, K])
        ident = sb("ident", [128, 128])
        ones = sb("ones", [128, 128])
        upper = sb("upper", [128, 128])
        gates = sb("gates", [128, 8])
        tg = sb("tg", [128, 8])
        half = sb("half", [128, 8])
        stats = sb("stats", [128, B, 6])
        mv = sb("mv", [128, B, 2])
        ve = sb("ve", [128, B])
        rstd = sb("rstd", [128, B])

        w = {}
        for n in ("L0q", "L0qs", "L0k", "L0ks", "L0v", "L0o", "L1q", "L1k", "L1v", "L1o"):
            w[n] = sb(n, [D, H * 64])
        for n in ("L1o2", "L3q", "L3k", "L3v", "L3o"):
            w[n] = sb(n, [D, D])
        gamma = sb("gamma", [128, D])
        cos = sb("cos", [128, S])
        sin = sb("sin", [128, S])
        headmask = sb("headmask", [128, H])
        maskI = sb("maskI", [S, B, K], I32)
        bias0 = sb("bias0", [S, B, K])
        validI = sb("validI", [128, B, K], I32)
        bias3 = sb("bias3", [S, B, K])
        causal = sb("causal", [S, K])
        wsim = sb("wsim", [D, 3])
        bsim = sb("bsim", [128, 1])
        wqv = sb("wqv", [D, 4, D])
        bqv = sb("bqv", [1, D])

        qT = [sb(f"qT{j}", [128, 8, S]) for j in range(2)]
        kM = [sb(f"kM{j}", [128, H, K]) for j in range(2)]
        va = [sb(f"va{j}", [K, H, 65]) for j in range(2)]
        va8 = [sb(f"va8{j}", [K, H, 9]) for j in range(2)]
        cb = [sb(f"cb{j}", [D, K]) for j in range(2)]
        k3 = sb("k3", [128, K])
        rope = [sb(f"rope{j}", [128, 2, 4, S]) for j in range(2)]
        sc = sb("sc", [S, NG, G, K])
        pr = sb("pr", [S, NG, G, K])
        pT = [sb(f"pT{j}", [K, G, S]) for j in range(2)]
        mx = sb("mx", [S, NG, G])
        rc = sb("rc", [S, NG, G])
        on = sb("on", [S, H * 64])
        oT = sb("oT", [128, 8, S])
        zT = sb("zT", [D, S])
        yb = sb("yb", [S, B, D])

        wr = {n: sb(f"wr{n}", [D, E]) for n in range(4)}
        br = {n: sb(f"br{n}", [128, E]) for n in (1, 2, 3)}
        b2 = {n: sb(f"b2{n}", [E, D]) for n in (1, 2, 3)}
        wg = sb("wg", [D, 2 * 128])
        NB = {0: 2, 1: 2, 2: 4, 3: 4}
        row = {0: 2 * D, 1: 256 + 2 * D + 2, 2: 512 + 4 * D + 4, 3: 512 + 4 * D + 4}
        we = {n: [sb(f"we{n}{j}", [128, row[n]]) for j in range(2)] for n in range(4)}
        hT = [sb(f"hT{j}", [128, 4, HALF]) for j in range(2)]
        lng = sb("lng", [D, 2])
        small = {n: sb(f"r_{n}", [128, B, E]) for n in
                 ("L", "L2", "ex", "eq", "one1", "one2", "pri", "cb", "m")}
        col = {n: sb(f"c_{n}", [128, B]) for n in ("m1", "m2", "z", "rz", "km", "s")}
        combT = sb("combT", [E, B, S])
        c3 = sb("c3", [D, B, K])
        c2 = sb("c2", [D, B, K])
        aT = [sb(f"aT{j}", [K, S]) for j in range(2)]
        fq = sb("fq", [D, B, S])
        fm = sb("fm", [D, B, S])
        fc = sb("fc", [D, B, S])
        sim = sb("sim", [S, B, K])
        m8 = sb("m8", [S, B])
        nm8 = sb("nm8", [S, B])
        z8 = sb("z8", [S, B])
        mT = sb("mT", [B, S])
        row1 = sb("row1", [B, 4])
        bT = sb("bT", [S, B])
        hc = sb("hc", [D, B])

        filled = [sem(f"filled{i}") for i in range(8)]
        taken = [sem(f"taken{i}") for i in range(8)]
        uses, count, attn, ffn = {}, [0] * 8, {}, {}

        def plan_use(key, bank):
            uses[key] = (bank, count[bank])
            count[bank] += 1

        for b in range(B):
            plan_use(("cx", b), b)
        for n in range(4):
            for c_ in range(2):
                plan_use(("turn", f"a{n}", c_), 6 + c_)
            if n == 2:
                for b in range(B):
                    plan_use(("sim", b), b % 2)
                    plan_use(("aT", b), 2 + b % 2)
                    plan_use(("hq", b), 4 + b % 2)
                plan_use("mT", 6)
                plan_use("bT", 7)
                plan_use("hc", 6)
                for b in range(B):
                    plan_use(("feat", b), 6 + b % 2)
            else:
                attn[n] = Attention(PROJECTIONS[n], 8 if n == 3 else 64, 8.0 ** -0.5 if n == 3 else 64.0 ** -0.5,
                                    n != 1, n == 1, count)
                count[:] = attn[n].end()
            for c_ in range(2):
                plan_use(("turn", f"f{n}", c_), 6 + c_)
            plan_use(("logits", n), 6)
            if n == 3:
                for c_ in range(2):
                    plan_use(("turn", "i3", c_), 6 + c_)
            if n == SHARED:
                plan_use("rank", 7)
            else:
                plan_use(("combT", n, 0), 6)
                plan_use(("combT", n, 1), 7)
            ffn[n] = list(count)
            if n == SHARED:
                for k in range(4):
                    count[k] += 1
            else:
                for k in range(4):
                    count[k] += UNITS if HIDDEN_BLOCKS[n] == 4 else UNITS // 2
            count[4] += UNITS // 2
            count[5] += UNITS // 2
            if n != SHARED:
                plan_use(("b2", n, 0), 4)
                plan_use(("b2", n, 1), 5)

        def hidden_use(n, i, q, nb):
            if HIDDEN_BLOCKS[n] == 4:
                return nb, 4 * i + (ffn[n][nb] + q)
            bank = 2 * (q % 2) + nb
            return bank, 2 * i + (ffn[n][bank] + q // 2)

        def out_use(n, i, q):
            return 4 + q % 2, 2 * i + (ffn[n][4 + q % 2] + q // 2)

        def fill(pe, use):
            if positive(use[1]):
                pe.wait_ge(taken[use[0]], use[1])
            return P[use[0]]

        def read(eng, use):
            eng.wait_ge(filled[use[0]], use[1] + 1)
            return P[use[0]]

        def after(eng, use):
            eng.wait_ge(taken[use[0]], use[1] + 1)

        block = ctx.enter_context(nc.Block())

        def bc(ap, shape):
            return ap.to_broadcast(shape)

        loads = {}

        def loaded(eng, group):
            eng.wait_ge(sem("ld_" + group), loads[group])

        def row_of(ap):
            return ap.rearrange("(a n) -> a n", a=1)

        def all_rows(ap, n):
            return row_of(ap).to_broadcast([128, n])

        plan = []

        def want(group, dst, src):
            plan.append((group, dst, src))
            loads[group] = loads.get(group, 0) + 16

        want("x", x[:, :, :], A["x"].rearrange("b t d -> t b d"))
        want("cx", cx[:, :, :], A["ctx_1024"].rearrange("b t d -> t b d"))
        want("gates", gates[:, 0:4], all_rows(A["g_xattn"], 4))
        want("gates", gates[:, 4:8], all_rows(A["g_ffn"], 4))
        want("w0", w["L0v"][:, :], A["L0_xattn_Wv"])
        want("w0", w["L0q"][:, :], A["L0_xattn_Wq"])
        want("w0", w["L0qs"][:, :], A["L0_xattn_Wq_swapped"])
        want("w0", w["L0k"][:, :], A["L0_xattn_Wk"])
        want("w0", w["L0ks"][:, :], A["L0_xattn_Wk_swapped"])
        want("cos", cos[:, :], A["rope_cos"])
        want("cos", sin[:, :], A["rope_sin"])
        want("mask", maskI[:, :, :], A["mask_BxSxS2_ik0"].rearrange("b q k -> q b k"))
        want("wo0", w["L0o"][:, :].rearrange("p (n d) -> p n d", d=D), A["L0_xattn_Wo"].rearrange("(n p) d -> p n d", p=128))
        want("f0", wr[0][:, :], A["L0_ffn_w_router"])
        want("f0", wg[:, :], A["L0_ffn_w_gate"])
        for j in range(2):
            want(f"e0{j}", we[0][j][:, :], A["L0_experts"][j])
        want("w1", w["L1v"][:, :], A["L1_xattn_w_kv"][:, H * 64:])
        want("w1", w["L1q"][:, :], A["L1_xattn_w_q"])
        want("w1", w["L1k"][:, :], A["L1_xattn_w_kv"][:, 0:H * 64])
        want("w1", w["L1o"][:, :].rearrange("p (n d) -> p n d", d=D), A["L1_xattn_w_out1"].rearrange("(n p) d -> p n d", p=128))
        want("w1", w["L1o2"][:, :], A["L1_xattn_w_out2"])
        want("w1", gamma[:, :], all_rows(A["L1_xattn_gamma"], D))
        want("f1", wr[1][:, :], A["L1_ffn_Wg"])
        want("f1", br[1][:, :], all_rows(A["L1_ffn_bg"], E))
        want("f1", b2[1][:, :], A["L1_ffn_b2"])
        want("w2", wsim[:, :], A["L2_xattn_w_sim"])
        want("w2", bsim[:, :], all_rows(A["L2_xattn_b_sim"], 1))
        want("w2", wqv[:, :, :], A["L2_xattn_W_qv"].rearrange("(n p) d -> p n d", p=128))
        want("w2", bqv[:, :], row_of(A["L2_xattn_b_qv"]))
        want("f2", wr[2][:, :], A["L2_ffn_gate_w"])
        want("f2", br[2][:, :], all_rows(A["L2_ffn_gate_b"], E))
        want("f2", b2[2][:, :], A["L2_ffn_b2"])
        want("w3", w["L3q"][:, :], A["L3_xattn_Wq"])
        want("w3", w["L3k"][:, :], A["L3_xattn_Wk"])
        want("w3", w["L3v"][:, :], A["L3_xattn_Wv"])
        want("w3", w["L3o"][:, :], A["L3_xattn_Wo"])
        want("w3", validI[:, :, :], A["mask_BxS2_if1"].rearrange("(a b) k -> a b k", a=1).to_broadcast([128, B, K]))
        want("f3", wr[3][:, :], A["L3_ffn_Wr"])
        want("f3", br[3][:, :], all_rows(A["L3_ffn_br"], E))
        want("f3", b2[3][:, :], A["L3_ffn_b2"])
        want("f3", lng[:, :], A["L3_ffn_ln"])
        for n in (1, 2, 3):
            for j in range(2):
                want(f"e{n}{j}", we[n][j][:, :], A[f"L{n}_experts"][j])

        @block.sync
        def _(sp):
            for group, dst, src in plan:
                sp.dma_start(dst, src).then_inc(sem("ld_" + group), 16)
            for n in range(4):
                with sp.Fori(1, E // 2) as i:
                    for j in range(2):
                        sp.wait_ge(filled[5], 2 * i + (ffn[n][5] + j - 1))
                        sp.dma_start(we[n][j][:, :], A[f"L{n}_experts"][bass.ds(2 * i + j, 1), :, :].rearrange("a p f -> (a p) f"))\
                          .then_inc(sem(f"ld_e{n}{j}"), 16)
            after(sp, uses["b2", 3, 0])
            after(sp, uses["b2", 3, 1])
            sp.dma_start(out.rearrange("b t d -> t b d"), x[:, :, :]).then_inc(sem("stored"), 16)
            sp.wait_ge(sem("stored"), 16)

        def one(tile, b):
            return tile[:, bass.ds(b, 1), :].rearrange("p a n -> p (a n)")

        LN = {name: i for i, name in enumerate(("a0", "f0", "a1", "y1", "f1", "a2", "f2", "a3", "f3", "i3"))}

        def normalise(v, c, st, src, dst):
            for t in range(B):
                c(v.bn_stats(stats[:, t, :], src[:, t, :]))
                c(v.bn_aggr(mv[:, t, :], stats[:, t, :]))
            v.tensor_scalar(ve[:, :], mv[:, :, 1], EPS, None, ALU.add).then_inc(sem("ln_var"), 1)
            v.wait_ge(sem("ln_rstd"), LN[st] + 1)
            for t in range(B):
                v.tensor_scalar(dst[:, t, :], src[:, t, :], mv[:, t, 0:1], rstd[:, t:t + 1], ALU.subtract, ALU.mult)\
                 .then_inc(sem("ln_out"), 1)

        def root(g, st):
            g.wait_ge(sem("ln_var"), LN[st] + 1)
            g.tensor_tensor(rstd[:, :], ve[:, :], half[:, :], ALU.pow).then_inc(sem("ln_rstd"), 1)

        def turn_tensor(pe, st, src):
            for c_ in range(2):
                bank = fill(pe, uses["turn", st, c_])
                for t in range(4):
                    pe.wait_ge(sem("ln_out"), B * LN[st] + 4 * c_ + t + 1)
                    last = nc.tensor.transpose(bank[:, t * S:(t + 1) * S], src[:, 4 * c_ + t, :], ident[:, :])
                last.then_inc(filled[6 + c_], 1)

        def turn_scalar(a, st, dst):
            for c_ in range(2):
                bank = read(a, uses["turn", st, c_])
                if st == "i3":
                    nc.scalar.activation(dst[:, 4 * c_:4 * c_ + 4, :], bank[:, :].rearrange("p (t s) -> p t s", t=4),
                                         ACT.Identity, bias=lng[:, 1:2], scale=lng[:, 0:1]).then_inc(taken[6 + c_], 1)
                else:
                    nc.scalar.activation(dst[:, 4 * c_:4 * c_ + 4, :], bank[:, :].rearrange("p (t s) -> p t s", t=4),
                                         ACT.Copy).then_inc(taken[6 + c_], 1)

        def turned(eng, st):
            after(eng, uses["turn", st, 0])
            after(eng, uses["turn", st, 1])

        def rounds(eng, m, project, step):
            for f in range(len(m.fills)):
                project(0, 0, f)
            with eng.Fori(0, B // 2 - 1) as i:
                for j in range(2):
                    step(2 * i + j, j, True)
            for b in range(B - 2, B):
                step(b, b % 2, b < B - 1)

        def mha_tensor(pe, n):
            m = attn[n]

            def project(b, j, f):
                kind, part = m.fills[f]
                use = m.projection(f, b)
                bank = fill(pe, use)
                xb, cxb = one(xnT, b), one(cxT, b)
                if kind == "v":
                    pe.wait_ge(sem(f"cb{n}"), b + 1)
                    width = 512 if m.wide else D
                    last = nc.tensor.matmul(bank[0:K, 0:width], cb[j][:, :], w[f"L{n}v"][:, part * 512:part * 512 + width],
                                            start=True, stop=True)
                elif kind == "qk":
                    nc.tensor.matmul(bank[:, 0:S], w["L3q"][:, :], xb, start=True, stop=True)
                    last = nc.tensor.matmul(bank[:, S:S + K], w["L3k"][:, :], cxb, start=True, stop=True)
                else:
                    rhs, width = (xb, S) if kind[0] == "q" else (cxb, K)
                    for i in range(4):
                        o = part * 512 + i * 128
                        last = nc.tensor.matmul(bank[:, i * width:(i + 1) * width], w[f"L{n}{kind}"][:, o:o + 128], rhs,
                                                start=True, stop=True)
                last.then_inc(filled[use[0]], 1)

            def step(b, j, more):
                def projections_taken():
                    for k in (6, 7):
                        pe.wait_ge(taken[k], b * m.each[k] + (m.start[k] + m.first[k]))

                for slot in m.slots:
                    kind, g = slot
                    if kind == "F":
                        if more:
                            project(b + 1, 1 - j, g)
                        continue
                    use = m.use(slot, b, more)
                    bank = fill(pe, use)
                    if kind == "S":
                        if g == 0:
                            projections_taken()
                            if n == 0:
                                pe.wait_ge(sem("roped"), 6 * b + 6)
                            elif n == 1:
                                pe.wait_ge(sem("k_low"), 2 * b + 2)
                            else:
                                pe.wait_ge(sem("k_spread"), b + 1)
                        if m.wide:
                            for i in range(2):
                                h = G * g + 2 * i
                                last = nc.tensor.matmul(bank[:, 2 * i * K:2 * (i + 1) * K], qT[j][:, h // 2, :],
                                                        kM[j][:, h:h + 2, :], start=True, stop=True)
                        else:
                            last = nc.tensor.matmul(bank[:, 0:G * K], qT[j][:, 0, :], kM[j][:, G * g:G * g + G, :],
                                                    start=True, stop=True)
                    elif kind == "T":
                        pe.wait_ge(sem(f"probs{n}"), NG * b + (g + 1))
                        for i in range(G):
                            last = nc.tensor.transpose(bank[0:K, i * S:(i + 1) * S], pr[:, g, i, :], ident[:, :])
                    elif kind == "A":
                        after(pe, m.use(("T", g), b, more))
                        width = m.dh + 1
                        values = va[j] if m.wide else va8[j]
                        for i in range(G):
                            last = nc.tensor.matmul(bank[:, i * width:(i + 1) * width], pT[g % 2][:, i, :],
                                                    values[:, G * g + i, :], start=True, stop=True)
                    elif kind == "R":
                        for k in ((0, 1) if g == 0 and m.wide else (2, 3)):
                            after(pe, m.use(("A", k), b, more))
                        for i in range(4 if m.wide else 1):
                            k = 4 * g + i
                            last = nc.tensor.transpose(bank[:, i * S:(i + 1) * S], on[:, k * 128:(k + 1) * 128], ident[:, :])
                    elif kind == "Z":
                        after(pe, m.use(("R", 0), b, more))
                        after(pe, m.use(("R", 1), b, more))
                        for i in range(8):
                            last = nc.tensor.matmul(bank[:, 0:S], w["L1o"][:, i * D:(i + 1) * D], oT[:, i, :],
                                                    start=i == 0, stop=i == 7)
                    elif n == 1:
                        after(pe, m.use(("Z", 0), b, more))
                        last = nc.tensor.matmul(bank[:, 0:D], zT[:, :], w["L1o2"][:, :], start=True, stop=True)
                    else:
                        if n == 0:
                            loaded(pe, "wo0")
                        blocks = 8 if m.wide else 1
                        for r in range(2 if m.wide else 1):
                            after(pe, m.use(("R", r), b, more))
                        for i in range(blocks):
                            last = nc.tensor.matmul(bank[:, 0:D], oT[:, i, :], w[f"L{n}o"][:, i * D:(i + 1) * D],
                                                    start=i == 0, stop=i == blocks - 1)
                    last.then_inc(filled[use[0]], 1)

            loaded(pe, f"w{n}")
            turned(pe, f"a{n}")
            if n == 0:
                for b in range(B):
                    after(pe, uses["cx", b])
            rounds(pe, m, project, step)

        def mha_vector(v, n):
            m = attn[n]
            c = Chain(v, sem(f"vector{n}"))
            per_step = NG * 2

            def project(b, j, f):
                kind, part = m.fills[f]
                use = m.projection(f, b)
                if f == 0:
                    if positive(b):
                        for k in (6, 7):
                            v.wait_ge(filled[k], (b - 1) * m.each[k] + (m.start[k] + m.first[k]))
                    v.tensor_scalar(cb[j][:, :], one(cxT, b), 1.0, None, ALU.mult).then_inc(sem(f"cb{n}"), 1)
                if n == 0 and kind != "v":
                    is_k, is_swapped = kind[0] == "k", kind.endswith("s")
                    pair, width = 2 * part + is_k, K if is_k else S
                    if not is_swapped:
                        done = 6 * b + {0: -2, 1: 0, 2: 1, 3: 3}[pair]
                        if positive(done):
                            v.wait_ge(sem("roped"), done)
                    bank = read(v, use)
                    table = (sin if is_swapped else cos)[:, 0:width].unsqueeze(1).to_broadcast([128, 4, width])
                    v.tensor_tensor(rope[pair % 2][:, int(is_swapped), :, 0:width],
                                    bank[:, 0:4 * width].rearrange("p (n t) -> p n t", n=4), table, ALU.mult)\
                     .then_inc(taken[use[0]], 1)
                if n == 1 and kind == "k":
                    bank = read(v, use)
                    for e, done in ((0, sem("k_low")), (1, taken[use[0]])):
                        p_ = slice(64 * e, 64 * e + 64)
                        v.tensor_copy(kM[j][p_, 8 * part + e:8 * part + 8:2, :],
                                      bank[p_, 0:4 * K].rearrange("p (n t) -> p n t", n=4)).then_inc(done, 1)

            def step(b, j, more):
                c.at(b * per_step)
                for slot in m.slots:
                    kind, g = slot
                    if kind == "F":
                        if more:
                            project(b + 1, 1 - j, g)
                        continue
                    use = m.use(slot, b, more)
                    if kind == "S":
                        raw = read(v, use)[:, 0:G * K].rearrange("p (h k) -> p h k", h=G)
                        if m.masked:
                            bias = (bias0 if n == 0 else bias3)[:, bass.ds(b, 1), :].to_broadcast([S, G, K])
                            v.tensor_tensor(sc[:, g, :, :], raw, bias, ALU.add).then_inc(taken[use[0]], 1)
                            after(v, use)
                            raw = sc[:, g, :, :]
                        c(v.tensor_reduce(mx[:, g, :], raw, AX_X, ALU.max))
                        v.tensor_tensor(sc[:, g, :, :], raw, mx[:, g, :].unsqueeze(2).to_broadcast([S, G, K]), ALU.subtract)\
                         .then_inc(sem("shifted3" if n == 3 else "shifted0") if m.masked else taken[use[0]], 1)
                    if kind == "A":
                        width = m.dh + 1
                        raw = read(v, use)[:, 0:G * width].rearrange("p (h d) -> p h d", h=G)
                        c(v.reciprocal(rc[:, g, :], raw[:, :, m.dh]))
                        v.tensor_tensor(on[:, G * g * m.dh:G * (g + 1) * m.dh].rearrange("p (h d) -> p h d", h=G),
                                        raw[:, :, 0:m.dh], rc[:, g, :].unsqueeze(2).to_broadcast([S, G, m.dh]), ALU.mult)\
                         .then_inc(taken[use[0]], 1)
                    if kind == "Y":
                        bank = read(v, use)
                        if n == 1:
                            v.tensor_copy(one(yb, b), bank[:, 0:D]).then_inc(taken[use[0]], 1)
                        else:
                            v.scalar_tensor_tensor(one(x, b), bank[:, 0:D], tg[:, n:n + 1], one(x, b), ALU.mult, ALU.add)\
                             .then_inc(taken[use[0]], 1)

            rounds(v, m, project, step)
            after(v, m.use(("Y", 0), B - 1, False))

        def mha_scalar(a, n):
            m = attn[n]

            def project(b, j, f):
                kind, part = m.fills[f]
                use = m.projection(f, b)
                if kind == "v":
                    bank = read(a, use)
                    if m.wide:
                        nc.scalar.activation(va[j][:, 8 * part:8 * part + 8, 0:64],
                                             bank[0:K, 0:512].rearrange("p (h d) -> p h d", h=8), ACT.Copy)\
                          .then_inc(taken[use[0]], 1)
                    else:
                        nc.scalar.activation(va8[j][:, :, 0:8], bank[0:K, 0:D].rearrange("p (h d) -> p h d", h=H), ACT.Copy)\
                          .then_inc(taken[use[0]], 1)
                if n == 1 and kind == "q":
                    bank = read(a, use)
                    nc.scalar.activation(qT[j][:, 4 * part:4 * part + 4, :], bank[:, :].rearrange("p (n t) -> p n t", n=4),
                                         ACT.Copy).then_inc(taken[use[0]], 1)
                if kind == "qk":
                    bank = read(a, use)
                    nc.scalar.activation(qT[j][:, 0, :], bank[:, 0:S], ACT.Copy).then_inc(sem("q_taken"), 1)
                    if positive(b):
                        a.wait_ge(sem("k_spread"), b)
                    nc.scalar.activation(k3[:, :], bank[:, S:S + K], ACT.Copy).then_inc(taken[use[0]], 1)

            def step(b, j, more):
                for slot in m.slots:
                    kind, g = slot
                    if kind == "F":
                        if more:
                            project(b + 1, 1 - j, g)
                        continue
                    use = m.use(slot, b, more)
                    if kind == "S":
                        if m.masked:
                            a.wait_ge(sem("shifted3" if n == 3 else "shifted0"), NG * b + (g + 1))
                        else:
                            after(a, use)
                        nc.scalar.activation(pr[:, g, :, :], sc[:, g, :, :], ACT.Exp, scale=m.scale).then_inc(sem(f"probs{n}"), 1)
                    if kind == "T":
                        bank = read(a, use)
                        nc.scalar.activation(pT[g % 2][:, :, :], bank[0:K, :].rearrange("p (h t) -> p h t", h=G), ACT.Copy)\
                          .then_inc(taken[use[0]], 1)
                    if kind == "R":
                        bank = read(a, use)
                        blocks = 4 if m.wide else 1
                        nc.scalar.activation(oT[:, 4 * g:4 * g + blocks, :],
                                             bank[:, 0:blocks * S].rearrange("p (n t) -> p n t", n=blocks), ACT.Copy)\
                          .then_inc(taken[use[0]], 1)
                    if kind == "Z":
                        bank = read(a, use)
                        nc.scalar.activation(zT[:, :], bank[:, 0:S], ACT.Relu).then_inc(taken[use[0]], 1)

            rounds(a, m, project, step)

        def mha_pool(g_, n):
            m = attn[n]

            def project(b, j, f):
                kind, part = m.fills[f]
                use = m.projection(f, b)
                if n == 0 and kind.endswith("s"):
                    is_k = kind[0] == "k"
                    pair, width = 2 * part + is_k, K if is_k else S
                    after(g_, m.projection(f - 1, b))
                    after(g_, use)
                    r = rope[pair % 2]
                    done = 6 * b + (0, 1, 3, 4)[pair]
                    if positive(done):
                        g_.wait_ge(sem("roped"), done)
                    if not is_k:
                        g_.tensor_tensor(qT[j][:, 4 * part:4 * part + 4, :], r[:, 0, :, :], r[:, 1, :, :], ALU.add)\
                          .then_inc(sem("roped"), 1)
                    else:
                        for e in range(2):
                            p_ = slice(64 * e, 64 * e + 64)
                            if e:
                                g_.wait_ge(sem("roped"), done + 1)
                            g_.tensor_tensor(kM[j][p_, 8 * part + e:8 * part + 8:2, :], r[p_, 0, :, 0:K], r[p_, 1, :, 0:K], ALU.add)\
                              .then_inc(sem("roped"), 1)
                if kind == "qk":
                    after(g_, use)
                    g_.tensor_tensor(kM[j][:, :, :], k3[:, :].unsqueeze(1).to_broadcast([128, H, K]),
                                     headmask[:, :].unsqueeze(2).to_broadcast([128, H, K]), ALU.mult)\
                      .then_inc(sem("k_spread"), 1)

            def step(b, j, more):
                for kind, f in m.slots:
                    if kind == "F" and more:
                        project(b + 1, 1 - j, f)

            if n != 1:
                rounds(g_, m, project, step)

        def coat_tensor(pe):
            loaded(pe, "w2")
            turned(pe, "a2")
            pe.wait_ge(sem("c3"), 2)
            for b in range(B):
                bank = fill(pe, uses["sim", b])
                nc.tensor.matmul(bank[:, 0:K], xnT[:, b, :], c3[:, b, :], start=True, stop=False)
                nc.tensor.matmul(bank[:, 0:K], ones[:, :], c2[:, b, :], start=False, stop=True).then_inc(filled[b % 2], 1)
                if b:
                    coat_turn(pe, b - 1)
            coat_turn(pe, B - 1)
            bank = fill(pe, uses["mT"])
            pe.wait_ge(sem("largest"), B)
            nc.tensor.transpose(bank[0:B, 0:S], m8[:, :], ident[:, :]).then_inc(filled[6], 1)
            bank = fill(pe, uses["bT"])
            pe.wait_ge(sem("token_weights"), 1)
            nc.tensor.transpose(bank[:, 0:B], mT[:, :], ident[0:B, 0:B]).then_inc(filled[7], 1)
            bank = fill(pe, uses["hc"])
            after(pe, uses["bT"])
            for b in range(B):
                last = nc.tensor.matmul(bank[:, b:b + 1], xn[:, b, :], bT[:, b:b + 1], start=True, stop=True)
            last.then_inc(filled[6], 1)
            for b in range(B):
                bank = fill(pe, uses["feat", b])
                pe.wait_ge(sem("by_bar"), b + 1)
                for i, feature in enumerate((xnT, fq, fm, fc)):
                    nc.tensor.matmul(bank[:, 0:D], feature[:, b, :], wqv[:, i, :], start=i == 0, stop=False)
                nc.tensor.matmul(bank[:, 0:D], ones[0:1, :], bqv[:, :], start=False, stop=True).then_inc(filled[6 + b % 2], 1)

        def coat_turn(pe, b):
            bank = fill(pe, uses["aT", b])
            pe.wait_ge(sem("a_weights"), b + 1)
            nc.tensor.transpose(bank[0:K, 0:S], sim[:, b, :], ident[:, :]).then_inc(filled[2 + b % 2], 1)
            bank = fill(pe, uses["hq", b])
            after(pe, uses["aT", b])
            nc.tensor.matmul(bank[:, 0:S], cx[:, b, :], aT[b % 2][:, :], start=True, stop=True).then_inc(filled[4 + b % 2], 1)

        def coat_scalar(a):
            for b in range(B):
                a.wait_ge(sem("largest_neg"), b + 1)
                nc.scalar.activation(sim[:, b, :], sim[:, b, :], ACT.Exp, bias=nm8[:, b:b + 1], accum_out=z8[:, b:b + 1])\
                  .then_inc(sem("a_exp"), 1)
                if b:
                    coat_take(a, b - 1)
            coat_take(a, B - 1)
            a.wait_ge(sem("row_max"), 1)
            nc.scalar.activation(mT[:, :], mT[:, :], ACT.Exp, bias=row1[:, 0:1], accum_out=row1[:, 1:2]).then_inc(sem("row_exp"), 1)

        def coat_take(a, b):
            bank = read(a, uses["aT", b])
            nc.scalar.activation(aT[b % 2][:, :], bank[0:K, 0:S], ACT.Copy).then_inc(taken[2 + b % 2], 1)

        def coat_vector(v, c):
            loaded(v, "w2")
            v.tensor_scalar(c3[:, :, :], cxT[:, :, :], wsim[:, 2:3], wsim[:, 0:1], ALU.mult, ALU.add).then_inc(sem("c3"), 1)
            v.tensor_scalar(c2[:, :, :], cxT[:, :, :], wsim[:, 1:2], None, ALU.mult).then_inc(sem("c3"), 1)

            def features(b):
                bank = read(v, uses["hq", b])
                c(v.tensor_copy(fq[:, b, :], bank[:, 0:S]))
                v.tensor_tensor(fm[:, b, :], bank[:, 0:S], xnT[:, b, :], ALU.mult).then_inc(taken[4 + b % 2], 1)

            def weights(b):
                v.wait_ge(sem("a_exp"), b + 1)
                c(v.reciprocal(col["rz"][:, b:b + 1], z8[:, b:b + 1]))
                v.tensor_scalar(sim[:, b, :], sim[:, b, :], col["rz"][:, b:b + 1], None, ALU.mult).then_inc(sem("a_weights"), 1)

            for b in range(B):
                bank = read(v, uses["sim", b])
                v.tensor_scalar(sim[:, b, :], bank[:, 0:K], bsim[:, 0:1], None, ALU.add).then_inc(taken[b % 2], 1)
                after(v, uses["sim", b])
                v.tensor_reduce(m8[:, b:b + 1], sim[:, b, :], AX_X, ALU.max).then_inc(sem("largest"), 1)
                v.wait_ge(sem("largest"), b + 1)
                v.tensor_scalar(nm8[:, b:b + 1], m8[:, b:b + 1], -1.0, None, ALU.mult).then_inc(sem("largest_neg"), 1)
                if b:
                    weights(b - 1)
                if b > 1:
                    features(b - 2)
            weights(B - 1)
            features(B - 2)
            features(B - 1)
            bank = read(v, uses["mT"])
            v.tensor_copy(mT[:, :], bank[0:B, 0:S]).then_inc(taken[6], 1)
            after(v, uses["mT"])
            v.tensor_reduce(row1[:, 0:1], mT[:, :], AX_X, ALU.max, negate=True).then_inc(sem("row_max"), 1)
            v.wait_ge(sem("row_exp"), 1)
            c(v.reciprocal(row1[:, 2:3], row1[:, 1:2]))
            v.tensor_scalar(mT[:, :], mT[:, :], row1[:, 2:3], None, ALU.mult).then_inc(sem("token_weights"), 1)
            bank = read(v, uses["bT"])
            v.tensor_copy(bT[:, :], bank[:, 0:B]).then_inc(taken[7], 1)
            bank = read(v, uses["hc"])
            v.tensor_copy(hc[:, :], bank[:, 0:B]).then_inc(taken[6], 1)
            after(v, uses["hc"])
            for b in range(B):
                v.tensor_scalar(fc[:, b, :], xnT[:, b, :], hc[:, b:b + 1], None, ALU.mult).then_inc(sem("by_bar"), 1)
            for b in range(B):
                bank = read(v, uses["feat", b])
                v.scalar_tensor_tensor(x[:, b, :], bank[:, 0:D], tg[:, 2:3], x[:, b, :], ALU.mult, ALU.add)\
                 .then_inc(taken[6 + b % 2], 1)
            after(v, uses["feat", B - 2])
            after(v, uses["feat", B - 1])

        def ffn_loop(eng, unit):
            with eng.Fori(0, E // 2 - 1) as i:
                for q in range(4):
                    unit(i, q)
            for q in range(4):
                unit(E // 2 - 1, q)

        def ffn_tensor(pe, n):
            blocks = HIDDEN_BLOCKS[n]
            width = 128 * blocks
            src = fq if n == 3 else xnT

            def hidden(i, q):
                j = q // 2
                if n != SHARED and q % 2 == 0:
                    pe.wait_ge(sem(f"ld_e{n}{j}"), 16 * i + 16)
                weights = wg if n == SHARED else we[n][j]
                for nb in range(blocks):
                    use = hidden_use(n, i, q, nb)
                    bank = fill(pe, use)
                    nc.tensor.matmul(bank[:, :], weights[:, nb * 128:(nb + 1) * 128], src[:, 4 * (q % 2):4 * (q % 2) + 4, :],
                                     start=True, stop=True).then_inc(filled[use[0]], 1)

            def outputs(i, q):
                j, c_ = q // 2, q % 2
                offset = 0 if n == SHARED else width
                if n == SHARED and c_ == 0:
                    pe.wait_ge(sem(f"ld_e{n}{j}"), 16 * i + 16)
                use = out_use(n, i, q)
                bank = fill(pe, use)
                for t in range(4):
                    for nb in range(blocks):
                        if n == SHARED:
                            if t == 0:
                                after(pe, hidden_use(n, 0, c_, nb))
                        elif t == 0:
                            after(pe, hidden_use(n, i, q, nb))
                        last = nc.tensor.matmul(bank[:, t * D:(t + 1) * D], hT[c_][:, nb, t * S:(t + 1) * S],
                                                we[n][j][:, offset + nb * D:offset + (nb + 1) * D],
                                                start=nb == 0, stop=nb == blocks - 1)
                last.then_inc(filled[use[0]], 1)

            def unit(i, q):
                if n != SHARED:
                    if q < 3:
                        hidden(i, q + 1)
                    elif not isinstance(i, int):
                        hidden(i + 1, 0)
                outputs(i, q)

            loaded(pe, f"f{n}")
            turned(pe, f"f{n}")
            bank = fill(pe, uses["logits", n])
            for t in range(B):
                last = nc.tensor.matmul(bank[:, t * E:(t + 1) * E], xnT[:, t, :], wr[n][:, :], start=True, stop=True)
            last.then_inc(filled[6], 1)
            if n == 3:
                turn_tensor(pe, "i3", yb)
                turned(pe, "i3")
            hidden(0, 0)
            if n == SHARED:
                hidden(0, 1)
                pe.wait_ge(sem("chosen"), 1)
                bank = fill(pe, uses["rank"])
                nc.tensor.matmul(bank[:, 0:E], upper[:, :], small["m"][:, 0, :], start=True, stop=True)
                nc.tensor.matmul(bank[:, E:B * E], upper[:, :], small["m"][:, 1:B, :], start=True, stop=False)
                for t in range(B - 2, -1, -1):
                    later = B - 1 - t
                    last = nc.tensor.matmul(bank[:, (t + 1) * E:B * E], ones[:, :],
                                            small["m"][:, t:t + 1, :].to_broadcast([128, later, E]),
                                            start=False, stop=t == 0, skip_group_check=t > 0)
                last.then_inc(filled[7], 1)
            ffn_loop(pe, unit)
            if n != SHARED:
                for c_ in range(2):
                    bank = fill(pe, uses["combT", n, c_])
                    if c_ == 0:
                        pe.wait_ge(sem("combined"), n + 1)
                    for t in range(4):
                        last = nc.tensor.transpose(bank[0:E, t * S:(t + 1) * S], small["cb"][:, 4 * c_ + t, :], ident[:, :])
                    last.then_inc(filled[6 + c_], 1)
                for c_ in range(2):
                    bank = fill(pe, uses["b2", n, c_])
                    after(pe, uses["combT", n, c_])
                    for t in range(4):
                        last = nc.tensor.matmul(bank[:, t * D:(t + 1) * D], combT[:, 4 * c_ + t, :], b2[n][:, :],
                                                start=True, stop=True)
                    last.then_inc(filled[4 + c_], 1)

        def ffn_scalar(a, n):
            blocks = HIDDEN_BLOCKS[n]
            func = {0: ACT.Silu, 1: ACT.Relu, 2: ACT.Gelu, 3: ACT.Relu}[n]

            def hidden(i, q):
                for nb in range(blocks):
                    use = hidden_use(n, i, q, nb)
                    bank = read(a, use)
                    if n == SHARED:
                        nc.scalar.activation(hT[q % 2][:, nb, :], bank[:, :], func).then_inc(taken[use[0]], 1)
                    else:
                        at = 2 * 128 * blocks + nb
                        nc.scalar.activation(hT[q % 2][:, nb, :], bank[:, :], func, bias=we[n][q // 2][:, at:at + 1])\
                          .then_inc(taken[use[0]], 1)

            def unit(i, q):
                if q < 3:
                    hidden(i, q + 1)
                elif not isinstance(i, int):
                    hidden(i + 1, 0)

            a.wait_ge(sem("route_max"), n + 1)
            nc.scalar.activation(small["ex"][:, :, :], small["ex"][:, :, :], ACT.Exp).then_inc(sem("route_exp"), 1)
            if n == 3:
                loaded(a, "f3")
                turn_scalar(a, "i3", fq)
            hidden(0, 0)
            if n == SHARED:
                hidden(0, 1)
            else:
                ffn_loop(a, unit)
                for c_ in range(2):
                    bank = read(a, uses["combT", n, c_])
                    nc.scalar.activation(combT[:, 4 * c_:4 * c_ + 4, :], bank[0:E, :].rearrange("p (t s) -> p t s", t=4), ACT.Copy)\
                      .then_inc(taken[6 + c_], 1)

        def ffn_vector(v, c, n):
            s3 = small

            def wide(tile):
                return tile[:, :].unsqueeze(2).to_broadcast([128, B, E])

            def first_largest(values, largest, chosen):
                c(v.tensor_tensor(s3["eq"][:, :, :], values[:, :, :], wide(largest), ALU.is_equal))
                c(v.tensor_tensor(s3["eq"][:, :, :], s3["eq"][:, :, :], s3["pri"][:, :, :], ALU.mult))
                c(v.tensor_reduce(col["km"][:, :], s3["eq"][:, :, :], AX_X, ALU.max))
                c(v.tensor_tensor(chosen[:, :, :], s3["eq"][:, :, :], wide(col["km"]), ALU.is_equal))

            loaded(v, f"f{n}")
            use = uses["logits", n]
            logits = read(v, use)[:, 0:B * E].rearrange("p (t e) -> p t e", t=B)
            if n == SHARED:
                v.tensor_copy(s3["L"][:, :, :], logits).then_inc(taken[6], 1)
            else:
                v.tensor_tensor(s3["L"][:, :, :], logits, br[n][:, :].unsqueeze(1).to_broadcast([128, B, E]), ALU.add)\
                 .then_inc(taken[6], 1)
            after(v, use)
            c(v.tensor_reduce(col["m1"][:, :], s3["L"][:, :, :], AX_X, ALU.max))
            v.tensor_tensor(s3["ex"][:, :, :], s3["L"][:, :, :], wide(col["m1"]), ALU.subtract).then_inc(sem("route_max"), 1)
            if n == 3:
                normalise(v, c, "i3", xn, yb)
            first_largest(s3["L"], col["m1"], s3["one1"])
            v.wait_ge(sem("route_exp"), n + 1)
            if n in (0, 3):
                c(v.tensor_reduce(col["z"][:, :], s3["ex"][:, :, :], AX_X, ALU.add))
                c(v.reciprocal(col["rz"][:, :], col["z"][:, :]))
            if n == 3:
                c(v.tensor_scalar(s3["m"][:, :, :], s3["one1"][:, :, :], tg[:, 7:8], None, ALU.mult))
                v.tensor_tensor(s3["cb"][:, :, :], s3["m"][:, :, :], wide(col["rz"]), ALU.mult).then_inc(sem("combined"), 1)
            else:
                c(v.scalar_tensor_tensor(s3["L2"][:, :, :], s3["one1"][:, :, :], -3.0e38, s3["L"][:, :, :], ALU.mult, ALU.add))
                c(v.tensor_reduce(col["m2"][:, :], s3["L2"][:, :, :], AX_X, ALU.max))
                first_largest(s3["L2"], col["m2"], s3["one2"])
                v.tensor_tensor(s3["m"][:, :, :], s3["one1"][:, :, :], s3["one2"][:, :, :], ALU.add).then_inc(sem("chosen"), 1)
                v.wait_ge(sem("chosen"), n + 1)
                if n == SHARED:
                    c(v.tensor_tensor(s3["ex"][:, :, :], s3["ex"][:, :, :], wide(col["rz"]), ALU.mult))
                c(v.tensor_tensor(s3["ex"][:, :, :], s3["ex"][:, :, :], s3["m"][:, :, :], ALU.mult))
                if n == SHARED:
                    use = uses["rank"]
                    rank = read(v, use)[:, 0:B * E].rearrange("p (t e) -> p t e", t=B)
                    v.scalar_tensor_tensor(s3["ex"][:, :, :], rank, CAPACITY + 0.5, s3["ex"][:, :, :], ALU.is_lt, ALU.mult)\
                     .then_inc(taken[7], 1)
                    after(v, use)
                c(v.tensor_reduce(col["s"][:, :], s3["ex"][:, :, :], AX_X, ALU.add))
                if n == SHARED:
                    c(v.tensor_scalar(col["s"][:, :], col["s"][:, :], 1e-6, None, ALU.add))
                c(v.reciprocal(col["km"][:, :], col["s"][:, :]))
                c(v.tensor_scalar(col["km"][:, :], col["km"][:, :], tg[:, 4 + n:5 + n], None, ALU.mult))
                v.tensor_tensor(s3["cb"][:, :, :], s3["ex"][:, :, :], wide(col["km"]), ALU.mult).then_inc(sem("combined"), 1)
            v.wait_ge(sem("combined"), n + 1)

            def unit(i, q):
                use = out_use(n, i, q)
                bank = read(v, use)
                v.wait_ge(taken[use[0]], use[1])
                for t in range(4):
                    tile = 4 * (q % 2) + t
                    last = v.scalar_tensor_tensor(x[:, tile, :], bank[:, t * D:(t + 1) * D],
                                                  s3["cb"][:, tile, bass.ds(2 * i + q // 2, 1)], x[:, tile, :], ALU.mult, ALU.add)
                last.then_inc(taken[use[0]], 1)

            ffn_loop(v, unit)
            if n != SHARED:
                for c_ in range(2):
                    use = uses["b2", n, c_]
                    bank = read(v, use)
                    v.wait_ge(taken[use[0]], use[1])
                    xs = x[:, 4 * c_:4 * c_ + 4, :]
                    v.tensor_tensor(xs, xs, bank[:, :].rearrange("p (t d) -> p t d", t=4), ALU.add).then_inc(taken[4 + c_], 1)
                    after(v, use)
            else:
                for q in (2, 3):
                    after(v, out_use(n, E // 2 - 1, q))

        @block.gpsimd
        def _(g):
            done = sem("constants")
            g.memset(ident[:, :], 0.0).then_inc(done, 1)
            g.memset(ones[:, :], 1.0).then_inc(done, 1)
            g.memset(upper[:, :], 1.0).then_inc(done, 1)
            g.memset(headmask[:, :], 1.0).then_inc(done, 1)
            g.memset(causal[:, :], 0.0).then_inc(done, 1)
            g.memset(half[:, :], -0.5).then_inc(done, 1)
            for j in range(2):
                g.memset(kM[j][:, :, :], 0.0).then_inc(done, 1)
                g.memset(va[j][:, :, 64:65], 1.0).then_inc(done, 1)
                g.memset(va8[j][:, :, 8:9], 1.0).then_inc(done, 1)
            for e in range(E):
                g.memset(small["pri"][:, :, e:e + 1], float(E - e)).then_inc(done, 1)
            g.wait_ge(done, 12 + E)
            g.affine_select(out=ident[:, :], in_=ident[:, :], compare_op=ALU.not_equal, fill=1.0, base=0,
                            pattern=[[-1, 128]], channel_multiplier=1).then_inc(done, 1)
            g.affine_select(out=upper[:, :], in_=upper[:, :], compare_op=ALU.is_ge, fill=0.0, base=0,
                            pattern=[[1, 128]], channel_multiplier=-1).then_inc(done, 1)
            g.affine_select(out=causal[:, :], in_=causal[:, :], compare_op=ALU.is_ge, fill=NEG, base=0,
                            pattern=[[-1, K]], channel_multiplier=1).then_inc(done, 1)
            g.affine_select(out=headmask[:, :], in_=headmask[:, :], compare_op=ALU.is_ge, fill=0.0, base=0,
                            pattern=[[-8, H]], channel_multiplier=1).then_inc(done, 1)
            g.wait_ge(done, 16 + E)
            g.affine_select(out=headmask[:, :], in_=headmask[:, :], compare_op=ALU.is_ge, fill=0.0, base=7,
                            pattern=[[8, H]], channel_multiplier=-1).then_inc(done, 1)
            g.wait_ge(done, 17 + E)
            for n in range(4):
                if n < LAYERS:
                    root(g, f"a{n}")
                    if n != 2:
                        mha_pool(g, n)
                    if n == 1:
                        root(g, "y1")
                    root(g, f"f{n}")
                    if n == 3:
                        root(g, "i3")

        CONSTANTS = 17 + E

        @block.tensor
        def _(pe):
            pe.wait_ge(sem("constants"), CONSTANTS)
            loaded(pe, "cx")
            for b in range(B):
                bank = fill(pe, uses["cx", b])
                nc.tensor.transpose(bank[:, 0:K], cx[:, b, :], ident[0:K, 0:K]).then_inc(filled[b], 1)
            for n in range(LAYERS):
                turn_tensor(pe, f"a{n}", xn)
                if n == 2:
                    coat_tensor(pe)
                else:
                    mha_tensor(pe, n)
                turn_tensor(pe, f"f{n}", xn)
                ffn_tensor(pe, n)

        @block.scalar
        def _(a):
            loaded(a, "gates")
            nc.scalar.activation(tg[:, :], gates[:, :], ACT.Tanh).then_inc(sem("tg"), 1)
            for b in range(B):
                bank = read(a, uses["cx", b])
                nc.scalar.activation(cxT[:, b, :], bank[:, 0:K], ACT.Copy).then_inc(taken[b], 1)
            a.wait_ge(sem("constants"), CONSTANTS)
            for n in range(LAYERS):
                turn_scalar(a, f"a{n}", xnT)
                if n == 2:
                    coat_scalar(a)
                else:
                    mha_scalar(a, n)
                turn_scalar(a, f"f{n}", xnT)
                ffn_scalar(a, n)

        @block.vector
        def _(v):
            c = Chain(v, sem("vector"))
            loaded(v, "x")
            normalise(v, c, "a0", x, xn)
            v.wait_ge(sem("constants"), CONSTANTS)
            v.wait_ge(sem("tg"), 1)
            loaded(v, "mask")
            loaded(v, "cos")
            c(v.tensor_scalar(bias0[:, :, :], maskI[:, :, :], 0, NEG, ALU.is_equal, ALU.mult))
            for b in range(B):
                after(v, uses["cx", b])
            for n in range(LAYERS):
                if n:
                    normalise(v, c, f"a{n}", x, xn)
                if n == 3:
                    loaded(v, "w3")
                    c(v.tensor_scalar(bias3[:, :, :], validI[:, :, :], 0, NEG, ALU.is_equal, ALU.mult))
                    c(v.tensor_tensor(bias3[:, :, :], bias3[:, :, :], causal[:, :].unsqueeze(1).to_broadcast([S, B, K]), ALU.min))
                if n == 2:
                    coat_vector(v, c)
                else:
                    mha_vector(v, n)
                if n == 1:
                    loaded(v, "w1")
                    normalise(v, c, "y1", yb, yb)
                    v.wait_ge(sem("ln_out"), B * (LN["y1"] + 1))
                    c(v.tensor_scalar(gamma[:, :], gamma[:, :], tg[:, 1:2], None, ALU.mult))
                    c(v.tensor_tensor(yb[:, :, :], yb[:, :, :], gamma[:, :].unsqueeze(1).to_broadcast([S, B, D]), ALU.mult))
                    c(v.tensor_tensor(x[:, :, :], x[:, :, :], yb[:, :, :], ALU.add))
                normalise(v, c, f"f{n}", x, xn)
                ffn_vector(v, c, n)


def kernel(**inputs):
    import numpy as _np
    import concourse.bacc as _bacc
    from concourse.bass_utils import run_bass_kernel_spmd as _run

    given = {n: _np.asarray(a) for n, a in inputs.items()}
    plain = ["x", "ctx_1024", "mask_BxSxS2_ik0", "mask_BxS2_if1", "g_xattn", "g_ffn", "L0_xattn_Wq", "L0_xattn_Wk",
             "L0_xattn_Wv", "L0_xattn_Wo", "L1_xattn_w_kv", "L1_xattn_w_q", "L1_xattn_w_out1", "L1_xattn_w_out2",
             "L1_xattn_gamma", "L1_ffn_Wg", "L1_ffn_bg", "L1_ffn_b2", "L2_xattn_b_sim", "L2_xattn_W_qv", "L2_xattn_b_qv",
             "L2_ffn_gate_b", "L2_ffn_b2", "L3_ffn_Wr", "L3_ffn_br", "L3_ffn_b2"]
    arrays = {n: given[n] for n in plain}
    for n in ("L0_ffn_w_router", "L0_ffn_w_gate", "L2_ffn_gate_w", "L3_xattn_Wq", "L3_xattn_Wk", "L3_xattn_Wv", "L3_xattn_Wo"):
        arrays[n] = given[n].T
    for n in ("L0_xattn_Wq", "L0_xattn_Wk"):
        arrays[n + "_swapped"] = given[n].reshape(D, -1, 2)[:, :, ::-1].reshape(D, -1)
    arrays["L2_xattn_w_sim"] = given["L2_xattn_w_sim"].reshape(3, D).T
    arrays["L3_ffn_ln"] = _np.stack([given["L3_ffn_ln_g"], given["L3_ffn_ln_b"]], axis=1)

    def rows(a):
        e, r, m = a.shape
        return a.reshape(e, r // 128, 128, m).transpose(0, 2, 1, 3).reshape(e, 128, -1)

    arrays["L0_experts"] = rows(given["L0_ffn_w_down"].transpose(0, 2, 1))
    for n, (w1, b1, w2) in {1: ("W1", "b1", "W2"), 2: ("w1", "b1", "w2"), 3: ("W1", "b1", "W2")}.items():
        w1, b1, w2 = (given[f"L{n}_ffn_{k}"] for k in (w1, b1, w2))
        arrays[f"L{n}_experts"] = _np.concatenate([w1, rows(w2), rows(b1[:, :, None])], axis=2)

    inv = (1.0 / _np.float32(10000.0) ** (_np.arange(0, 64, 2, dtype=_np.float32) / _np.float32(64))).astype(_np.float32)
    angle = (_np.arange(S, dtype=_np.float32)[:, None] * inv).astype(_np.float32).T
    sign = _np.array([-1.0, 1.0], _np.float32)[None, :, None]
    one_head = [_np.repeat(_np.cos(angle)[:, None], 2, axis=1).reshape(64, S),
                (_np.sin(angle)[:, None] * sign).reshape(64, S)]
    arrays["rope_cos"], arrays["rope_sin"] = (_np.tile(a, (2, 1)).astype(_np.float32) for a in one_head)

    nc = _bacc.Bacc("TRN2", target_bir_lowering=False, num_devices=1)
    aps, feed = {}, {}
    for n, a in arrays.items():
        a = _np.ascontiguousarray(a)
        feed[f"in_{n}"] = a
        aps[n] = nc.dram_tensor(f"in_{n}", a.shape, mybir.dt.from_np(a.dtype), kind="ExternalInput").ap()
    out = nc.dram_tensor("out_0", (B, S, D), F32, kind="ExternalOutput").ap()
    build(nc, aps, out)
    r = _run(nc, [feed], core_ids=[0])
    return r.results[0]["out_0"]
```

```python
from contextlib import ExitStack

import concourse.bass as bass
from concourse import mybir

F32 = mybir.dt.float32
I32 = mybir.dt.int32
ALU = mybir.AluOpType
ACT = mybir.ActivationFunctionType
AX_X = mybir.AxisListType.X

B = 8
S = 128
D = 128
K = 77
H = 16
G = 4
NG = H // G
E = 8
HALF = 4 * S
UNITS = 2 * E
CAPACITY = 160
NEG = -1.0e30
EPS = 1e-5
LAYERS = 4


class Chain:

    def __init__(self, eng, sem):
        self.eng, self.sem, self.base, self.n = eng, sem, 0, 0

    def at(self, base):
        self.base, self.n = base, 0

    def __call__(self, instruction):
        instruction.then_inc(self.sem, 1)
        self.n += 1
        self.eng.wait_ge(self.sem, self.base + self.n)


def positive(value):
    return not isinstance(value, int) or value > 0


class Attention:

    BANK = {"S": (0,), "T": (1,), "A": (2,), "R": (3,), "Z": (3,), "Y": (3,), "F": (4, 5, 6, 7)}
    PROJECTED = BANK["F"]

    def __init__(self, fills, dh, scale, masked, hidden, spread, start):
        self.fills, self.dh, self.scale, self.masked = fills, dh, scale, masked
        self.wide = dh == 64
        self.slots = []
        left = list(range(len(fills)))
        late = {}

        def due(kind, n, group, ticks, place):
            tick = group + ticks
            late.setdefault((tick % NG, place), []).append((kind, n, tick // NG))

        for g in range(NG):
            due("X", g, g, 0, 3)
            if self.wide:
                due("N", g, g, 1, 1)
            due("T", g, g, 2, 2)
            due("A", g, g, 3, 4)
        if hidden:
            due("Z", 0, 3, 4, 1)
        if not self.wide:
            due("R", 0, 3, 4, 1)
        due("Y", 0, 3, 4, 5)
        for tick in range(NG):
            self.slots.append(("S", tick, 0))
            for place in range(1, 6):
                self.slots += late.get((tick, place), [])
                if place in (1, 3, 5):
                    n = (spread[tick] + (5 - place) // 2) // 3
                    self.slots += [("F", left.pop(0), -1) for _ in range(n)]
        assert not left and max(s[2] for s in self.slots) == 1
        self.start = list(start)
        self.first = [sum(self.bank(("F", f)) == k for f in range(len(fills))) for k in range(8)]
        self.each = [sum(self.bank(s) == k for s in self.slots) for k in range(8)]

    def bank(self, slot):
        return None if slot[0] in "XN" else self.BANK[slot[0]][slot[1] % len(self.BANK[slot[0]])]

    def there(self, slot, step):
        return not isinstance(step, int) or 0 <= step - slot[2] < B

    def before(self, bank, step):
        base = self.start[bank] + self.first[bank]
        if isinstance(step, int):
            return base + sum(self.bank(s) == bank and self.there(s, e) for e in range(step) for s in self.slots)
        one = self.before(bank, 1)
        return (step - 1) * self.each[bank] + one

    def use(self, kind, n, b):
        slot = next(s for s in self.slots if s[:2] == (kind, n))
        step, bank = b + slot[2], self.bank(slot)
        if isinstance(step, int) and step < 0:
            return bank, self.start[bank] + sum(self.bank(("F", f)) == bank for f in range(n))
        earlier = [s for s in self.slots[:self.slots.index(slot)] if self.bank(s) == bank and self.there(s, step)]
        return bank, self.before(bank, step) + len(earlier)

    def end(self):
        return [self.before(k, B + 1) for k in range(8)]


PROJECTIONS = {
    0: [("q", 0), ("qs", 0), ("k", 0), ("ks", 0), ("q", 1), ("qs", 1), ("k", 1), ("ks", 1), ("v", 0), ("v", 1)],
    1: [("q", 0), ("k", 0), ("q", 1), ("k", 1), ("v", 0), ("v", 1)],
    3: [("qk", 0), ("v", 0)],
}
SPREAD = {0: (3, 3, 2, 2), 1: (2, 1, 1, 2), 3: (1, 0, 0, 1)}
HIDDEN_BLOCKS = {0: 2, 1: 2, 2: 4, 3: 4}
SHARED = 0


def build(nc, A, out):
    ctx = ExitStack()
    with ctx:
        def sb(name, shape, dt=F32):
            return ctx.enter_context(nc.sbuf_tensor(name, shape, dt))

        sems = {}

        def sem(name):
            if name not in sems:
                sems[name] = ctx.enter_context(nc.semaphore(name))
            return sems[name]

        P = [ctx.enter_context(nc.psum_tensor(f"bank{i}", [128, 512], F32)) for i in range(8)]

        x = sb("x", [S, B, D])
        xn = sb("xn", [S, B, D])
        xnT = sb("xnT", [D, B, S])
        cx = sb("cx", [K, B, D])
        cxT = sb("cxT", [D, B, K])
        ident = sb("ident", [128, 128])
        ones = sb("ones", [128, 128])
        upper = sb("upper", [128, 128])
        gates = sb("gates", [128, 8])
        tg = sb("tg", [128, 8])
        half = sb("half", [128, 8])
        stats = sb("stats", [128, B, 6])
        mv = sb("mv", [128, B, 2])
        ve = sb("ve", [128, B])
        rstd = sb("rstd", [128, B])

        w = {}
        for n in ("L0q", "L0qs", "L0k", "L0ks", "L0v", "L0o", "L1q", "L1k", "L1v", "L1o"):
            w[n] = sb(n, [D, H * 64])
        for n in ("L1o2", "L3q", "L3k", "L3v", "L3o"):
            w[n] = sb(n, [D, D])
        gamma = sb("gamma", [128, D])
        cos = sb("cos", [128, S])
        sin = sb("sin", [128, S])
        headmask = sb("headmask", [128, H])
        maskI = sb("maskI", [S, B, K], I32)
        bias0 = sb("bias0", [S, B, K])
        validI = sb("validI", [128, B, K], I32)
        bias3 = sb("bias3", [S, B, K])
        causal = sb("causal", [S, K])
        wsim = sb("wsim", [D, 3])
        bsim = sb("bsim", [128, 1])
        wqv = sb("wqv", [D, 4, D])
        bqv = sb("bqv", [1, D])

        qT = [sb(f"qT{j}", [128, 8, S]) for j in range(2)]
        kM = [sb(f"kM{j}", [128, H, K]) for j in range(2)]
        va = [sb(f"va{j}", [K, H * 64]) for j in range(2)]
        va8 = [sb(f"va8{j}", [K, H, 9]) for j in range(2)]
        cb = [sb(f"cb{j}", [D, K]) for j in range(2)]
        k3 = sb("k3", [128, K])
        rope = [sb(f"rope{j}", [128, 2, 4, S]) for j in range(2)]
        sc = sb("sc", [S, NG, G, K])
        pr = sb("pr", [S, NG, G, K])
        pT = [sb(f"pT{g}", [K, G, S]) for g in range(NG)]
        mx = sb("mx", [S, NG, G])
        rc = sb("rc", [S, NG, G])
        on = sb("on", [S, D])
        oT = [sb(f"oT{j}", [128, 8, S]) for j in range(2)]
        zT = sb("zT", [D, S])
        yb = sb("yb", [S, B, D])

        wr = {n: sb(f"wr{n}", [D, E]) for n in range(4)}
        br = {n: sb(f"br{n}", [128, E]) for n in (1, 2, 3)}
        b2 = {n: sb(f"b2{n}", [E, D]) for n in (1, 2, 3)}
        wg = sb("wg", [D, 2 * 128])
        NB = {0: 2, 1: 2, 2: 4, 3: 4}
        row = {0: 2 * D, 1: 256 + 2 * D + 2, 2: 512 + 4 * D + 4, 3: 512 + 4 * D + 4}
        we = {n: [sb(f"we{n}{j}", [128, row[n]]) for j in range(2)] for n in range(4)}
        hT = [sb(f"hT{j}", [128, 4, HALF]) for j in range(2)]
        lng = sb("lng", [D, 2])
        small = {n: sb(f"r_{n}", [128, B, E]) for n in
                 ("L", "L2", "ex", "eq", "one1", "one2", "pri", "cb", "m")}
        col = {n: sb(f"c_{n}", [128, B]) for n in ("m1", "m2", "z", "rz", "km", "s")}
        combT = sb("combT", [E, B, S])
        c3 = sc[:, 0:2, :, :].rearrange("p a b k -> p (a b) k")
        c2 = sc[:, 2:4, :, :].rearrange("p a b k -> p (a b) k")
        aT = [sb(f"aT{j}", [K, S]) for j in range(2)]
        fq = qT[1]
        fm = yb
        fc = qT[0]
        sim = pr[:, 0:2, :, :].rearrange("p a b k -> p (a b) k")
        m8 = sb("m8", [S, B])
        nm8 = sb("nm8", [S, B])
        z8 = sb("z8", [S, B])
        mT = sb("mT", [B, S])
        row1 = sb("row1", [B, 4])
        bT = sb("bT", [S, B])
        hc = sb("hc", [D, B])

        filled = [sem(f"filled{i}") for i in range(8)]
        taken = [sem(f"taken{i}") for i in range(8)]
        uses, count, attn, ffn = {}, [0] * 8, {}, {}

        def plan_use(key, bank):
            uses[key] = (bank, count[bank])
            count[bank] += 1

        for b in range(B):
            plan_use(("cx", b), b)
        for n in range(4):
            for c_ in range(2):
                plan_use(("turn", f"a{n}", c_), 6 + c_)
            if n == 2:
                for b in range(B):
                    plan_use(("sim", b), b % 2)
                    plan_use(("aT", b), 2 + b % 2)
                    plan_use(("hq", b), 4 + b % 2)
                plan_use("mT", 6)
                plan_use("bT", 7)
                plan_use("hc", 6)
                for b in range(B):
                    plan_use(("feat", b), 6 + b % 2)
            else:
                attn[n] = Attention(PROJECTIONS[n], 8 if n == 3 else 64, 8.0 ** -0.5 if n == 3 else 64.0 ** -0.5,
                                    n != 1, n == 1, SPREAD[n], count)
                count[:] = attn[n].end()
            for c_ in range(2):
                plan_use(("turn", f"f{n}", c_), 6 + c_)
            plan_use(("logits", n), 6)
            if n == 3:
                for c_ in range(2):
                    plan_use(("turn", "i3", c_), 6 + c_)
            if n == SHARED:
                plan_use("rank", 7)
            else:
                plan_use(("combT", n, 0), 6)
                plan_use(("combT", n, 1), 7)
            ffn[n] = list(count)
            if n == SHARED:
                for k in range(4):
                    count[k] += 1
            else:
                for k in range(4):
                    count[k] += UNITS if HIDDEN_BLOCKS[n] == 4 else UNITS // 2
            count[4] += UNITS // 2
            count[5] += UNITS // 2
            if n != SHARED:
                plan_use(("b2", n, 0), 4)
                plan_use(("b2", n, 1), 5)

        def hidden_use(n, i, q, nb):
            if HIDDEN_BLOCKS[n] == 4:
                return nb, 4 * i + (ffn[n][nb] + q)
            bank = 2 * (q % 2) + nb
            return bank, 2 * i + (ffn[n][bank] + q // 2)

        def out_use(n, i, q):
            return 4 + q % 2, 2 * i + (ffn[n][4 + q % 2] + q // 2)

        def fill(pe, use):
            if positive(use[1]):
                pe.wait_ge(taken[use[0]], use[1])
            return P[use[0]]

        def read(eng, use):
            eng.wait_ge(filled[use[0]], use[1] + 1)
            return P[use[0]]

        def after(eng, use):
            eng.wait_ge(taken[use[0]], use[1] + 1)

        block = ctx.enter_context(nc.Block())

        def bc(ap, shape):
            return ap.to_broadcast(shape)

        loads = {}

        def loaded(eng, group):
            eng.wait_ge(sem("ld_" + group), loads[group])

        def row_of(ap):
            return ap.rearrange("(a n) -> a n", a=1)

        def all_rows(ap, n):
            return row_of(ap).to_broadcast([128, n])

        plan = []

        def want(group, dst, src):
            plan.append((group, dst, src))
            loads[group] = loads.get(group, 0) + 16

        want("x", x[:, :, :], A["x"].rearrange("b t d -> t b d"))
        want("cx", cx[:, :, :], A["ctx_1024"].rearrange("b t d -> t b d"))
        want("gates", gates[:, 0:4], all_rows(A["g_xattn"], 4))
        want("gates", gates[:, 4:8], all_rows(A["g_ffn"], 4))
        want("w0", w["L0v"][:, :], A["L0_xattn_Wv"])
        want("w0", w["L0q"][:, :], A["L0_xattn_Wq"])
        want("w0", w["L0qs"][:, :], A["L0_xattn_Wq_swapped"])
        want("w0", w["L0k"][:, :], A["L0_xattn_Wk"])
        want("w0", w["L0ks"][:, :], A["L0_xattn_Wk_swapped"])
        want("cos", cos[:, :], A["rope_cos"])
        want("cos", sin[:, :], A["rope_sin"])
        want("mask", maskI[:, :, :], A["mask_BxSxS2_ik0"].rearrange("b q k -> q b k"))
        want("wo0", w["L0o"][:, :].rearrange("p (n d) -> p n d", d=D), A["L0_xattn_Wo"].rearrange("(n p) d -> p n d", p=128))
        want("f0", wr[0][:, :], A["L0_ffn_w_router"])
        want("f0", wg[:, :], A["L0_ffn_w_gate"])
        for j in range(2):
            want(f"e0{j}", we[0][j][:, :], A["L0_experts"][j])
        want("w1", w["L1v"][:, :], A["L1_xattn_w_kv"][:, H * 64:])
        want("w1", w["L1q"][:, :], A["L1_xattn_w_q"])
        want("w1", w["L1k"][:, :], A["L1_xattn_w_kv"][:, 0:H * 64])
        want("w1", w["L1o"][:, :].rearrange("p (n d) -> p n d", d=D), A["L1_xattn_w_out1"].rearrange("(n p) d -> p n d", p=128))
        want("w1", w["L1o2"][:, :], A["L1_xattn_w_out2"])
        want("w1", gamma[:, :], all_rows(A["L1_xattn_gamma"], D))
        want("f1", wr[1][:, :], A["L1_ffn_Wg"])
        want("f1", br[1][:, :], all_rows(A["L1_ffn_bg"], E))
        want("f1", b2[1][:, :], A["L1_ffn_b2"])
        want("w2", wsim[:, :], A["L2_xattn_w_sim"])
        want("w2", bsim[:, :], all_rows(A["L2_xattn_b_sim"], 1))
        want("w2", wqv[:, :, :], A["L2_xattn_W_qv"].rearrange("(n p) d -> p n d", p=128))
        want("w2", bqv[:, :], row_of(A["L2_xattn_b_qv"]))
        want("f2", wr[2][:, :], A["L2_ffn_gate_w"])
        want("f2", br[2][:, :], all_rows(A["L2_ffn_gate_b"], E))
        want("f2", b2[2][:, :], A["L2_ffn_b2"])
        want("w3", w["L3q"][:, :], A["L3_xattn_Wq"])
        want("w3", w["L3k"][:, :], A["L3_xattn_Wk"])
        want("w3", w["L3v"][:, :], A["L3_xattn_Wv"])
        want("w3", w["L3o"][:, :], A["L3_xattn_Wo"])
        want("w3", validI[:, :, :], A["mask_BxS2_if1"].rearrange("(a b) k -> a b k", a=1).to_broadcast([128, B, K]))
        want("f3", wr[3][:, :], A["L3_ffn_Wr"])
        want("f3", br[3][:, :], all_rows(A["L3_ffn_br"], E))
        want("f3", b2[3][:, :], A["L3_ffn_b2"])
        want("f3", lng[:, :], A["L3_ffn_ln"])
        for n in (1, 2, 3):
            for j in range(2):
                want(f"e{n}{j}", we[n][j][:, :], A[f"L{n}_experts"][j])

        @block.sync
        def _(sp):
            for group, dst, src in plan:
                sp.dma_start(dst, src).then_inc(sem("ld_" + group), 16)
            for n in range(4):
                with sp.Fori(1, E // 2) as i:
                    for j in range(2):
                        sp.wait_ge(filled[5], 2 * i + (ffn[n][5] + j - 1))
                        sp.dma_start(we[n][j][:, :], A[f"L{n}_experts"][bass.ds(2 * i + j, 1), :, :].rearrange("a p f -> (a p) f"))\
                          .then_inc(sem(f"ld_e{n}{j}"), 16)
            after(sp, uses["b2", 3, 0])
            after(sp, uses["b2", 3, 1])
            sp.dma_start(out.rearrange("b t d -> t b d"), x[:, :, :]).then_inc(sem("stored"), 16)
            sp.wait_ge(sem("stored"), 16)

        def one(tile, b):
            return tile[:, bass.ds(b, 1), :].rearrange("p a n -> p (a n)")

        LN = {name: i for i, name in enumerate(("a0", "f0", "a1", "y1", "f1", "a2", "f2", "a3", "f3", "i3"))}

        def normalise(v, c, st, src, dst):
            for t in range(B):
                c(v.bn_stats(stats[:, t, :], src[:, t, :]))
                c(v.bn_aggr(mv[:, t, :], stats[:, t, :]))
            v.tensor_scalar(ve[:, :], mv[:, :, 1], EPS, None, ALU.add).then_inc(sem("ln_var"), 1)
            v.wait_ge(sem("ln_rstd"), LN[st] + 1)
            for t in range(B):
                v.tensor_scalar(dst[:, t, :], src[:, t, :], mv[:, t, 0:1], rstd[:, t:t + 1], ALU.subtract, ALU.mult)\
                 .then_inc(sem("ln_out"), 1)

        def root(g, st):
            g.wait_ge(sem("ln_var"), LN[st] + 1)
            g.tensor_tensor(rstd[:, :], ve[:, :], half[:, :], ALU.pow).then_inc(sem("ln_rstd"), 1)

        def turn_tensor(pe, st, src):
            for c_ in range(2):
                bank = fill(pe, uses["turn", st, c_])
                for t in range(4):
                    pe.wait_ge(sem("ln_out"), B * LN[st] + 4 * c_ + t + 1)
                    last = nc.tensor.transpose(bank[:, t * S:(t + 1) * S], src[:, 4 * c_ + t, :], ident[:, :])
                last.then_inc(filled[6 + c_], 1)

        def turn_scalar(a, st, dst):
            for c_ in range(2):
                bank = read(a, uses["turn", st, c_])
                if st == "i3":
                    nc.scalar.activation(dst[:, 4 * c_:4 * c_ + 4, :], bank[:, :].rearrange("p (t s) -> p t s", t=4),
                                         ACT.Identity, bias=lng[:, 1:2], scale=lng[:, 0:1]).then_inc(taken[6 + c_], 1)
                else:
                    nc.scalar.activation(dst[:, 4 * c_:4 * c_ + 4, :], bank[:, :].rearrange("p (t s) -> p t s", t=4),
                                         ACT.Copy).then_inc(taken[6 + c_], 1)

        def turned(eng, st):
            after(eng, uses["turn", st, 0])
            after(eng, uses["turn", st, 1])

        def rounds(eng, m, project, work):

            def step(s, parity):
                for slot in m.slots:
                    if m.there(slot, s):
                        kind, n, late = slot
                        if kind == "F":
                            project(s + 1, 1 - parity, n)
                        else:
                            work(kind, n, s - late, (parity + late) % 2)

            for f in range(len(m.fills)):
                project(0, 0, f)
            for s in (0, 1):
                step(s, s % 2)
            with eng.Fori(1, B // 2 - 1) as i:
                for j in range(2):
                    step(2 * i + j, j)
            for s in range(B - 2, B + 1):
                step(s, s % 2)

        def mha_tensor(pe, n):
            m = attn[n]

            def project(b, j, f):
                kind, part = m.fills[f]
                use = m.use("F", f, b)
                bank = fill(pe, use)
                xb, cxb = one(xnT, b), one(cxT, b)
                if kind == "v":
                    pe.wait_ge(sem(f"cb{n}"), b + 1)
                    width = 512 if m.wide else D
                    last = nc.tensor.matmul(bank[0:K, 0:width], cb[j][:, :], w[f"L{n}v"][:, part * 512:part * 512 + width],
                                            start=True, stop=True)
                elif kind == "qk":
                    nc.tensor.matmul(bank[:, 0:S], w["L3q"][:, :], xb, start=True, stop=True)
                    last = nc.tensor.matmul(bank[:, S:S + K], w["L3k"][:, :], cxb, start=True, stop=True)
                else:
                    rhs, width = (xb, S) if kind[0] == "q" else (cxb, K)
                    for i in range(4):
                        o = part * 512 + i * 128
                        last = nc.tensor.matmul(bank[:, i * width:(i + 1) * width], w[f"L{n}{kind}"][:, o:o + 128], rhs,
                                                start=True, stop=True)
                last.then_inc(filled[use[0]], 1)

            def projected(pe, b, values):
                for k in m.PROJECTED:
                    last = [f for f, (kind, _) in enumerate(m.fills) if (kind == "v") == values and m.bank(("F", f)) == k]
                    if last:
                        after(pe, m.use("F", last[-1], b))

            def work(kind, g, b, j):
                if kind not in "XN":
                    use = m.use(kind, g, b)
                    bank = fill(pe, use)
                    if kind == "A" and g == 0:
                        projected(pe, b, True)
                    if kind == "S":
                        if g == 0:
                            projected(pe, b, False)
                            if n == 0:
                                pe.wait_ge(sem("roped"), 6 * b + 6)
                            elif n == 1:
                                pe.wait_ge(sem("k_low"), 2 * b + 2)
                            else:
                                pe.wait_ge(sem("k_spread"), b + 1)
                        if m.wide:
                            for i in range(2):
                                h = G * g + 2 * i
                                last = nc.tensor.matmul(bank[:, 2 * i * K:2 * (i + 1) * K], qT[j][:, h // 2, :],
                                                        kM[j][:, h:h + 2, :], start=True, stop=True)
                        else:
                            last = nc.tensor.matmul(bank[:, 0:G * K], qT[j][:, 0, :], kM[j][:, G * g:G * g + G, :],
                                                    start=True, stop=True)
                    elif kind == "T":
                        pe.wait_ge(sem(f"weights{n}" if m.wide else f"probs{n}"), NG * b + (g + 1))
                        for i in range(G):
                            last = nc.tensor.transpose(bank[0:K, i * S:(i + 1) * S], pr[:, g, i, :], ident[:, :])
                    elif kind == "A" and m.wide:
                        after(pe, m.use("T", g, b))
                        for i in range(2):
                            h = G * g + 2 * i
                            last = nc.tensor.matmul(bank[:, 2 * i * S:2 * (i + 1) * S], va[j][:, h * 64:(h + 2) * 64],
                                                    pT[g][:, 2 * i:2 * i + 2, :], start=True, stop=True)
                    elif kind == "A":
                        after(pe, m.use("T", g, b))
                        for i in range(G):
                            last = nc.tensor.matmul(bank[:, i * 9:(i + 1) * 9], pT[g][:, i, :], va8[j][:, G * g + i, :],
                                                    start=True, stop=True)
                    elif kind == "R":
                        after(pe, m.use("A", NG - 1, b))
                        last = nc.tensor.transpose(bank[:, 0:S], on[:, :], ident[:, :])
                    elif kind == "Z":
                        after(pe, m.use("A", NG - 1, b))
                        for i in range(8):
                            last = nc.tensor.matmul(bank[:, 0:S], w["L1o"][:, i * D:(i + 1) * D], oT[j][:, i, :],
                                                    start=i == 0, stop=i == 7)
                    elif n == 1:
                        last = nc.tensor.matmul(bank[:, 0:D], zT[:, :], w["L1o2"][:, :], start=True, stop=True)
                    else:
                        if n == 0:
                            loaded(pe, "wo0")
                        after(pe, m.use(*(("A", NG - 1) if m.wide else ("R", 0)), b))
                        blocks = 8 if m.wide else 1
                        for i in range(blocks):
                            last = nc.tensor.matmul(bank[:, 0:D], oT[j][:, i, :], w[f"L{n}o"][:, i * D:(i + 1) * D],
                                                    start=i == 0, stop=i == blocks - 1)
                    last.then_inc(filled[use[0]], 1)

            loaded(pe, f"w{n}")
            turned(pe, f"a{n}")
            if n == 0:
                for b in range(B):
                    after(pe, uses["cx", b])
            rounds(pe, m, project, work)

        def mha_vector(v, n):
            m = attn[n]

            def project(b, j, f):
                kind, part = m.fills[f]
                use = m.use("F", f, b)
                if f == 0:
                    if positive(b):
                        for k in m.PROJECTED:
                            v.wait_ge(filled[k], m.before(k, b - 1))
                    v.tensor_scalar(cb[j][:, :], one(cxT, b), 1.0, None, ALU.mult).then_inc(sem(f"cb{n}"), 1)
                if n == 0 and kind != "v":
                    is_k, is_swapped = kind[0] == "k", kind.endswith("s")
                    pair, width = 2 * part + is_k, K if is_k else S
                    if not is_swapped:
                        done = 6 * b + {0: -2, 1: 0, 2: 1, 3: 3}[pair]
                        if positive(done):
                            v.wait_ge(sem("roped"), done)
                    bank = read(v, use)
                    table = (sin if is_swapped else cos)[:, 0:width].unsqueeze(1).to_broadcast([128, 4, width])
                    v.tensor_tensor(rope[pair % 2][:, int(is_swapped), :, 0:width],
                                    bank[:, 0:4 * width].rearrange("p (n t) -> p n t", n=4), table, ALU.mult)\
                     .then_inc(taken[use[0]], 1)
                if n == 1 and kind == "k":
                    bank = read(v, use)
                    for e, done in ((0, sem("k_low")), (1, taken[use[0]])):
                        p_ = slice(64 * e, 64 * e + 64)
                        v.tensor_copy(kM[j][p_, 8 * part + e:8 * part + 8:2, :],
                                      bank[p_, 0:4 * K].rearrange("p (n t) -> p n t", n=4)).then_inc(done, 1)

            def work(kind, g, b, j):
                if kind not in "XN":
                    use = m.use(kind, g, b)
                    if kind == "S":
                        raw = read(v, use)[:, 0:G * K].rearrange("p (h k) -> p h k", h=G)
                        if m.masked:
                            bias = (bias0 if n == 0 else bias3)[:, bass.ds(b, 1), :].to_broadcast([S, G, K])
                            v.tensor_tensor(sc[:, g, :, :], raw, bias, ALU.add).then_inc(taken[use[0]], 1)
                            after(v, use)
                            raw = sc[:, g, :, :]
                        v.tensor_reduce(mx[:, g, :], raw, AX_X, ALU.max).then_inc(sem(f"max{n}"), 1)
                        v.wait_ge(sem(f"max{n}"), NG * b + (g + 1))
                        v.tensor_tensor(sc[:, g, :, :], raw, mx[:, g, :].unsqueeze(2).to_broadcast([S, G, K]), ALU.subtract)\
                         .then_inc(sem("shifted3" if n == 3 else "shifted0") if m.masked else taken[use[0]], 1)
                    if kind == "A" and not m.wide:
                        raw = read(v, use)[:, 0:G * 9].rearrange("p (h d) -> p h d", h=G)
                        v.reciprocal(rc[:, g, :], raw[:, :, 8]).then_inc(sem(f"inverse{n}"), 1)
                        v.wait_ge(sem(f"inverse{n}"), NG * b + (g + 1))
                        v.tensor_tensor(on[:, G * g * 8:G * (g + 1) * 8].rearrange("p (h d) -> p h d", h=G),
                                        raw[:, :, 0:8], rc[:, g, :].unsqueeze(2).to_broadcast([S, G, 8]), ALU.mult)\
                         .then_inc(taken[use[0]], 1)
                    if kind == "Y":
                        bank = read(v, use)
                        if n == 1:
                            v.tensor_copy(one(yb, b), bank[:, 0:D]).then_inc(taken[use[0]], 1)
                        else:
                            v.scalar_tensor_tensor(one(x, b), bank[:, 0:D], tg[:, n:n + 1], one(x, b), ALU.mult, ALU.add)\
                             .then_inc(taken[use[0]], 1)
                elif kind == "N":
                    v.wait_ge(sem(f"probs{n}"), NG * b + (g + 1))
                    v.tensor_reduce(mx[:, g, :], pr[:, g, :, :], AX_X, ALU.add).then_inc(sem(f"sum{n}"), 1)
                    v.wait_ge(sem(f"sum{n}"), NG * b + (g + 1))
                    v.reciprocal(rc[:, g, :], mx[:, g, :]).then_inc(sem(f"inverse{n}"), 1)
                    v.wait_ge(sem(f"inverse{n}"), NG * b + (g + 1))
                    v.tensor_tensor(pr[:, g, :, :], pr[:, g, :, :], rc[:, g, :].unsqueeze(2).to_broadcast([S, G, K]), ALU.mult)\
                     .then_inc(sem(f"weights{n}"), 1)

            rounds(v, m, project, work)
            after(v, m.use("Y", 0, B - 1))

        def mha_scalar(a, n):
            m = attn[n]

            def project(b, j, f):
                kind, part = m.fills[f]
                use = m.use("F", f, b)
                if kind == "v":
                    bank = read(a, use)
                    if m.wide:
                        nc.scalar.activation(va[j][:, 512 * part:512 * part + 512], bank[0:K, 0:512], ACT.Copy)\
                          .then_inc(taken[use[0]], 1)
                    else:
                        nc.scalar.activation(va8[j][:, :, 0:8], bank[0:K, 0:D].rearrange("p (h d) -> p h d", h=H), ACT.Copy)\
                          .then_inc(taken[use[0]], 1)
                if n == 1 and kind == "q":
                    bank = read(a, use)
                    nc.scalar.activation(qT[j][:, 4 * part:4 * part + 4, :], bank[:, :].rearrange("p (n t) -> p n t", n=4),
                                         ACT.Copy).then_inc(taken[use[0]], 1)
                if kind == "qk":
                    bank = read(a, use)
                    nc.scalar.activation(qT[j][:, 0, :], bank[:, 0:S], ACT.Copy).then_inc(sem("q_taken"), 1)
                    if positive(b):
                        a.wait_ge(sem("k_spread"), b)
                    nc.scalar.activation(k3[:, :], bank[:, S:S + K], ACT.Copy).then_inc(taken[use[0]], 1)

            def work(kind, g, b, j):
                if kind == "X":
                        if m.masked:
                            a.wait_ge(sem("shifted3" if n == 3 else "shifted0"), NG * b + (g + 1))
                        else:
                            after(a, m.use("S", g, b))
                        nc.scalar.activation(pr[:, g, :, :], sc[:, g, :, :], ACT.Exp, scale=m.scale).then_inc(sem(f"probs{n}"), 1)
                elif kind != "N":
                    use = m.use(kind, g, b)
                    if kind == "T":
                        bank = read(a, use)
                        nc.scalar.activation(pT[g][:, :, :], bank[0:K, :].rearrange("p (h t) -> p h t", h=G), ACT.Copy)\
                          .then_inc(taken[use[0]], 1)
                    if kind == "A" and m.wide:
                        bank = read(a, use)
                        for e in range(2):
                            p_ = slice(64 * e, 64 * e + 64)
                            last = nc.scalar.activation(oT[j][p_, 2 * g:2 * g + 2, :],
                                                        bank[p_, :].rearrange("p (i e t) -> p i e t", i=2, e=2)[:, :, e, :], ACT.Copy)
                        last.then_inc(taken[use[0]], 1)
                    if kind == "R":
                        bank = read(a, use)
                        nc.scalar.activation(oT[j][:, 0, :], bank[:, 0:S], ACT.Copy).then_inc(taken[use[0]], 1)
                    if kind == "Z":
                        bank = read(a, use)
                        nc.scalar.activation(zT[:, :], bank[:, 0:S], ACT.Relu).then_inc(taken[use[0]], 1)

            rounds(a, m, project, work)

        def mha_pool(g_, n):
            m = attn[n]

            def project(b, j, f):
                kind, part = m.fills[f]
                use = m.use("F", f, b)
                if n == 0 and kind.endswith("s"):
                    is_k = kind[0] == "k"
                    pair, width = 2 * part + is_k, K if is_k else S
                    after(g_, m.use("F", f - 1, b))
                    after(g_, use)
                    r = rope[pair % 2]
                    done = 6 * b + (0, 1, 3, 4)[pair]
                    if positive(done):
                        g_.wait_ge(sem("roped"), done)
                    if not is_k:
                        g_.tensor_tensor(qT[j][:, 4 * part:4 * part + 4, :], r[:, 0, :, :], r[:, 1, :, :], ALU.add)\
                          .then_inc(sem("roped"), 1)
                    else:
                        for e in range(2):
                            p_ = slice(64 * e, 64 * e + 64)
                            if e:
                                g_.wait_ge(sem("roped"), done + 1)
                            g_.tensor_tensor(kM[j][p_, 8 * part + e:8 * part + 8:2, :], r[p_, 0, :, 0:K], r[p_, 1, :, 0:K], ALU.add)\
                              .then_inc(sem("roped"), 1)
                if kind == "qk":
                    after(g_, use)
                    g_.tensor_tensor(kM[j][:, :, :], k3[:, :].unsqueeze(1).to_broadcast([128, H, K]),
                                     headmask[:, :].unsqueeze(2).to_broadcast([128, H, K]), ALU.mult)\
                      .then_inc(sem("k_spread"), 1)

            if n != 1:
                rounds(g_, m, project, lambda *slot: None)

        def coat_tensor(pe):
            loaded(pe, "w2")
            turned(pe, "a2")
            pe.wait_ge(sem("c3"), 2)
            for b in range(B):
                bank = fill(pe, uses["sim", b])
                nc.tensor.matmul(bank[:, 0:K], xnT[:, b, :], c3[:, b, :], start=True, stop=False)
                nc.tensor.matmul(bank[:, 0:K], ones[:, :], c2[:, b, :], start=False, stop=True).then_inc(filled[b % 2], 1)
                if b:
                    coat_turn(pe, b - 1)
            coat_turn(pe, B - 1)
            bank = fill(pe, uses["mT"])
            pe.wait_ge(sem("largest"), B)
            nc.tensor.transpose(bank[0:B, 0:S], m8[:, :], ident[:, :]).then_inc(filled[6], 1)
            bank = fill(pe, uses["bT"])
            pe.wait_ge(sem("token_weights"), 1)
            nc.tensor.transpose(bank[:, 0:B], mT[:, :], ident[0:B, 0:B]).then_inc(filled[7], 1)
            bank = fill(pe, uses["hc"])
            after(pe, uses["bT"])
            for b in range(B):
                last = nc.tensor.matmul(bank[:, b:b + 1], xn[:, b, :], bT[:, b:b + 1], start=True, stop=True)
            last.then_inc(filled[6], 1)
            for b in range(B):
                bank = fill(pe, uses["feat", b])
                pe.wait_ge(sem("by_bar"), b + 1)
                for i, feature in enumerate((xnT, fq, fm, fc)):
                    nc.tensor.matmul(bank[:, 0:D], feature[:, b, :], wqv[:, i, :], start=i == 0, stop=False)
                nc.tensor.matmul(bank[:, 0:D], ones[0:1, :], bqv[:, :], start=False, stop=True).then_inc(filled[6 + b % 2], 1)

        def coat_turn(pe, b):
            bank = fill(pe, uses["aT", b])
            pe.wait_ge(sem("a_weights"), b + 1)
            nc.tensor.transpose(bank[0:K, 0:S], sim[:, b, :], ident[:, :]).then_inc(filled[2 + b % 2], 1)
            bank = fill(pe, uses["hq", b])
            after(pe, uses["aT", b])
            nc.tensor.matmul(bank[:, 0:S], cx[:, b, :], aT[b % 2][:, :], start=True, stop=True).then_inc(filled[4 + b % 2], 1)

        def coat_scalar(a):
            for b in range(B):
                a.wait_ge(sem("largest_neg"), b + 1)
                nc.scalar.activation(sim[:, b, :], sim[:, b, :], ACT.Exp, bias=nm8[:, b:b + 1], accum_out=z8[:, b:b + 1])\
                  .then_inc(sem("a_exp"), 1)
                if b:
                    coat_take(a, b - 1)
            coat_take(a, B - 1)
            a.wait_ge(sem("row_max"), 1)
            nc.scalar.activation(mT[:, :], mT[:, :], ACT.Exp, bias=row1[:, 0:1], accum_out=row1[:, 1:2]).then_inc(sem("row_exp"), 1)

        def coat_take(a, b):
            bank = read(a, uses["aT", b])
            nc.scalar.activation(aT[b % 2][:, :], bank[0:K, 0:S], ACT.Copy).then_inc(taken[2 + b % 2], 1)

        def coat_vector(v, c):
            loaded(v, "w2")
            v.tensor_scalar(c3[:, :, :], cxT[:, :, :], wsim[:, 2:3], wsim[:, 0:1], ALU.mult, ALU.add).then_inc(sem("c3"), 1)
            v.tensor_scalar(c2[:, :, :], cxT[:, :, :], wsim[:, 1:2], None, ALU.mult).then_inc(sem("c3"), 1)

            def features(b):
                bank = read(v, uses["hq", b])
                c(v.tensor_copy(fq[:, b, :], bank[:, 0:S]))
                v.tensor_tensor(fm[:, b, :], bank[:, 0:S], xnT[:, b, :], ALU.mult).then_inc(taken[4 + b % 2], 1)

            def weights(b):
                v.wait_ge(sem("a_exp"), b + 1)
                c(v.reciprocal(col["rz"][:, b:b + 1], z8[:, b:b + 1]))
                v.tensor_scalar(sim[:, b, :], sim[:, b, :], col["rz"][:, b:b + 1], None, ALU.mult).then_inc(sem("a_weights"), 1)

            for b in range(B):
                bank = read(v, uses["sim", b])
                v.tensor_scalar(sim[:, b, :], bank[:, 0:K], bsim[:, 0:1], None, ALU.add).then_inc(taken[b % 2], 1)
                after(v, uses["sim", b])
                v.tensor_reduce(m8[:, b:b + 1], sim[:, b, :], AX_X, ALU.max).then_inc(sem("largest"), 1)
                v.wait_ge(sem("largest"), b + 1)
                v.tensor_scalar(nm8[:, b:b + 1], m8[:, b:b + 1], -1.0, None, ALU.mult).then_inc(sem("largest_neg"), 1)
                if b:
                    weights(b - 1)
                if b > 1:
                    features(b - 2)
            weights(B - 1)
            features(B - 2)
            features(B - 1)
            bank = read(v, uses["mT"])
            v.tensor_copy(mT[:, :], bank[0:B, 0:S]).then_inc(taken[6], 1)
            after(v, uses["mT"])
            v.tensor_reduce(row1[:, 0:1], mT[:, :], AX_X, ALU.max, negate=True).then_inc(sem("row_max"), 1)
            v.wait_ge(sem("row_exp"), 1)
            c(v.reciprocal(row1[:, 2:3], row1[:, 1:2]))
            v.tensor_scalar(mT[:, :], mT[:, :], row1[:, 2:3], None, ALU.mult).then_inc(sem("token_weights"), 1)
            bank = read(v, uses["bT"])
            v.tensor_copy(bT[:, :], bank[:, 0:B]).then_inc(taken[7], 1)
            bank = read(v, uses["hc"])
            v.tensor_copy(hc[:, :], bank[:, 0:B]).then_inc(taken[6], 1)
            after(v, uses["hc"])
            for b in range(B):
                v.tensor_scalar(fc[:, b, :], xnT[:, b, :], hc[:, b:b + 1], None, ALU.mult).then_inc(sem("by_bar"), 1)
            for b in range(B):
                bank = read(v, uses["feat", b])
                v.scalar_tensor_tensor(x[:, b, :], bank[:, 0:D], tg[:, 2:3], x[:, b, :], ALU.mult, ALU.add)\
                 .then_inc(taken[6 + b % 2], 1)
            after(v, uses["feat", B - 2])
            after(v, uses["feat", B - 1])

        def ffn_loop(eng, unit):
            with eng.Fori(0, E // 2 - 1) as i:
                for q in range(4):
                    unit(i, q)
            for q in range(4):
                unit(E // 2 - 1, q)

        def ffn_tensor(pe, n):
            blocks = HIDDEN_BLOCKS[n]
            width = 128 * blocks
            src = fq if n == 3 else xnT

            def hidden(i, q):
                j = q // 2
                if n != SHARED and q % 2 == 0:
                    pe.wait_ge(sem(f"ld_e{n}{j}"), 16 * i + 16)
                weights = wg if n == SHARED else we[n][j]
                for nb in range(blocks):
                    use = hidden_use(n, i, q, nb)
                    bank = fill(pe, use)
                    nc.tensor.matmul(bank[:, :], weights[:, nb * 128:(nb + 1) * 128], src[:, 4 * (q % 2):4 * (q % 2) + 4, :],
                                     start=True, stop=True).then_inc(filled[use[0]], 1)

            def outputs(i, q):
                j, c_ = q // 2, q % 2
                offset = 0 if n == SHARED else width
                if n == SHARED and c_ == 0:
                    pe.wait_ge(sem(f"ld_e{n}{j}"), 16 * i + 16)
                use = out_use(n, i, q)
                bank = fill(pe, use)
                for t in range(4):
                    for nb in range(blocks):
                        if n == SHARED:
                            if t == 0:
                                after(pe, hidden_use(n, 0, c_, nb))
                        elif t == 0:
                            after(pe, hidden_use(n, i, q, nb))
                        last = nc.tensor.matmul(bank[:, t * D:(t + 1) * D], hT[c_][:, nb, t * S:(t + 1) * S],
                                                we[n][j][:, offset + nb * D:offset + (nb + 1) * D],
                                                start=nb == 0, stop=nb == blocks - 1)
                last.then_inc(filled[use[0]], 1)

            def unit(i, q):
                if n != SHARED:
                    if q < 3:
                        hidden(i, q + 1)
                    elif not isinstance(i, int):
                        hidden(i + 1, 0)
                outputs(i, q)

            loaded(pe, f"f{n}")
            turned(pe, f"f{n}")
            bank = fill(pe, uses["logits", n])
            for t in range(B):
                last = nc.tensor.matmul(bank[:, t * E:(t + 1) * E], xnT[:, t, :], wr[n][:, :], start=True, stop=True)
            last.then_inc(filled[6], 1)
            if n == 3:
                turn_tensor(pe, "i3", yb)
                turned(pe, "i3")
            hidden(0, 0)
            if n == SHARED:
                hidden(0, 1)
                pe.wait_ge(sem("chosen"), 1)
                bank = fill(pe, uses["rank"])
                nc.tensor.matmul(bank[:, 0:E], upper[:, :], small["m"][:, 0, :], start=True, stop=True)
                nc.tensor.matmul(bank[:, E:B * E], upper[:, :], small["m"][:, 1:B, :], start=True, stop=False)
                for t in range(B - 2, -1, -1):
                    later = B - 1 - t
                    last = nc.tensor.matmul(bank[:, (t + 1) * E:B * E], ones[:, :],
                                            small["m"][:, t:t + 1, :].to_broadcast([128, later, E]),
                                            start=False, stop=t == 0, skip_group_check=t > 0)
                last.then_inc(filled[7], 1)
            ffn_loop(pe, unit)
            if n != SHARED:
                for c_ in range(2):
                    bank = fill(pe, uses["combT", n, c_])
                    if c_ == 0:
                        pe.wait_ge(sem("combined"), n + 1)
                    for t in range(4):
                        last = nc.tensor.transpose(bank[0:E, t * S:(t + 1) * S], small["cb"][:, 4 * c_ + t, :], ident[:, :])
                    last.then_inc(filled[6 + c_], 1)
                for c_ in range(2):
                    bank = fill(pe, uses["b2", n, c_])
                    after(pe, uses["combT", n, c_])
                    for t in range(4):
                        last = nc.tensor.matmul(bank[:, t * D:(t + 1) * D], combT[:, 4 * c_ + t, :], b2[n][:, :],
                                                start=True, stop=True)
                    last.then_inc(filled[4 + c_], 1)

        def ffn_scalar(a, n):
            blocks = HIDDEN_BLOCKS[n]
            func = {0: ACT.Silu, 1: ACT.Relu, 2: ACT.Gelu, 3: ACT.Relu}[n]

            def hidden(i, q):
                for nb in range(blocks):
                    use = hidden_use(n, i, q, nb)
                    bank = read(a, use)
                    if n == SHARED:
                        nc.scalar.activation(hT[q % 2][:, nb, :], bank[:, :], func).then_inc(taken[use[0]], 1)
                    else:
                        at = 2 * 128 * blocks + nb
                        nc.scalar.activation(hT[q % 2][:, nb, :], bank[:, :], func, bias=we[n][q // 2][:, at:at + 1])\
                          .then_inc(taken[use[0]], 1)

            def unit(i, q):
                if q < 3:
                    hidden(i, q + 1)
                elif not isinstance(i, int):
                    hidden(i + 1, 0)

            a.wait_ge(sem("route_max"), n + 1)
            nc.scalar.activation(small["ex"][:, :, :], small["ex"][:, :, :], ACT.Exp).then_inc(sem("route_exp"), 1)
            if n == 3:
                loaded(a, "f3")
                turn_scalar(a, "i3", fq)
            hidden(0, 0)
            if n == SHARED:
                hidden(0, 1)
            else:
                ffn_loop(a, unit)
                for c_ in range(2):
                    bank = read(a, uses["combT", n, c_])
                    nc.scalar.activation(combT[:, 4 * c_:4 * c_ + 4, :], bank[0:E, :].rearrange("p (t s) -> p t s", t=4), ACT.Copy)\
                      .then_inc(taken[6 + c_], 1)

        def ffn_vector(v, c, n):
            s3 = small

            def wide(tile):
                return tile[:, :].unsqueeze(2).to_broadcast([128, B, E])

            def first_largest(values, largest, chosen):
                c(v.tensor_tensor(s3["eq"][:, :, :], values[:, :, :], wide(largest), ALU.is_equal))
                c(v.tensor_tensor(s3["eq"][:, :, :], s3["eq"][:, :, :], s3["pri"][:, :, :], ALU.mult))
                c(v.tensor_reduce(col["km"][:, :], s3["eq"][:, :, :], AX_X, ALU.max))
                c(v.tensor_tensor(chosen[:, :, :], s3["eq"][:, :, :], wide(col["km"]), ALU.is_equal))

            loaded(v, f"f{n}")
            use = uses["logits", n]
            logits = read(v, use)[:, 0:B * E].rearrange("p (t e) -> p t e", t=B)
            if n == SHARED:
                v.tensor_copy(s3["L"][:, :, :], logits).then_inc(taken[6], 1)
            else:
                v.tensor_tensor(s3["L"][:, :, :], logits, br[n][:, :].unsqueeze(1).to_broadcast([128, B, E]), ALU.add)\
                 .then_inc(taken[6], 1)
            after(v, use)
            c(v.tensor_reduce(col["m1"][:, :], s3["L"][:, :, :], AX_X, ALU.max))
            v.tensor_tensor(s3["ex"][:, :, :], s3["L"][:, :, :], wide(col["m1"]), ALU.subtract).then_inc(sem("route_max"), 1)
            if n == 3:
                normalise(v, c, "i3", xn, yb)
            first_largest(s3["L"], col["m1"], s3["one1"])
            v.wait_ge(sem("route_exp"), n + 1)
            if n in (0, 3):
                c(v.tensor_reduce(col["z"][:, :], s3["ex"][:, :, :], AX_X, ALU.add))
                c(v.reciprocal(col["rz"][:, :], col["z"][:, :]))
            if n == 3:
                c(v.tensor_scalar(s3["m"][:, :, :], s3["one1"][:, :, :], tg[:, 7:8], None, ALU.mult))
                v.tensor_tensor(s3["cb"][:, :, :], s3["m"][:, :, :], wide(col["rz"]), ALU.mult).then_inc(sem("combined"), 1)
            else:
                c(v.scalar_tensor_tensor(s3["L2"][:, :, :], s3["one1"][:, :, :], -3.0e38, s3["L"][:, :, :], ALU.mult, ALU.add))
                c(v.tensor_reduce(col["m2"][:, :], s3["L2"][:, :, :], AX_X, ALU.max))
                first_largest(s3["L2"], col["m2"], s3["one2"])
                v.tensor_tensor(s3["m"][:, :, :], s3["one1"][:, :, :], s3["one2"][:, :, :], ALU.add).then_inc(sem("chosen"), 1)
                v.wait_ge(sem("chosen"), n + 1)
                if n == SHARED:
                    c(v.tensor_tensor(s3["ex"][:, :, :], s3["ex"][:, :, :], wide(col["rz"]), ALU.mult))
                c(v.tensor_tensor(s3["ex"][:, :, :], s3["ex"][:, :, :], s3["m"][:, :, :], ALU.mult))
                if n == SHARED:
                    use = uses["rank"]
                    rank = read(v, use)[:, 0:B * E].rearrange("p (t e) -> p t e", t=B)
                    v.scalar_tensor_tensor(s3["ex"][:, :, :], rank, CAPACITY + 0.5, s3["ex"][:, :, :], ALU.is_lt, ALU.mult)\
                     .then_inc(taken[7], 1)
                    after(v, use)
                c(v.tensor_reduce(col["s"][:, :], s3["ex"][:, :, :], AX_X, ALU.add))
                if n == SHARED:
                    c(v.tensor_scalar(col["s"][:, :], col["s"][:, :], 1e-6, None, ALU.add))
                c(v.reciprocal(col["km"][:, :], col["s"][:, :]))
                c(v.tensor_scalar(col["km"][:, :], col["km"][:, :], tg[:, 4 + n:5 + n], None, ALU.mult))
                v.tensor_tensor(s3["cb"][:, :, :], s3["ex"][:, :, :], wide(col["km"]), ALU.mult).then_inc(sem("combined"), 1)
            v.wait_ge(sem("combined"), n + 1)

            def unit(i, q):
                use = out_use(n, i, q)
                bank = read(v, use)
                v.wait_ge(taken[use[0]], use[1])
                for t in range(4):
                    tile = 4 * (q % 2) + t
                    last = v.scalar_tensor_tensor(x[:, tile, :], bank[:, t * D:(t + 1) * D],
                                                  s3["cb"][:, tile, bass.ds(2 * i + q // 2, 1)], x[:, tile, :], ALU.mult, ALU.add)
                last.then_inc(taken[use[0]], 1)

            ffn_loop(v, unit)
            if n != SHARED:
                for c_ in range(2):
                    use = uses["b2", n, c_]
                    bank = read(v, use)
                    v.wait_ge(taken[use[0]], use[1])
                    xs = x[:, 4 * c_:4 * c_ + 4, :]
                    v.tensor_tensor(xs, xs, bank[:, :].rearrange("p (t d) -> p t d", t=4), ALU.add).then_inc(taken[4 + c_], 1)
                    after(v, use)
            else:
                for q in (2, 3):
                    after(v, out_use(n, E // 2 - 1, q))

        @block.gpsimd
        def _(g):
            done = sem("constants")
            g.memset(ident[:, :], 0.0).then_inc(done, 1)
            g.memset(ones[:, :], 1.0).then_inc(done, 1)
            g.memset(upper[:, :], 1.0).then_inc(done, 1)
            g.memset(headmask[:, :], 1.0).then_inc(done, 1)
            g.memset(causal[:, :], 0.0).then_inc(done, 1)
            g.memset(half[:, :], -0.5).then_inc(done, 1)
            for j in range(2):
                g.memset(kM[j][:, :, :], 0.0).then_inc(done, 1)
                g.memset(va8[j][:, :, 8:9], 1.0).then_inc(done, 1)
            for e in range(E):
                g.memset(small["pri"][:, :, e:e + 1], float(E - e)).then_inc(done, 1)
            g.wait_ge(done, 10 + E)
            g.affine_select(out=ident[:, :], in_=ident[:, :], compare_op=ALU.not_equal, fill=1.0, base=0,
                            pattern=[[-1, 128]], channel_multiplier=1).then_inc(done, 1)
            g.affine_select(out=upper[:, :], in_=upper[:, :], compare_op=ALU.is_ge, fill=0.0, base=0,
                            pattern=[[1, 128]], channel_multiplier=-1).then_inc(done, 1)
            g.affine_select(out=causal[:, :], in_=causal[:, :], compare_op=ALU.is_ge, fill=NEG, base=0,
                            pattern=[[-1, K]], channel_multiplier=1).then_inc(done, 1)
            g.affine_select(out=headmask[:, :], in_=headmask[:, :], compare_op=ALU.is_ge, fill=0.0, base=0,
                            pattern=[[-8, H]], channel_multiplier=1).then_inc(done, 1)
            g.wait_ge(done, 14 + E)
            g.affine_select(out=headmask[:, :], in_=headmask[:, :], compare_op=ALU.is_ge, fill=0.0, base=7,
                            pattern=[[8, H]], channel_multiplier=-1).then_inc(done, 1)
            g.wait_ge(done, 15 + E)
            for n in range(4):
                if n < LAYERS:
                    root(g, f"a{n}")
                    if n != 2:
                        mha_pool(g, n)
                    if n == 1:
                        root(g, "y1")
                    root(g, f"f{n}")
                    if n == 3:
                        root(g, "i3")

        CONSTANTS = 15 + E

        @block.tensor
        def _(pe):
            pe.wait_ge(sem("constants"), CONSTANTS)
            loaded(pe, "cx")
            for b in range(B):
                bank = fill(pe, uses["cx", b])
                nc.tensor.transpose(bank[:, 0:K], cx[:, b, :], ident[0:K, 0:K]).then_inc(filled[b], 1)
            for n in range(LAYERS):
                turn_tensor(pe, f"a{n}", xn)
                if n == 2:
                    coat_tensor(pe)
                else:
                    mha_tensor(pe, n)
                turn_tensor(pe, f"f{n}", xn)
                ffn_tensor(pe, n)

        @block.scalar
        def _(a):
            loaded(a, "gates")
            nc.scalar.activation(tg[:, :], gates[:, :], ACT.Tanh).then_inc(sem("tg"), 1)
            for b in range(B):
                bank = read(a, uses["cx", b])
                nc.scalar.activation(cxT[:, b, :], bank[:, 0:K], ACT.Copy).then_inc(taken[b], 1)
            a.wait_ge(sem("constants"), CONSTANTS)
            for n in range(LAYERS):
                turn_scalar(a, f"a{n}", xnT)
                if n == 2:
                    coat_scalar(a)
                else:
                    mha_scalar(a, n)
                turn_scalar(a, f"f{n}", xnT)
                ffn_scalar(a, n)

        @block.vector
        def _(v):
            c = Chain(v, sem("vector"))
            loaded(v, "x")
            normalise(v, c, "a0", x, xn)
            v.wait_ge(sem("constants"), CONSTANTS)
            v.wait_ge(sem("tg"), 1)
            loaded(v, "mask")
            loaded(v, "cos")
            c(v.tensor_scalar(bias0[:, :, :], maskI[:, :, :], 0, NEG, ALU.is_equal, ALU.mult))
            for b in range(B):
                after(v, uses["cx", b])
            for n in range(LAYERS):
                if n:
                    normalise(v, c, f"a{n}", x, xn)
                if n == 3:
                    loaded(v, "w3")
                    c(v.tensor_scalar(bias3[:, :, :], validI[:, :, :], 0, NEG, ALU.is_equal, ALU.mult))
                    c(v.tensor_tensor(bias3[:, :, :], bias3[:, :, :], causal[:, :].unsqueeze(1).to_broadcast([S, B, K]), ALU.min))
                if n == 2:
                    coat_vector(v, c)
                else:
                    mha_vector(v, n)
                if n == 1:
                    loaded(v, "w1")
                    normalise(v, c, "y1", yb, yb)
                    v.wait_ge(sem("ln_out"), B * (LN["y1"] + 1))
                    c(v.tensor_scalar(gamma[:, :], gamma[:, :], tg[:, 1:2], None, ALU.mult))
                    c(v.tensor_tensor(yb[:, :, :], yb[:, :, :], gamma[:, :].unsqueeze(1).to_broadcast([S, B, D]), ALU.mult))
                    c(v.tensor_tensor(x[:, :, :], x[:, :, :], yb[:, :, :], ALU.add))
                normalise(v, c, f"f{n}", x, xn)
                ffn_vector(v, c, n)


def kernel(**inputs):
    import numpy as _np
    import concourse.bacc as _bacc
    from concourse.bass_utils import run_bass_kernel_spmd as _run

    given = {n: _np.asarray(a) for n, a in inputs.items()}
    plain = ["x", "ctx_1024", "mask_BxSxS2_ik0", "mask_BxS2_if1", "g_xattn", "g_ffn", "L0_xattn_Wq", "L0_xattn_Wk",
             "L0_xattn_Wv", "L0_xattn_Wo", "L1_xattn_w_kv", "L1_xattn_w_q", "L1_xattn_w_out1", "L1_xattn_w_out2",
             "L1_xattn_gamma", "L1_ffn_Wg", "L1_ffn_bg", "L1_ffn_b2", "L2_xattn_b_sim", "L2_xattn_W_qv", "L2_xattn_b_qv",
             "L2_ffn_gate_b", "L2_ffn_b2", "L3_ffn_Wr", "L3_ffn_br", "L3_ffn_b2"]
    arrays = {n: given[n] for n in plain}
    for n in ("L0_ffn_w_router", "L0_ffn_w_gate", "L2_ffn_gate_w", "L3_xattn_Wq", "L3_xattn_Wk", "L3_xattn_Wv", "L3_xattn_Wo"):
        arrays[n] = given[n].T
    for n in ("L0_xattn_Wq", "L0_xattn_Wk"):
        arrays[n + "_swapped"] = given[n].reshape(D, -1, 2)[:, :, ::-1].reshape(D, -1)
    arrays["L2_xattn_w_sim"] = given["L2_xattn_w_sim"].reshape(3, D).T
    arrays["L3_ffn_ln"] = _np.stack([given["L3_ffn_ln_g"], given["L3_ffn_ln_b"]], axis=1)

    def rows(a):
        e, r, m = a.shape
        return a.reshape(e, r // 128, 128, m).transpose(0, 2, 1, 3).reshape(e, 128, -1)

    arrays["L0_experts"] = rows(given["L0_ffn_w_down"].transpose(0, 2, 1))
    for n, (w1, b1, w2) in {1: ("W1", "b1", "W2"), 2: ("w1", "b1", "w2"), 3: ("W1", "b1", "W2")}.items():
        w1, b1, w2 = (given[f"L{n}_ffn_{k}"] for k in (w1, b1, w2))
        arrays[f"L{n}_experts"] = _np.concatenate([w1, rows(w2), rows(b1[:, :, None])], axis=2)

    inv = (1.0 / _np.float32(10000.0) ** (_np.arange(0, 64, 2, dtype=_np.float32) / _np.float32(64))).astype(_np.float32)
    angle = (_np.arange(S, dtype=_np.float32)[:, None] * inv).astype(_np.float32).T
    sign = _np.array([-1.0, 1.0], _np.float32)[None, :, None]
    one_head = [_np.repeat(_np.cos(angle)[:, None], 2, axis=1).reshape(64, S),
                (_np.sin(angle)[:, None] * sign).reshape(64, S)]
    arrays["rope_cos"], arrays["rope_sin"] = (_np.tile(a, (2, 1)).astype(_np.float32) for a in one_head)

    nc = _bacc.Bacc("TRN2", target_bir_lowering=False, num_devices=1)
    aps, feed = {}, {}
    for n, a in arrays.items():
        a = _np.ascontiguousarray(a)
        feed[f"in_{n}"] = a
        aps[n] = nc.dram_tensor(f"in_{n}", a.shape, mybir.dt.from_np(a.dtype), kind="ExternalInput").ap()
    out = nc.dram_tensor("out_0", (B, S, D), F32, kind="ExternalOutput").ap()
    build(nc, aps, out)
    r = _run(nc, [feed], core_ids=[0])
    return r.results[0]["out_0"]
```

```python
from contextlib import ExitStack

import concourse.bass as bass
from concourse import mybir

F32 = mybir.dt.float32
F32R = mybir.dt.float32r
I32 = mybir.dt.int32
ALU = mybir.AluOpType
ACT = mybir.ActivationFunctionType
AX_X = mybir.AxisListType.X

B = 8
S = 128
D = 128
K = 77
H = 16
G = 4
NG = H // G
E = 8
HALF = 4 * S
UNITS = 2 * E
CAPACITY = 160
NEG = -1.0e30
EPS = 1e-5


class Chain:

    def __init__(self, eng, sem):
        self.eng, self.sem, self.n = eng, sem, 0

    def __call__(self, instruction):
        instruction.then_inc(self.sem, 1)
        self.n += 1
        self.eng.wait_ge(self.sem, self.n)


def positive(value):
    return not isinstance(value, int) or value > 0


class Attention:

    BANK = {"S": (0,), "T": (1,), "A": (2,), "R": (3,), "Z": (3,), "Y": (3,), "F": (4, 5, 6, 7)}
    PROJECTED = BANK["F"]

    def __init__(self, fills, dh, scale, masked, hidden, spread, start):
        self.fills, self.dh, self.scale, self.masked = fills, dh, scale, masked
        self.wide = dh == 64
        self.slots = []
        left = list(range(len(fills)))
        late = {}

        def due(kind, n, group, ticks, place):
            tick = group + ticks
            late.setdefault((tick % NG, place), []).append((kind, n, tick // NG))

        for g in range(NG):
            due("X", g, g, 0, 3)
            if self.wide:
                due("N", g, g, 1, 1)
            due("T", g, g, 2, 2)
            due("A", g, g, 3, 4)
        if hidden:
            due("Z", 0, 3, 4, 1)
        if not self.wide:
            due("R", 0, 3, 4, 1)
        due("Y", 0, 3, 4, 5)
        for tick in range(NG):
            self.slots.append(("S", tick, 0))
            for place in range(1, 6):
                self.slots += late.get((tick, place), [])
                if place in (1, 3, 5):
                    n = (spread[tick] + (5 - place) // 2) // 3
                    self.slots += [("F", left.pop(0), -1) for _ in range(n)]
        assert not left and max(s[2] for s in self.slots) == 1
        self.start = list(start)
        self.first = [sum(self.bank(("F", f)) == k for f in range(len(fills))) for k in range(8)]
        self.each = [sum(self.bank(s) == k for s in self.slots) for k in range(8)]

    def bank(self, slot):
        return None if slot[0] in "XN" else self.BANK[slot[0]][slot[1] % len(self.BANK[slot[0]])]

    def there(self, slot, step):
        return not isinstance(step, int) or 0 <= step - slot[2] < B

    def before(self, bank, step):
        base = self.start[bank] + self.first[bank]
        if isinstance(step, int):
            return base + sum(self.bank(s) == bank and self.there(s, e) for e in range(step) for s in self.slots)
        one = self.before(bank, 1)
        return (step - 1) * self.each[bank] + one

    def use(self, kind, n, b):
        slot = next(s for s in self.slots if s[:2] == (kind, n))
        step, bank = b + slot[2], self.bank(slot)
        if isinstance(step, int) and step < 0:
            return bank, self.start[bank] + sum(self.bank(("F", f)) == bank for f in range(n))
        earlier = [s for s in self.slots[:self.slots.index(slot)] if self.bank(s) == bank and self.there(s, step)]
        return bank, self.before(bank, step) + len(earlier)

    def end(self):
        return [self.before(k, B + 1) for k in range(8)]


PROJECTIONS = {
    0: [("q", 0), ("qs", 0), ("k", 0), ("ks", 0), ("q", 1), ("qs", 1), ("k", 1), ("ks", 1), ("v", 0), ("v", 1)],
    1: [("q", 0), ("k", 0), ("q", 1), ("k", 1), ("v", 0), ("v", 1)],
    3: [("qk", 0), ("v", 0)],
}
SPREAD = {0: (3, 3, 2, 2), 1: (2, 1, 1, 2), 3: (1, 0, 0, 1)}
HIDDEN_BLOCKS = {0: 2, 1: 2, 2: 4, 3: 4}
SHARED = 0


def build(nc, A, out):
    ctx = ExitStack()
    with ctx:
        def sb(name, shape, dt=F32):
            return ctx.enter_context(nc.sbuf_tensor(name, shape, dt))

        sems = {}

        def sem(name):
            if name not in sems:
                sems[name] = ctx.enter_context(nc.semaphore(name))
            return sems[name]

        P = [ctx.enter_context(nc.psum_tensor(f"bank{i}", [128, 512], F32)) for i in range(8)]

        x = sb("x", [S, B, D])
        xn = sb("xn", [S, B, D])
        xnT = sb("xnT", [D, B, S])
        cx = sb("cx", [K, B, D])
        cxT = sb("cxT", [D, B, K])
        ident = sb("ident", [128, 128])
        ones = sb("ones", [128, 128])
        upper = sb("upper", [128, 128])
        gates = sb("gates", [128, 8])
        tg = sb("tg", [128, 8])
        exponent = sb("exponent", [128, 8])
        stats = [sb(f"stats{i}", [128, B, 6]) for i in range(2)]
        mv = [sb(f"mv{i}", [128, B, 2]) for i in range(2)]
        ve = [sb(f"ve{i}", [128, B]) for i in range(2)]
        rstd = [sb(f"rstd{i}", [128, B]) for i in range(2)]

        w = {}
        for n in ("L0q", "L0qs", "L0k", "L0ks", "L0v", "L0o"):
            w[n] = sb(n, [D, H * 64])
        for n in "qkvo":
            w["L1" + n] = w["L0" + n]
        for n in ("L1o2", "L3q", "L3k", "L3v", "L3o"):
            w[n] = sb(n, [D, D])
        gamma = sb("gamma", [128, D])
        cos = sb("cos", [128, S])
        sin = sb("sin", [128, S])
        headmask = sb("headmask", [128, H])
        maskI = sb("maskI", [S, B, K], I32)
        bias0 = sb("bias0", [S, B, K])
        validI = sb("validI", [128, B, K], I32)
        bias3 = sb("bias3", [S, B, K])
        causal = sb("causal", [S, K])
        wsim = sb("wsim", [D, 3])
        bsim = sb("bsim", [128, 1])
        wqv = sb("wqv", [D, 4, D])
        bqv = sb("bqv", [1, D])

        qT = [sb(f"qT{j}", [128, 8, S]) for j in range(2)]
        kM = [sb(f"kM{j}", [128, H, K]) for j in range(2)]
        va = [sb(f"va{j}", [K, H * 64]) for j in range(2)]
        va8 = [sb(f"va8{j}", [K, H, 9]) for j in range(2)]
        cb = [sb(f"cb{j}", [D, K]) for j in range(2)]
        k3 = sb("k3", [128, K])
        rope = [sb(f"rope{j}", [128, 2, 4, S]) for j in range(2)]
        sc = sb("sc", [S, NG, G, K])
        pr = sb("pr", [S, NG, G, K])
        pT = [sb(f"pT{g}", [K, G, S]) for g in range(NG)]
        mx = sb("mx", [S, NG, G])
        total = sb("total", [S, NG, G])
        rc = sb("rc", [S, NG, G])
        on = sb("on", [S, D])
        oT = [sb(f"oT{j}", [128, 8, S]) for j in range(2)]
        zT = sb("zT", [D, S])
        yb = sb("yb", [S, B, D])

        wr = {n: sb(f"wr{n}", [D, E]) for n in range(4)}
        br = {n: sb(f"br{n}", [128, E]) for n in (1, 2, 3)}
        b2 = {n: sb(f"b2{n}", [E, D]) for n in (1, 2, 3)}
        wg = sb("wg", [D, 2 * 128])
        row = {n: 2 * 128 * HIDDEN_BLOCKS[n] + HIDDEN_BLOCKS[n] if n else 2 * D for n in range(4)}
        we = {n: [sb(f"we{n}{j}", [128, row[n]]) for j in range(2)] for n in range(4)}
        EXPERT_PARTS = {0: {"w2": slice(0, row[0])}}
        for n in (1, 2, 3):
            m = 128 * HIDDEN_BLOCKS[n]
            EXPERT_PARTS[n] = {"w1": slice(0, m), "b1": slice(2 * m, 2 * m + HIDDEN_BLOCKS[n]), "w2": slice(m, 2 * m)}
        hT = [sb(f"hT{j}", [128, 4, HALF]) for j in range(2)]
        tokens_high = sb("tokens_high", [D, B, S], F32R)
        tokens_low = sb("tokens_low", [D, B, S], F32R)
        w1_high = [sb(f"w1_high{j}", [D, 512], F32R) for j in range(2)]
        w1_low = [sb(f"w1_low{j}", [D, 512], F32R) for j in range(2)]
        lng = sb("lng", [D, 2])
        small = {n: sb(f"r_{n}", [128, B, E]) for n in
                 ("L", "L2", "ex", "eq", "one1", "one2", "pri", "cb", "m")}
        col = {n: sb(f"c_{n}", [128, B]) for n in ("m1", "m2", "z", "rz", "km", "s")}
        combT = sb("combT", [E, B, S])
        c3 = sc[:, 0:2, :, :].rearrange("p a b k -> p (a b) k")
        c2 = sc[:, 2:4, :, :].rearrange("p a b k -> p (a b) k")
        aT = pT
        attended_context = qT[1]
        times_token = yb
        times_bar = qT[0]
        sim = pr[:, 0:2, :, :].rearrange("p a b k -> p (a b) k")
        m8 = sb("m8", [S, B])
        z8 = sb("z8", [S, B])
        rz8 = sb("rz8", [S, B])
        mT = sb("mT", [B, S])
        row1 = sb("row1", [B, 4])
        bT = sb("bT", [S, B])
        hc = sb("hc", [D, B])

        filled = [sem(f"filled{i}") for i in range(8)]
        taken = [sem(f"taken{i}") for i in range(8)]
        uses, count, attn, ffn = {}, [0] * 8, {}, {}

        def plan_use(key, bank):
            uses[key] = (bank, count[bank])
            count[bank] += 1

        for b in range(B):
            plan_use(("cx", b), b)
        for n in range(4):
            plan_use(("turn", f"a{n}", 0), 6)
            plan_use(("turn", f"a{n}", 1), 7 if n == 2 else 3)
            if n == 2:
                for c_ in range(2):
                    plan_use(("sim", c_), c_)
                    plan_use(("aT", c_), c_)
                    plan_use(("hq", c_), 4 + c_)
                plan_use("mT", 6)
                plan_use("bT", 7)
                plan_use("hc", 6)
                for c_ in range(2):
                    plan_use(("own", c_), 2 + c_)
                for b in range(B):
                    plan_use(("feat", b), 6 + b % 2)
            else:
                attn[n] = Attention(PROJECTIONS[n], 8 if n == 3 else 64, 8.0 ** -0.5 if n == 3 else 64.0 ** -0.5,
                                    n != 1, n == 1, SPREAD[n], count)
                count[:] = attn[n].end()
            for c_ in range(2):
                plan_use(("turn", f"f{n}", c_), 6 + c_)
            plan_use(("logits", n), 6)
            if n == 3:
                for c_ in range(2):
                    plan_use(("turn", "i3", c_), 4 + c_)
            if n == SHARED:
                plan_use("rank", 7)
            else:
                plan_use(("combT", n, 0), 6)
                plan_use(("combT", n, 1), 7)
            ffn[n] = list(count)
            if n == SHARED:
                for k in range(4):
                    count[k] += 1
            else:
                for k in range(4):
                    count[k] += UNITS if HIDDEN_BLOCKS[n] == 4 else UNITS // 2
            for c_ in range(2):
                if n != SHARED:
                    uses["b2", n, c_] = (4 + c_, count[4 + c_] + UNITS // 2 - 2)
                count[4 + c_] += UNITS // 2 + (n != SHARED)

        def hidden_use(n, i, q, nb):
            if HIDDEN_BLOCKS[n] == 4:
                return nb, 4 * i + (ffn[n][nb] + q)
            bank = 2 * (q % 2) + nb
            return bank, 2 * i + (ffn[n][bank] + q // 2)

        def out_use(n, i, q):
            after_b2 = isinstance(i, int) and n != SHARED
            return 4 + q % 2, 2 * i + (ffn[n][4 + q % 2] + q // 2 + after_b2)

        def fill(pe, use):
            if positive(use[1]):
                pe.wait_ge(taken[use[0]], use[1])
            return P[use[0]]

        def read(eng, use):
            eng.wait_ge(filled[use[0]], use[1] + 1)
            return P[use[0]]

        def after(eng, use):
            eng.wait_ge(taken[use[0]], use[1] + 1)

        block = ctx.enter_context(nc.Block())

        loads = {}

        def loaded(eng, group):
            eng.wait_ge(sem("ld_" + group), loads[group])

        def row_of(ap):
            return ap.rearrange("(a n) -> a n", a=1)

        def all_rows(ap, n):
            return row_of(ap).to_broadcast([128, n])

        plan = []

        def want(group, dst, src):
            plan.append((group, dst, src))
            loads[group] = loads.get(group, 0) + 16

        for c_ in range(2):
            want(f"x{c_}", x[:, 4 * c_:4 * c_ + 4, :], A["x"][4 * c_:4 * c_ + 4].rearrange("b t d -> t b d"))
        want("cx", cx[:, :, :], A["ctx_1024"].rearrange("b t d -> t b d"))
        want("gates", gates[:, 0:4], all_rows(A["g_xattn"], 4))
        want("gates", gates[:, 4:8], all_rows(A["g_ffn"], 4))
        want("w0q", w["L0q"][:, :], A["L0_xattn_Wq"])
        want("w0qs", w["L0qs"][:, :], A["L0_xattn_Wq_swapped"])
        want("cos", cos[:, :], A["rope_cos"])
        want("cos", sin[:, :], A["rope_sin"])
        want("w0k", w["L0k"][:, :], A["L0_xattn_Wk"])
        want("w0ks", w["L0ks"][:, :], A["L0_xattn_Wk_swapped"])
        want("w0v", w["L0v"][:, :], A["L0_xattn_Wv"])
        want("mask", maskI[:, :, :], A["mask_BxSxS2_ik0"].rearrange("b q k -> q b k"))
        want("wo0", w["L0o"][:, :].rearrange("p (n d) -> p n d", d=D), A["L0_xattn_Wo"].rearrange("(n p) d -> p n d", p=128))
        want("f0", wr[0][:, :], A["L0_ffn_w_router"])
        want("f0", wg[:, :], A["L0_ffn_w_gate"])
        for j in range(2):
            want(f"w2_0{j}", we[0][j][:, :], A["L0_experts"][j])
        want("w1", w["L1o2"][:, :], A["L1_xattn_w_out2"])
        want("w1", gamma[:, :], all_rows(A["L1_xattn_gamma"], D))
        want("f1", wr[1][:, :], A["L1_ffn_Wg"])
        want("f1", br[1][:, :], all_rows(A["L1_ffn_bg"], E))
        want("f1", b2[1][:, :], A["L1_ffn_b2"])
        want("w2", wsim[:, :], A["L2_xattn_w_sim"])
        want("w2", bsim[:, :], all_rows(A["L2_xattn_b_sim"], 1))
        want("w2", wqv[:, :, :], A["L2_xattn_W_qv"].rearrange("(n p) d -> p n d", p=128))
        want("w2", bqv[:, :], row_of(A["L2_xattn_b_qv"]))
        want("f2", wr[2][:, :], A["L2_ffn_gate_w"])
        want("f2", br[2][:, :], all_rows(A["L2_ffn_gate_b"], E))
        want("f2", b2[2][:, :], A["L2_ffn_b2"])
        want("w3", w["L3q"][:, :], A["L3_xattn_Wq"])
        want("w3", w["L3k"][:, :], A["L3_xattn_Wk"])
        want("w3", w["L3v"][:, :], A["L3_xattn_Wv"])
        want("w3", w["L3o"][:, :], A["L3_xattn_Wo"])
        want("w3", validI[:, :, :], A["mask_BxS2_if1"].rearrange("(a b) k -> a b k", a=1).to_broadcast([128, B, K]))
        want("f3", wr[3][:, :], A["L3_ffn_Wr"])
        want("f3", br[3][:, :], all_rows(A["L3_ffn_br"], E))
        want("f3", b2[3][:, :], A["L3_ffn_b2"])
        want("f3", lng[:, :], A["L3_ffn_ln"])
        for n in (1, 2, 3):
            for j in range(2):
                for name, columns in EXPERT_PARTS[n].items():
                    want(f"{name}_{n}{j}", we[n][j][:, columns], A[f"L{n}_experts"][j][:, columns])

        late_plan = [(w["L1q"][:, :], A["L1_xattn_w_q"]),
                     (w["L1k"][:, :], A["L1_xattn_w_kv"][:, 0:H * 64]),
                     (w["L1v"][:, :], A["L1_xattn_w_kv"][:, H * 64:]),
                     (w["L1o"][:, :].rearrange("p (n d) -> p n d", d=D),
                      A["L1_xattn_w_out1"].rearrange("(n p) d -> p n d", p=128))]
        loads["late"] = 16 * len(late_plan)

        @block.sync
        def _(sp):
            for group, dst, src in plan:
                sp.dma_start(dst, src).then_inc(sem("ld_" + group), 16)
            for n in range(4):
                with sp.Fori(1, E // 2) as i:
                    for j in range(2):
                        for name, columns in EXPERT_PARTS[n].items():
                            if name == "w1":
                                sp.wait_ge(sem(f"w1_split{n}"), 2 * i + (j - 1))
                            elif name == "b1":
                                after(sp, hidden_use(n, i - 1, 2 * j + 1, HIDDEN_BLOCKS[n] - 1))
                            else:
                                sp.wait_ge(filled[5], 2 * i + (ffn[n][5] + j - 1))
                            sp.dma_start(we[n][j][:, columns],
                                         A[f"L{n}_experts"][bass.ds(2 * i + j, 1), :, columns].rearrange("a p f -> (a p) f"))\
                              .then_inc(sem(f"ld_{name}_{n}{j}"), 16)
            for c_ in range(2):
                after(sp, out_use(3, E // 2 - 1, 2 * c_ + 1))
                sp.dma_start(out[4 * c_:4 * c_ + 4].rearrange("b t d -> t b d"), x[:, 4 * c_:4 * c_ + 4, :])\
                  .then_inc(sem("stored"), 16)
            sp.wait_ge(sem("stored"), 32)

        def one(tile, b):
            return tile[:, bass.ds(b, 1), :].rearrange("p a n -> p (a n)")

        def own(st):
            return int(st in ("y1", "i3"))

        def norm_begin(v, c, st, lo, hi, src):
            o = own(st)
            for t in range(lo, hi):
                last = v.bn_stats(stats[o][:, t, :], src[:, t, :])
            c(last)
            for t in range(lo, hi):
                last = v.bn_aggr(mv[o][:, t, :], stats[o][:, t, :])
            c(last)
            v.tensor_scalar(ve[o][:, lo:hi], mv[o][:, lo:hi, 1], EPS, None, ALU.add).then_inc(sem(f"var_{st}"), hi - lo)

        rooted = []

        def norm_root(g, st, lo, hi):
            o = own(st)
            if rooted:
                g.wait_ge(*rooted[-1])
            rooted.append((sem(f"rstd_{st}"), hi))
            g.wait_ge(sem(f"var_{st}"), hi)
            g.tensor_tensor(rstd[o][:, lo:hi], ve[o][:, lo:hi], exponent[:, lo:hi], ALU.pow).then_inc(sem(f"rstd_{st}"), hi - lo)

        def norm_end(v, st, lo, hi, src, dst):
            o = own(st)
            v.wait_ge(sem(f"rstd_{st}"), hi)
            for t in range(lo, hi):
                v.tensor_scalar(dst[:, t, :], src[:, t, :], mv[o][:, t, 0:1], rstd[o][:, t:t + 1], ALU.subtract, ALU.mult)\
                 .then_inc(sem(f"out_{st}"), 1)

        def norm_half(v, c, st, c_, src, dst):
            norm_begin(v, c, st, 4 * c_, 4 * c_ + 4, src)
            norm_end(v, st, 4 * c_, 4 * c_ + 4, src, dst)

        def between_stages(n):
            return {1: ("y1", "f1"), 3: ("f3", "i3")}.get(n, (f"f{n}",))

        def between_order(n):
            last = len(between_stages(n))
            if n == 2:
                places = [(b, 0) for b in range(B)]
            elif n == 1:
                places = [(6, 0), (6, 1), (6, 2), (6, 3), (7, 0), (7, 2), (8, 1), (8, 3)]
            else:
                places = [(6, 3), (7, 0), (7, 1), (7, 2), (7, 3), (8, 0), (8, 1), (8, 3)]
            order = [(places[k], stage, k - stage) for k in range(B - 1) for stage in range(last + 1) if k >= stage]
            flush = places[B - 1] if n == 2 else (8, 2)
            order += [(flush, stage, k - stage) for k in range(B - 1, B - 1 + last) for stage in range(last + 1)
                      if k - stage < B - 1]
            return order + [(places[B - 1], stage, B - 1) for stage in range(last + 1)]

        def between_vector(v, c, n, place):
            norms = between_stages(n)
            for where, stage, t in between_order(n):
                if where != place:
                    continue
                if stage:
                    st = norms[stage - 1]
                    if st == "y1":
                        c(v.scalar_tensor_tensor(yb[:, t, :], yb[:, t, :], mv[1][:, t, 0:1], gamma[:, :], ALU.subtract, ALU.mult))
                        v.wait_ge(sem("rstd_y1"), t + 1)
                        c(v.scalar_tensor_tensor(x[:, t, :], yb[:, t, :], rstd[1][:, t:t + 1], x[:, t, :], ALU.mult, ALU.add))
                    else:
                        src, dst = (xn, yb) if st == "i3" else (x, xn)
                        norm_end(v, st, t, t + 1, src, dst)
                if stage < len(norms):
                    st = norms[stage]
                    if st == "i3":
                        v.wait_ge(sem("out_f3"), t + 1)
                    norm_begin(v, c, st, t, t + 1, {"y1": yb, "i3": xn}.get(st, x))

        def between_pool(g, n):
            norms = between_stages(n)
            for _, stage, t in between_order(n):
                if n != SHARED and (stage, t) == (0, B - 1):
                    split_tokens(g, n, 0)
                if stage < len(norms):
                    norm_root(g, norms[stage], t, t + 1)
            if n != SHARED:
                split_tokens(g, n, 1)

        def split_tokens(g, n, c_):
            src = attended_context if n == 3 else xnT
            g.wait_ge(*rooted[-1])
            after(g, uses["turn", "i3" if n == 3 else f"f{n}", c_])
            half = slice(4 * c_, 4 * c_ + 4)
            g.tensor_tensor(tokens_low[:, half, :], src[:, half, :], tokens_high[:, half, :], ALU.subtract)\
             .then_inc(sem(f"tokens_split{n}"), 1)

        def split_expert(g, n, i, j):
            width = 128 * HIDDEN_BLOCKS[n]
            g.wait_ge(sem(f"ld_w1_{n}{j}"), 16 * i + 16)
            if not isinstance(i, int):
                read(g, hidden_use(n, i - 1, 2 * j + 1, HIDDEN_BLOCKS[n] - 1))
            g.tensor_tensor(w1_high[j][:, 0:width], we[n][j][:, 0:width], ones[:, 0:1].to_broadcast([128, width]), ALU.mult)\
             .then_inc(sem(f"w1_high{n}"), 1)
            g.wait_ge(sem(f"w1_high{n}"), 2 * i + (j + 1))
            g.tensor_tensor(w1_low[j][:, 0:width], we[n][j][:, 0:width], w1_high[j][:, 0:width], ALU.subtract)\
             .then_inc(sem(f"w1_split{n}"), 1)

        def turn_tensor(pe, st, c_, src):
            use = uses["turn", st, c_]
            bank = fill(pe, use)
            for t in range(4):
                pe.wait_ge(sem(f"out_{st}"), 4 * c_ + t + 1)
                last = nc.tensor.transpose(bank[:, t * S:(t + 1) * S], src[:, 4 * c_ + t, :], ident[:, :])
            last.then_inc(filled[use[0]], 1)

        def turn_scalar(a, st, c_, dst):
            use = uses["turn", st, c_]
            bank = read(a, use)
            tiles = bank[:, :].rearrange("p (t s) -> p t s", t=4)
            for to in (dst,) + ((tokens_high,) if st in ("f1", "f2", "i3") else ()):
                to = to[:, 4 * c_:4 * c_ + 4, :]
                if st == "i3":
                    last = nc.scalar.activation(to, tiles, ACT.Identity, bias=lng[:, 1:2], scale=lng[:, 0:1])
                else:
                    last = nc.scalar.activation(to, tiles, ACT.Copy)
            last.then_inc(taken[use[0]], 1)

        def turn_first_half(pe, n):
            turn_tensor(pe, f"f{n}", 0, xn)
            if n == 3:
                turn_tensor(pe, "i3", 0, yb)

        def take_first_half(a, n):
            turn_scalar(a, f"f{n}", 0, xnT)
            if n == 3:
                loaded(a, "f3")
                turn_scalar(a, "i3", 0, attended_context)

        def route_half(pe, n, c_):
            if c_ == 0:
                loaded(pe, f"f{n}")
                fill(pe, uses["logits", n])
            after(pe, uses["turn", f"f{n}", c_])
            for t in range(4 * c_, 4 * c_ + 4):
                last = nc.tensor.matmul(P[uses["logits", n][0]][:, t * E:(t + 1) * E], xnT[:, t, :], wr[n][:, :],
                                        start=True, stop=True)
            return last

        def rounds(eng, m, project, work, begun=lambda: None, extra=lambda step, tick: None):

            def step(s, parity):
                for k, slot in enumerate(m.slots):
                    if k and slot[0] == "S" and isinstance(s, int):
                        extra(s, slot[1] - 1)
                    if m.there(slot, s):
                        kind, n, late = slot
                        if kind == "F":
                            project(s + 1, 1 - parity, n)
                        else:
                            work(kind, n, s - late, (parity + late) % 2)
                if isinstance(s, int):
                    extra(s, NG - 1)

            for f in range(len(m.fills)):
                project(0, 0, f)
            begun()
            for s in (0, 1):
                step(s, s % 2)
            with eng.Fori(1, B // 2 - 1) as i:
                for j in range(2):
                    step(2 * i + j, j)
            for s in range(B - 2, B + 1):
                step(s, s % 2)

        def mha_tensor(pe, n):
            m = attn[n]

            def project(b, j, f):
                kind, part = m.fills[f]
                use = m.use("F", f, b)
                bank = fill(pe, use)
                if n == 0 and isinstance(b, int) and b == 0:
                    loaded(pe, f"w0{kind}")
                xb, cxb = one(xnT, b), one(cxT, b)
                if kind == "v":
                    if isinstance(b, int):
                        context = cxT[:, b, :]
                    else:
                        pe.wait_ge(sem(f"cb{n}"), b - 2)
                        context = cb[j][:, :]
                    width = 512 if m.wide else D
                    last = nc.tensor.matmul(bank[0:K, 0:width], context, w[f"L{n}v"][:, part * 512:part * 512 + width],
                                            start=True, stop=True)
                elif kind == "qk":
                    nc.tensor.matmul(bank[:, 0:S], w["L3q"][:, :], xb, start=True, stop=True)
                    last = nc.tensor.matmul(bank[:, S:S + K], w["L3k"][:, :], cxb, start=True, stop=True)
                else:
                    rhs, width = (xb, S) if kind[0] == "q" else (cxb, K)
                    for i in range(4):
                        o = part * 512 + i * 128
                        last = nc.tensor.matmul(bank[:, i * width:(i + 1) * width], w[f"L{n}{kind}"][:, o:o + 128], rhs,
                                                start=True, stop=True)
                last.then_inc(filled[use[0]], 1)

            def out_projection(bank, j, lo, hi):
                for i in range(lo, hi):
                    block = w[f"L{n}o"][:, i * D:(i + 1) * D]
                    a, b = (block, oT[j][:, i, :]) if n == 1 else (oT[j][:, i, :], block)
                    last = nc.tensor.matmul(bank[:, 0:128], a, b, start=i == 0, stop=i == (7 if m.wide else 0))
                return last

            def projected(pe, b, values):
                for k in m.PROJECTED:
                    last = [f for f, (kind, _) in enumerate(m.fills) if (kind == "v") == values and m.bank(("F", f)) == k]
                    if last:
                        after(pe, m.use("F", last[-1], b))

            def work(kind, g, b, j):
                if kind not in "XN":
                    first = 0
                    if m.wide and isinstance(b, int) and b == B - 1:
                        if kind == "A" and g == NG - 1:
                            after(pe, m.use("A", NG - 2, b))
                            out_projection(fill(pe, m.use("Z" if n == 1 else "Y", 0, b)), j, 0, 6)
                        if kind == ("Z" if n == 1 else "Y"):
                            first = 6
                    use = m.use(kind, g, b)
                    bank = fill(pe, use)
                    if kind == "A" and g == 0:
                        projected(pe, b, True)
                    if kind == "S":
                        if g == 0:
                            projected(pe, b, False)
                            if n == 0:
                                pe.wait_ge(sem("roped"), 6 * b + 6)
                            elif n == 1:
                                pe.wait_ge(sem("k_low"), 2 * b + 2)
                            else:
                                pe.wait_ge(sem("k_spread"), b + 1)
                        if m.wide:
                            for i in range(2):
                                h = G * g + 2 * i
                                last = nc.tensor.matmul(bank[:, 2 * i * K:2 * (i + 1) * K], qT[j][:, h // 2, :],
                                                        kM[j][:, h:h + 2, :], start=True, stop=True)
                        else:
                            last = nc.tensor.matmul(bank[:, 0:G * K], qT[j][:, 0, :], kM[j][:, G * g:G * g + G, :],
                                                    start=True, stop=True)
                    elif kind == "T":
                        pe.wait_ge(sem(f"weights{n}" if m.wide else f"probs{n}"), NG * b + (g + 1))
                        for i in range(G):
                            last = nc.tensor.transpose(bank[0:K, i * S:(i + 1) * S], pr[:, g, i, :], ident[:, :])
                    elif kind == "A" and m.wide:
                        after(pe, m.use("T", g, b))
                        for i in range(2):
                            h = G * g + 2 * i
                            last = nc.tensor.matmul(bank[:, 2 * i * S:2 * (i + 1) * S], va[j][:, h * 64:(h + 2) * 64],
                                                    pT[g][:, 2 * i:2 * i + 2, :], start=True, stop=True)
                    elif kind == "A":
                        after(pe, m.use("T", g, b))
                        for i in range(G):
                            last = nc.tensor.matmul(bank[:, i * 9:(i + 1) * 9], pT[g][:, i, :], va8[j][:, G * g + i, :],
                                                    start=True, stop=True)
                    elif kind == "R":
                        after(pe, m.use("A", NG - 1, b))
                        last = nc.tensor.transpose(bank[:, 0:S], on[:, :], ident[:, :])
                    elif kind == "Z":
                        after(pe, m.use("A", NG - 1, b))
                        last = out_projection(bank, j, first, 8)
                    elif n == 1:
                        last = nc.tensor.matmul(bank[:, 0:D], zT[:, :], w["L1o2"][:, :], start=True, stop=True)
                    else:
                        if n == 0:
                            loaded(pe, "wo0")
                        after(pe, m.use(*(("A", NG - 1) if m.wide else ("R", 0)), b))
                        last = out_projection(bank, j, first, 8 if m.wide else 1)
                    last.then_inc(filled[use[0]], 1)

            def extra(s, tick):
                if (s, tick) == (1, NG - 1):
                    after(pe, uses["turn", f"a{n}", 1])
                if (s, tick) == (B, 1):
                    turn_first_half(pe, n)
                if (s, tick) == (B, 2):
                    route_half(pe, n, 0)

            if n:
                loaded(pe, f"w{n}")
            if n == 1:
                loaded(pe, "late")
            after(pe, uses["turn", f"a{n}", 0])
            if n == 0:
                for b in range(B):
                    after(pe, uses["cx", b])
            def begun():
                turn_tensor(pe, f"a{n}", 1, xn)
                if n == 0:
                    pe.wait_ge(sem("constants"), CONSTANTS)

            rounds(pe, m, project, work, begun, extra)

        def mha_vector(v, c, n):
            m = attn[n]

            def project(b, j, f):
                kind, part = m.fills[f]
                use = m.use("F", f, b)
                if f == 0 and not isinstance(b, int):
                    for k in m.PROJECTED:
                        v.wait_ge(filled[k], m.before(k, b - 1))
                    v.tensor_scalar(cb[j][:, :], one(cxT, b), 1.0, None, ALU.mult).then_inc(sem(f"cb{n}"), 1)
                if n == 0 and kind != "v":
                    is_k, is_swapped = kind[0] == "k", kind.endswith("s")
                    pair, width = 2 * part + is_k, K if is_k else S
                    if not is_swapped:
                        done = 6 * b + {0: -2, 1: 0, 2: 1, 3: 3}[pair]
                        if positive(done):
                            v.wait_ge(sem("roped"), done)
                    bank = read(v, use)
                    table = (sin if is_swapped else cos)[:, 0:width].unsqueeze(1).to_broadcast([128, 4, width])
                    v.tensor_tensor(rope[pair % 2][:, int(is_swapped), :, 0:width],
                                    bank[:, 0:4 * width].rearrange("p (n t) -> p n t", n=4), table, ALU.mult)\
                     .then_inc(taken[use[0]], 1)
                if n == 1 and kind == "k":
                    bank = read(v, use)
                    for e, done in ((0, sem("k_low")), (1, taken[use[0]])):
                        p_ = slice(64 * e, 64 * e + 64)
                        v.tensor_copy(kM[j][p_, 8 * part + e:8 * part + 8:2, :],
                                      bank[p_, 0:4 * K].rearrange("p (n t) -> p n t", n=4)).then_inc(done, 1)

            def add_up(g, b):
                v.wait_ge(sem(f"probs{n}"), NG * b + (g + 1))
                v.tensor_reduce(total[:, g, :], pr[:, g, :, :], AX_X, ALU.add).then_inc(sem(f"sum{n}"), 1)

            def invert(g, b):
                v.wait_ge(sem(f"sum{n}"), NG * b + (g + 1))
                v.reciprocal(rc[:, g, :], total[:, g, :]).then_inc(sem(f"inverse{n}"), 1)

            def divide(g, b):
                v.wait_ge(sem(f"inverse{n}"), NG * b + (g + 1))
                v.tensor_tensor(pr[:, g, :, :], pr[:, g, :, :], rc[:, g, :].unsqueeze(2).to_broadcast([S, G, K]), ALU.mult)\
                 .then_inc(sem(f"weights{n}"), 1)

            def work(kind, g, b, j):
                if kind == "S":
                    use = m.use("S", g, b)
                    before = (g - 1, b) if g else (NG - 1, b - 1)
                    weights = m.wide and not (isinstance(b, int) and b == 0 and g == 0)
                    raw = read(v, use)[:, 0:G * K].rearrange("p (h k) -> p h k", h=G)
                    group = sc[:, g, :, :]
                    if m.masked:
                        bias = (bias0 if n == 0 else bias3)[:, bass.ds(b, 1), :].to_broadcast([S, G, K])
                        v.tensor_tensor(group, raw, bias, ALU.add).then_inc(taken[use[0]], 1)
                        raw = group
                    if weights:
                        add_up(*before)
                    if m.masked:
                        after(v, use)
                    v.tensor_reduce(mx[:, g, :], raw, AX_X, ALU.max).then_inc(sem(f"max{n}"), 1)
                    if weights:
                        invert(*before)
                    v.wait_ge(sem(f"max{n}"), NG * b + (g + 1))
                    v.tensor_tensor(group, raw, mx[:, g, :].unsqueeze(2).to_broadcast([S, G, K]), ALU.subtract)\
                     .then_inc(sem(f"shifted{n}") if m.masked else taken[use[0]], 1)
                    if weights:
                        divide(*before)
                elif kind == "N":
                    if isinstance(b, int) and (g, b) == (NG - 1, B - 1):
                        add_up(g, b)
                        invert(g, b)
                        divide(g, b)
                elif kind != "X":
                    use = m.use(kind, g, b)
                    if kind == "A" and not m.wide:
                        raw = read(v, use)[:, 0:G * 9].rearrange("p (h d) -> p h d", h=G)
                        v.reciprocal(rc[:, g, :], raw[:, :, 8]).then_inc(sem(f"inverse{n}"), 1)
                        v.wait_ge(sem(f"inverse{n}"), NG * b + (g + 1))
                        v.tensor_tensor(on[:, G * g * 8:G * (g + 1) * 8].rearrange("p (h d) -> p h d", h=G),
                                        raw[:, :, 0:8], rc[:, g, :].unsqueeze(2).to_broadcast([S, G, 8]), ALU.mult)\
                         .then_inc(taken[use[0]], 1)
                    if kind == "Y":
                        bank = read(v, use)
                        if n == 1:
                            v.tensor_copy(one(yb, b), bank[:, 0:D]).then_inc(taken[use[0]], 1)
                        else:
                            v.scalar_tensor_tensor(one(x, b), bank[:, 0:D], tg[:, n:n + 1], one(x, b), ALU.mult, ALU.add)\
                             .then_inc(taken[use[0]], 1)

            def extra(s, tick):
                for place, stage, t in between_order(n):
                    if place == (s, tick) and stage == 0:
                        after(v, m.use("Y", 0, t))
                between_vector(v, c, n, (s, tick))

            def begun():
                if n == 0:
                    loaded(v, "mask")
                    c(v.tensor_scalar(bias0[:, :, :], maskI[:, :, :], 0, NEG, ALU.is_equal, ALU.mult))
                    v.wait_ge(sem("tg"), 1)
                    v.wait_ge(sem("constants"), CONSTANTS)
                    for b in range(B):
                        after(v, uses["cx", b])

            rounds(v, m, project, work, begun, extra)

        def mha_scalar(a, n):
            m = attn[n]

            def project(b, j, f):
                kind, part = m.fills[f]
                use = m.use("F", f, b)
                if kind == "v":
                    bank = read(a, use)
                    if m.wide:
                        nc.scalar.activation(va[j][:, 512 * part:512 * part + 512], bank[0:K, 0:512], ACT.Copy)\
                          .then_inc(taken[use[0]], 1)
                    else:
                        nc.scalar.activation(va8[j][:, :, 0:8], bank[0:K, 0:D].rearrange("p (h d) -> p h d", h=H), ACT.Copy)\
                          .then_inc(taken[use[0]], 1)
                if n == 1 and kind == "q":
                    bank = read(a, use)
                    nc.scalar.activation(qT[j][:, 4 * part:4 * part + 4, :], bank[:, :].rearrange("p (n t) -> p n t", n=4),
                                         ACT.Copy).then_inc(taken[use[0]], 1)
                if kind == "qk":
                    bank = read(a, use)
                    nc.scalar.activation(qT[j][:, 0, :], bank[:, 0:S], ACT.Copy).then_inc(sem("q_taken"), 1)
                    if positive(b):
                        a.wait_ge(sem("k_spread"), b)
                    nc.scalar.activation(k3[:, :], bank[:, S:S + K], ACT.Copy).then_inc(taken[use[0]], 1)

            def work(kind, g, b, j):
                if kind == "X":
                        if m.masked:
                            a.wait_ge(sem(f"shifted{n}"), NG * b + (g + 1))
                        else:
                            after(a, m.use("S", g, b))
                        nc.scalar.activation(pr[:, g, :, :], sc[:, g, :, :], ACT.Exp, scale=m.scale).then_inc(sem(f"probs{n}"), 1)
                elif kind != "N":
                    use = m.use(kind, g, b)
                    if kind == "T":
                        bank = read(a, use)
                        nc.scalar.activation(pT[g][:, :, :], bank[0:K, :].rearrange("p (h t) -> p h t", h=G), ACT.Copy)\
                          .then_inc(taken[use[0]], 1)
                    if kind == "A" and m.wide:
                        bank = read(a, use)
                        for e in range(2):
                            p_ = slice(64 * e, 64 * e + 64)
                            last = nc.scalar.activation(oT[j][p_, 2 * g:2 * g + 2, :],
                                                        bank[p_, :].rearrange("p (i e t) -> p i e t", i=2, e=2)[:, :, e, :], ACT.Copy)
                        last.then_inc(taken[use[0]], 1)
                    if kind == "R":
                        bank = read(a, use)
                        nc.scalar.activation(oT[j][:, 0, :], bank[:, 0:S], ACT.Copy).then_inc(taken[use[0]], 1)
                    if kind == "Z":
                        bank = read(a, use)
                        nc.scalar.activation(zT[:, :], bank[:, 0:S], ACT.Relu).then_inc(taken[use[0]], 1)

            def extra(s, tick):
                if (s, tick) == (B, 1):
                    take_first_half(a, n)

            rounds(a, m, project, work, lambda: turn_scalar(a, f"a{n}", 1, xnT), extra)

        def mha_pool(g_, n):
            m = attn[n]

            def project(b, j, f):
                kind, part = m.fills[f]
                use = m.use("F", f, b)
                if n == 0 and kind.endswith("s"):
                    is_k = kind[0] == "k"
                    pair, width = 2 * part + is_k, K if is_k else S
                    after(g_, m.use("F", f - 1, b))
                    after(g_, use)
                    r = rope[pair % 2]
                    done = 6 * b + (0, 1, 3, 4)[pair]
                    if positive(done):
                        g_.wait_ge(sem("roped"), done)
                    if not is_k:
                        g_.tensor_tensor(qT[j][:, 4 * part:4 * part + 4, :], r[:, 0, :, :], r[:, 1, :, :], ALU.add)\
                          .then_inc(sem("roped"), 1)
                    else:
                        for e in range(2):
                            p_ = slice(64 * e, 64 * e + 64)
                            if e:
                                g_.wait_ge(sem("roped"), done + 1)
                            g_.tensor_tensor(kM[j][p_, 8 * part + e:8 * part + 8:2, :], r[p_, 0, :, 0:K], r[p_, 1, :, 0:K], ALU.add)\
                              .then_inc(sem("roped"), 1)
                if kind == "qk":
                    after(g_, use)
                    g_.tensor_tensor(kM[j][:, :, :], k3[:, :].unsqueeze(1).to_broadcast([128, H, K]),
                                     headmask[:, :].unsqueeze(2).to_broadcast([128, H, K]), ALU.mult)\
                      .then_inc(sem("k_spread"), 1)

            if n != 1:
                rounds(g_, m, project, lambda *slot: None)
                g_.wait_ge(sem("roped") if n == 0 else sem("k_spread"), 6 * B if n == 0 else B)

        SIM = 4 * K

        def coat_tensor(pe):
            def turn_weights(c_):
                bank = fill(pe, uses["aT", c_])
                pe.wait_ge(sem("a_weights"), c_ + 1)
                for i in range(4):
                    last = nc.tensor.transpose(bank[0:K, i * S:(i + 1) * S], sim[:, 4 * c_ + i, :], ident[:, :])
                last.then_inc(filled[c_], 1)

            def project_own(c_):
                bank = fill(pe, uses["own", c_])
                for i in range(4):
                    block = bank[:, i * D:(i + 1) * D]
                    nc.tensor.matmul(block, ones[0:1, :], bqv[:, :], start=True, stop=False)
                    last = nc.tensor.matmul(block, xnT[:, 4 * c_ + i, :], wqv[:, 0, :], start=False, stop=True)
                last.then_inc(filled[2 + c_], 1)

            def attend(c_):
                bank = fill(pe, uses["hq", c_])
                after(pe, uses["aT", c_])
                for i in range(4):
                    last = nc.tensor.matmul(bank[:, i * S:(i + 1) * S], cx[:, 4 * c_ + i, :], aT[c_][:, i, :], start=True, stop=True)
                last.then_inc(filled[4 + c_], 1)

            loaded(pe, "w2")
            pe.wait_ge(sem("c3"), 2)
            for c_ in range(2):
                bank = fill(pe, uses["sim", c_])
                after(pe, uses["turn", "a2", c_])
                for i in range(4):
                    b, block = 4 * c_ + i, bank[:, i * K:(i + 1) * K]
                    nc.tensor.matmul(block, xnT[:, b, :], c3[:, b, :], start=True, stop=False)
                    last = nc.tensor.matmul(block, ones[:, :], c2[:, b, :], start=False, stop=True)
                last.then_inc(filled[c_], 1)
                project_own(c_)
                if c_ == 0:
                    turn_tensor(pe, "a2", 1, xn)
            turn_weights(0)
            bank = fill(pe, uses["mT"])
            pe.wait_ge(sem("largest"), 2)
            nc.tensor.transpose(bank[0:B, 0:S], m8[:, :], ident[:, :]).then_inc(filled[6], 1)
            attend(0)
            turn_weights(1)
            attend(1)
            bank = fill(pe, uses["bT"])
            pe.wait_ge(sem("token_weights"), 1)
            nc.tensor.transpose(bank[:, 0:B], mT[:, :], ident[0:B, 0:B]).then_inc(filled[7], 1)
            bank = fill(pe, uses["hc"])
            after(pe, uses["bT"])
            for b in range(B):
                last = nc.tensor.matmul(bank[:, b:b + 1], xn[:, b, :], bT[:, b:b + 1], start=True, stop=True)
            last.then_inc(filled[6], 1)
            for b in range(B):
                bank = fill(pe, uses["feat", b])
                pe.wait_ge(sem("by_token"), b // 4 + 1)
                pe.wait_ge(sem("by_bar"), b + 1)
                for i, feature in enumerate((attended_context, times_token, times_bar)):
                    last = nc.tensor.matmul(bank[:, 0:D], feature[:, b, :], wqv[:, i + 1, :], start=i == 0, stop=i == 2)
                last.then_inc(filled[6 + b % 2], 1)

        def coat_scalar(a):
            def take(c_):
                bank = read(a, uses["aT", c_])
                nc.scalar.activation(aT[c_][:, :, :], bank[0:K, :].rearrange("p (b t) -> p b t", b=4), ACT.Copy)\
                  .then_inc(taken[c_], 1)

            def attended(c_):
                bank = read(a, uses["hq", c_])
                nc.scalar.activation(attended_context[:, 4 * c_:4 * c_ + 4, :], bank[:, :].rearrange("p (b t) -> p b t", b=4), ACT.Copy)\
                  .then_inc(taken[4 + c_], 1)

            for c_ in range(2):
                a.wait_ge(sem("a_shifted"), c_ + 1)
                half = sim[:, 4 * c_:4 * c_ + 4, :]
                nc.scalar.activation(half, half, ACT.Exp).then_inc(sem("a_exp"), 1)
            take(0)
            a.wait_ge(sem("row_max"), 1)
            nc.scalar.activation(mT[:, :], mT[:, :], ACT.Exp, bias=row1[:, 0:1], accum_out=row1[:, 1:2]).then_inc(sem("row_exp"), 1)
            take(1)
            attended(0)
            attended(1)

        def coat_vector(v, c):

            def shift(c_):
                use, half, largest = uses["sim", c_], sim[:, 4 * c_:4 * c_ + 4, :], m8[:, 4 * c_:4 * c_ + 4]
                bank = read(v, use)
                v.tensor_scalar(half, bank[:, 0:SIM].rearrange("p (b k) -> p b k", b=4), bsim[:, 0:1], None, ALU.add)\
                 .then_inc(taken[c_], 1)
                after(v, use)
                v.tensor_reduce(largest, half, AX_X, ALU.max).then_inc(sem("largest"), 1)
                v.wait_ge(sem("largest"), c_ + 1)
                v.tensor_tensor(half, half, largest.unsqueeze(2).to_broadcast([S, 4, K]), ALU.subtract).then_inc(sem("a_shifted"), 1)

            def weights(c_):
                half = sim[:, 4 * c_:4 * c_ + 4, :]
                v.wait_ge(sem("a_exp"), c_ + 1)
                c(v.tensor_reduce(z8[:, 4 * c_:4 * c_ + 4], half, AX_X, ALU.add))
                c(v.reciprocal(rz8[:, 4 * c_:4 * c_ + 4], z8[:, 4 * c_:4 * c_ + 4]))
                v.tensor_tensor(half, half, rz8[:, 4 * c_:4 * c_ + 4].unsqueeze(2).to_broadcast([S, 4, K]), ALU.mult)\
                 .then_inc(sem("a_weights"), 1)

            def by_token(c_):
                after(v, uses["hq", c_])
                v.tensor_tensor(times_token[:, 4 * c_:4 * c_ + 4, :], attended_context[:, 4 * c_:4 * c_ + 4, :],
                                xnT[:, 4 * c_:4 * c_ + 4, :], ALU.mult).then_inc(sem("by_token"), 1)

            shift(0)
            shift(1)
            weights(0)
            bank = read(v, uses["mT"])
            v.tensor_copy(mT[:, :], bank[0:B, 0:S]).then_inc(taken[6], 1)
            after(v, uses["mT"])
            v.tensor_reduce(row1[:, 0:1], mT[:, :], AX_X, ALU.max, negate=True).then_inc(sem("row_max"), 1)
            weights(1)
            v.wait_ge(sem("row_exp"), 1)
            c(v.reciprocal(row1[:, 2:3], row1[:, 1:2]))
            v.tensor_scalar(mT[:, :], mT[:, :], row1[:, 2:3], None, ALU.mult).then_inc(sem("token_weights"), 1)
            for c_ in range(2):
                bank = read(v, uses["own", c_])
                for i in range(4):
                    b = 4 * c_ + i
                    last = v.scalar_tensor_tensor(x[:, b, :], bank[:, i * D:(i + 1) * D], tg[:, 2:3], x[:, b, :], ALU.mult, ALU.add)
                last.then_inc(taken[2 + c_], 1)
                by_token(c_)
            for c_ in range(2):
                after(v, uses["own", c_])
            bank = read(v, uses["bT"])
            v.tensor_copy(bT[:, :], bank[:, 0:B]).then_inc(taken[7], 1)
            bank = read(v, uses["hc"])
            v.tensor_copy(hc[:, :], bank[:, 0:B]).then_inc(taken[6], 1)
            after(v, uses["hc"])
            for b in range(B):
                v.tensor_scalar(times_bar[:, b, :], xnT[:, b, :], hc[:, b:b + 1], None, ALU.mult).then_inc(sem("by_bar"), 1)
            for b in range(B):
                bank = read(v, uses["feat", b])
                v.scalar_tensor_tensor(x[:, b, :], bank[:, 0:D], tg[:, 2:3], x[:, b, :], ALU.mult, ALU.add)\
                 .then_inc(taken[6 + b % 2], 1)
                after(v, uses["feat", b])
                between_vector(v, c, 2, (b, 0))

        def part(i, q):
            return (q % 2, q // 2) if isinstance(i, int) and i else (q // 2, q % 2)

        def ffn_loop(eng, unit, biases=None):
            with eng.Fori(0, E // 2 - 1) as i:
                for q in range(4):
                    unit(i, q)
            if biases:
                biases()
            for q in range(4):
                unit(E // 2 - 1, q)

        def ffn_tensor(pe, n):
            blocks = HIDDEN_BLOCKS[n]
            width = 128 * blocks

            def hidden(i, q):
                j, c_ = part(i, q)
                if n != SHARED and (j, q) in ((0, 0), (1, 1), (1, 2)):
                    pe.wait_ge(sem(f"w1_split{n}"), 2 * i + (j + 1))
                if n != SHARED and isinstance(i, int) and i == 0:
                    pe.wait_ge(sem(f"tokens_split{n}"), 1)
                for nb in range(blocks):
                    use = hidden_use(n, i, q, nb)
                    bank = fill(pe, use)
                    block, half = slice(nb * 128, (nb + 1) * 128), slice(4 * c_, 4 * c_ + 4)
                    if n == SHARED:
                        last = nc.tensor.matmul(bank[:, :], wg[:, block], xnT[:, half, :], start=True, stop=True)
                    else:
                        nc.tensor.matmul(bank[:, :], w1_high[j][:, block], tokens_high[:, half, :], start=True, stop=False)
                        nc.tensor.matmul(bank[:, :], w1_high[j][:, block], tokens_low[:, half, :], start=False, stop=False)
                        last = nc.tensor.matmul(bank[:, :], w1_low[j][:, block], tokens_high[:, half, :], start=False, stop=True)
                    last.then_inc(filled[use[0]], 1)

            def outputs(i, q):
                j, c_ = part(i, q)
                h = hT[c_ if n == SHARED else q % 2]
                offset = 0 if n == SHARED else width
                if (j, q) in ((0, 0), (1, 1), (1, 2)):
                    pe.wait_ge(sem(f"ld_w2_{n}{j}"), 16 * i + 16)
                use = out_use(n, i, q)
                bank = fill(pe, use)
                for t in range(4):
                    for nb in range(blocks):
                        if n == SHARED:
                            if t == 0:
                                after(pe, hidden_use(n, 0, c_, nb))
                        elif t == 0:
                            after(pe, hidden_use(n, i, q, nb))
                        last = nc.tensor.matmul(bank[:, t * D:(t + 1) * D], h[:, nb, t * S:(t + 1) * S],
                                                we[n][j][:, offset + nb * D:offset + (nb + 1) * D],
                                                start=nb == 0, stop=nb == blocks - 1)
                last.then_inc(filled[use[0]], 1)

            def unit(i, q):
                if n != SHARED:
                    if q < 3:
                        hidden(i, q + 1)
                    elif not isinstance(i, int):
                        hidden(i + 1, 0)
                outputs(i, q)

            if n == 2:
                turn_first_half(pe, n)
                route_half(pe, n, 0)
            turn_tensor(pe, f"f{n}", 1, xn)
            route_half(pe, n, 1).then_inc(filled[uses["logits", n][0]], 1)
            if n == 3:
                turn_tensor(pe, "i3", 1, yb)
                for c_ in range(2):
                    after(pe, uses["turn", "i3", c_])
            hidden(0, 0)
            if n != SHARED:
                pe.wait_ge(sem(f"tokens_split{n}"), 2)
            if n == SHARED:
                hidden(0, 1)
                pe.wait_ge(sem("chosen"), 1)
                bank = fill(pe, uses["rank"])
                nc.tensor.matmul(bank[:, 0:E], upper[:, :], small["m"][:, 0, :], start=True, stop=True)
                nc.tensor.matmul(bank[:, E:B * E], upper[:, :], small["m"][:, 1:B, :], start=True, stop=False)
                for t in range(B - 2, -1, -1):
                    later = B - 1 - t
                    last = nc.tensor.matmul(bank[:, (t + 1) * E:B * E], ones[:, :],
                                            small["m"][:, t:t + 1, :].to_broadcast([128, later, E]),
                                            start=False, stop=t == 0, skip_group_check=t > 0)
                last.then_inc(filled[7], 1)
            def biases():
                for c_ in range(2):
                    bank = fill(pe, uses["combT", n, c_])
                    if c_ == 0:
                        pe.wait_ge(sem("combined"), n + 1)
                    for t in range(4):
                        last = nc.tensor.transpose(bank[0:E, t * S:(t + 1) * S], small["cb"][:, 4 * c_ + t, :], ident[:, :])
                    last.then_inc(filled[6 + c_], 1)
                for c_ in range(2):
                    bank = fill(pe, uses["b2", n, c_])
                    after(pe, uses["combT", n, c_])
                    for t in range(4):
                        last = nc.tensor.matmul(bank[:, t * D:(t + 1) * D], combT[:, 4 * c_ + t, :], b2[n][:, :],
                                                start=True, stop=True)
                    last.then_inc(filled[4 + c_], 1)

            ffn_loop(pe, unit, biases if n != SHARED else None)

        def ffn_scalar(a, n):
            blocks = HIDDEN_BLOCKS[n]
            func = {0: ACT.Silu, 1: ACT.Relu, 2: ACT.Gelu, 3: ACT.Relu}[n]

            def hidden(i, q):
                for nb in range(blocks):
                    use = hidden_use(n, i, q, nb)
                    bank = read(a, use)
                    if n == SHARED:
                        nc.scalar.activation(hT[q % 2][:, nb, :], bank[:, :], func).then_inc(taken[use[0]], 1)
                    else:
                        j, at = part(i, q)[0], 2 * 128 * blocks + nb
                        if nb == 0 and (j, q) in ((0, 0), (1, 1), (1, 2)):
                            a.wait_ge(sem(f"ld_b1_{n}{j}"), 16 * i + 16)
                        nc.scalar.activation(hT[q % 2][:, nb, :], bank[:, :], func, bias=we[n][j][:, at:at + 1])\
                          .then_inc(taken[use[0]], 1)

            def unit(i, q):
                if q < 3:
                    hidden(i, q + 1)
                elif not isinstance(i, int):
                    hidden(i + 1, 0)

            a.wait_ge(sem("route_max"), n + 1)
            nc.scalar.activation(small["ex"][:, :, :], small["ex"][:, :, :], ACT.Exp).then_inc(sem("route_exp"), 1)
            if n == 3:
                loaded(a, "f3")
                turn_scalar(a, "i3", 1, attended_context)
            hidden(0, 0)
            if n == SHARED:
                hidden(0, 1)
            else:
                def biases():
                    for c_ in range(2):
                        bank = read(a, uses["combT", n, c_])
                        nc.scalar.activation(combT[:, 4 * c_:4 * c_ + 4, :], bank[0:E, :].rearrange("p (t s) -> p t s", t=4),
                                             ACT.Copy).then_inc(taken[6 + c_], 1)

                ffn_loop(a, unit, biases)

        def ffn_vector(v, c, n):
            s3 = small

            def wide(tile):
                return tile[:, :].unsqueeze(2).to_broadcast([128, B, E])

            def first_largest(values, largest, chosen):
                c(v.tensor_tensor(s3["eq"][:, :, :], values[:, :, :], wide(largest), ALU.is_equal))
                c(v.tensor_tensor(s3["eq"][:, :, :], s3["eq"][:, :, :], s3["pri"][:, :, :], ALU.mult))
                c(v.tensor_reduce(col["km"][:, :], s3["eq"][:, :, :], AX_X, ALU.max))
                c(v.tensor_tensor(chosen[:, :, :], s3["eq"][:, :, :], wide(col["km"]), ALU.is_equal))

            loaded(v, f"f{n}")
            use = uses["logits", n]
            logits = read(v, use)[:, 0:B * E].rearrange("p (t e) -> p t e", t=B)
            if n == SHARED:
                v.tensor_copy(s3["L"][:, :, :], logits).then_inc(taken[6], 1)
            else:
                v.tensor_tensor(s3["L"][:, :, :], logits, br[n][:, :].unsqueeze(1).to_broadcast([128, B, E]), ALU.add)\
                 .then_inc(taken[6], 1)
            after(v, use)
            c(v.tensor_reduce(col["m1"][:, :], s3["L"][:, :, :], AX_X, ALU.max))
            v.tensor_tensor(s3["ex"][:, :, :], s3["L"][:, :, :], wide(col["m1"]), ALU.subtract).then_inc(sem("route_max"), 1)
            first_largest(s3["L"], col["m1"], s3["one1"])
            v.wait_ge(sem("route_exp"), n + 1)
            if n in (0, 3):
                c(v.tensor_reduce(col["z"][:, :], s3["ex"][:, :, :], AX_X, ALU.add))
                c(v.reciprocal(col["rz"][:, :], col["z"][:, :]))
            if n == 3:
                c(v.tensor_scalar(s3["m"][:, :, :], s3["one1"][:, :, :], tg[:, 7:8], None, ALU.mult))
                v.tensor_tensor(s3["cb"][:, :, :], s3["m"][:, :, :], wide(col["rz"]), ALU.mult).then_inc(sem("combined"), 1)
            else:
                c(v.scalar_tensor_tensor(s3["L2"][:, :, :], s3["one1"][:, :, :], -3.0e38, s3["L"][:, :, :], ALU.mult, ALU.add))
                c(v.tensor_reduce(col["m2"][:, :], s3["L2"][:, :, :], AX_X, ALU.max))
                first_largest(s3["L2"], col["m2"], s3["one2"])
                v.tensor_tensor(s3["m"][:, :, :], s3["one1"][:, :, :], s3["one2"][:, :, :], ALU.add).then_inc(sem("chosen"), 1)
                v.wait_ge(sem("chosen"), n + 1)
                if n == SHARED:
                    c(v.tensor_tensor(s3["ex"][:, :, :], s3["ex"][:, :, :], wide(col["rz"]), ALU.mult))
                c(v.tensor_tensor(s3["ex"][:, :, :], s3["ex"][:, :, :], s3["m"][:, :, :], ALU.mult))
                if n == SHARED:
                    use = uses["rank"]
                    rank = read(v, use)[:, 0:B * E].rearrange("p (t e) -> p t e", t=B)
                    v.scalar_tensor_tensor(s3["ex"][:, :, :], rank, CAPACITY + 0.5, s3["ex"][:, :, :], ALU.is_lt, ALU.mult)\
                     .then_inc(taken[7], 1)
                    after(v, use)
                c(v.tensor_reduce(col["s"][:, :], s3["ex"][:, :, :], AX_X, ALU.add))
                if n == SHARED:
                    c(v.tensor_scalar(col["s"][:, :], col["s"][:, :], 1e-6, None, ALU.add))
                c(v.reciprocal(col["km"][:, :], col["s"][:, :]))
                c(v.tensor_scalar(col["km"][:, :], col["km"][:, :], tg[:, 4 + n:5 + n], None, ALU.mult))
                v.tensor_tensor(s3["cb"][:, :, :], s3["ex"][:, :, :], wide(col["km"]), ALU.mult).then_inc(sem("combined"), 1)
            v.wait_ge(sem("combined"), n + 1)

            def unit(i, q):
                use = out_use(n, i, q)
                bank = read(v, use)
                j, c_ = part(i, q)
                if not isinstance(i, int):
                    v.wait_ge(taken[use[0]], use[1])
                elif q:
                    after(v, out_use(n, i, q - 1))
                else:
                    for k in (4, 5):
                        v.wait_ge(taken[k], out_use(n, i, k - 4)[1])
                for t in range(4):
                    tile = 4 * c_ + t
                    last = v.scalar_tensor_tensor(x[:, tile, :], bank[:, t * D:(t + 1) * D],
                                                  s3["cb"][:, tile, bass.ds(2 * i + j, 1)], x[:, tile, :], ALU.mult, ALU.add)
                last.then_inc(taken[use[0]], 1)
                if isinstance(i, int) and q % 2:
                    after(v, use)
                    if n < 3:
                        norm_half(v, c, f"a{n + 1}", c_, x, xn)

            def biases():
                for c_ in range(2):
                    use = uses["b2", n, c_]
                    bank = read(v, use)
                    v.wait_ge(taken[use[0]], use[1])
                    xs = x[:, 4 * c_:4 * c_ + 4, :]
                    v.tensor_tensor(xs, xs, bank[:, :].rearrange("p (t d) -> p t d", t=4), ALU.add).then_inc(taken[4 + c_], 1)
                if n == 1:
                    loaded(v, "w2")
                    v.tensor_scalar(c3[:, :, :], cxT[:, :, :], wsim[:, 2:3], wsim[:, 0:1], ALU.mult, ALU.add).then_inc(sem("c3"), 1)
                    v.tensor_scalar(c2[:, :, :], cxT[:, :, :], wsim[:, 1:2], None, ALU.mult).then_inc(sem("c3"), 1)
                if n == 2:
                    loaded(v, "w3")
                    c(v.tensor_scalar(bias3[:, :, :], validI[:, :, :], 0, NEG, ALU.is_equal, ALU.mult))
                    c(v.tensor_tensor(bias3[:, :, :], bias3[:, :, :], causal[:, :].unsqueeze(1).to_broadcast([S, B, K]), ALU.min))

            ffn_loop(v, unit, biases if n != SHARED else None)

        @block.gpsimd
        def _(g):
            done = sem("constants")
            g.memset(ident[:, :], 0.0).then_inc(sem("identity"), 1)
            g.memset(exponent[:, :], -0.5).then_inc(sem("identity"), 1)
            g.wait_ge(sem("identity"), 2)
            g.affine_select(out=ident[:, :], in_=ident[:, :], compare_op=ALU.not_equal, fill=1.0, base=0,
                            pattern=[[-1, 128]], channel_multiplier=1).then_inc(sem("identity"), 1)
            g.wait_ge(sem("identity"), 3)
            for j in range(2):
                g.memset(kM[j][:, :, :], 0.0).then_inc(done, 1)
            for c_ in range(2):
                norm_root(g, "a0", 4 * c_, 4 * c_ + 4)
            g.wait_ge(*rooted[-1])
            g.memset(ones[:, :], 1.0).then_inc(done, 1)
            g.memset(upper[:, :], 1.0).then_inc(done, 1)
            g.memset(headmask[:, :], 1.0).then_inc(done, 1)
            g.memset(causal[:, :], 0.0).then_inc(done, 1)
            for j in range(2):
                g.memset(va8[j][:, :, 8:9], 1.0).then_inc(done, 1)
            for e in range(E):
                g.memset(small["pri"][:, :, e:e + 1], float(E - e)).then_inc(done, 1)
            g.wait_ge(done, 8 + E)
            g.affine_select(out=upper[:, :], in_=upper[:, :], compare_op=ALU.is_ge, fill=0.0, base=0,
                            pattern=[[1, 128]], channel_multiplier=-1).then_inc(done, 1)
            g.affine_select(out=causal[:, :], in_=causal[:, :], compare_op=ALU.is_ge, fill=NEG, base=0,
                            pattern=[[-1, K]], channel_multiplier=1).then_inc(done, 1)
            g.affine_select(out=headmask[:, :], in_=headmask[:, :], compare_op=ALU.is_ge, fill=0.0, base=0,
                            pattern=[[-8, H]], channel_multiplier=1).then_inc(done, 1)
            g.wait_ge(done, 11 + E)
            g.affine_select(out=headmask[:, :], in_=headmask[:, :], compare_op=ALU.is_ge, fill=0.0, base=7,
                            pattern=[[8, H]], channel_multiplier=-1).then_inc(done, 1)
            g.wait_ge(done, 12 + E)
            for n in range(4):
                for c_ in range(2 if n else 0):
                    norm_root(g, f"a{n}", 4 * c_, 4 * c_ + 4)
                if n != 2:
                    mha_pool(g, n)
                elif n == 2:
                    g.wait_ge(*rooted[-1])
                if n != SHARED:
                    if n == 1:
                        g.wait_ge(*rooted[-1])
                    for j in range(2):
                        split_expert(g, n, 0, j)
                        g.wait_ge(sem(f"w1_split{n}"), j + 1)
                between_pool(g, n)
                if n != SHARED:
                    with g.Fori(1, E // 2) as i:
                        for j in range(2):
                            split_expert(g, n, i, j)

        CONSTANTS = 12 + E

        @block.tensor
        def _(pe):
            pe.wait_ge(sem("identity"), 3)
            loaded(pe, "cx")
            for b in range(B):
                bank = fill(pe, uses["cx", b])
                nc.tensor.transpose(bank[:, 0:K], cx[:, b, :], ident[0:K, 0:K]).then_inc(filled[b], 1)
            for n in range(4):
                turn_tensor(pe, f"a{n}", 0, xn)
                if n == 2:
                    coat_tensor(pe)
                else:
                    mha_tensor(pe, n)
                ffn_tensor(pe, n)

        @block.scalar
        def _(a):
            loaded(a, "gates")
            nc.scalar.activation(tg[:, :], gates[:, :], ACT.Tanh).then_inc(sem("tg"), 1)
            for b in range(B):
                bank = read(a, uses["cx", b])
                nc.scalar.activation(cxT[:, b, :], bank[:, 0:K], ACT.Copy).then_inc(taken[b], 1)
            for n in range(4):
                turn_scalar(a, f"a{n}", 0, xnT)
                if n == 2:
                    turn_scalar(a, "a2", 1, xnT)
                    coat_scalar(a)
                else:
                    mha_scalar(a, n)
                if n == 0:
                    after(a, attn[0].use("Y", 0, B - 1))
                    for dst, src in late_plan:
                        nc.scalar.dma_start(dst, src).then_inc(sem("ld_late"), 16)
                if n == 2:
                    take_first_half(a, n)
                turn_scalar(a, f"f{n}", 1, xnT)
                ffn_scalar(a, n)

        @block.vector
        def _(v):
            c = Chain(v, sem("vector"))
            for c_ in range(2):
                loaded(v, f"x{c_}")
                norm_half(v, c, "a0", c_, x, xn)
            loaded(v, "cos")
            for n in range(4):
                if n == 1:
                    loaded(v, "w1")
                    c(v.tensor_scalar(gamma[:, :], gamma[:, :], tg[:, 1:2], None, ALU.mult))
                if n == 2:
                    coat_vector(v, c)
                else:
                    mha_vector(v, c, n)
                ffn_vector(v, c, n)


def kernel(**inputs):
    import numpy as _np
    import concourse.bacc as _bacc
    from concourse.bass_utils import run_bass_kernel_spmd as _run

    given = {n: _np.asarray(a) for n, a in inputs.items()}
    plain = ["x", "ctx_1024", "mask_BxSxS2_ik0", "mask_BxS2_if1", "g_xattn", "g_ffn", "L0_xattn_Wq", "L0_xattn_Wk",
             "L0_xattn_Wv", "L0_xattn_Wo", "L1_xattn_w_kv", "L1_xattn_w_q", "L1_xattn_w_out1", "L1_xattn_w_out2",
             "L1_xattn_gamma", "L1_ffn_Wg", "L1_ffn_bg", "L1_ffn_b2", "L2_xattn_b_sim", "L2_xattn_W_qv", "L2_xattn_b_qv",
             "L2_ffn_gate_b", "L2_ffn_b2", "L3_ffn_Wr", "L3_ffn_br", "L3_ffn_b2"]
    arrays = {n: given[n] for n in plain}
    for n in ("L0_ffn_w_router", "L0_ffn_w_gate", "L2_ffn_gate_w", "L3_xattn_Wq", "L3_xattn_Wk", "L3_xattn_Wv", "L3_xattn_Wo"):
        arrays[n] = given[n].T
    for n in ("L0_xattn_Wq", "L0_xattn_Wk"):
        arrays[n + "_swapped"] = given[n].reshape(D, -1, 2)[:, :, ::-1].reshape(D, -1)
    arrays["L2_xattn_w_sim"] = given["L2_xattn_w_sim"].reshape(3, D).T
    arrays["L3_ffn_ln"] = _np.stack([given["L3_ffn_ln_g"], given["L3_ffn_ln_b"]], axis=1)

    def rows(a):
        e, r, m = a.shape
        return a.reshape(e, r // 128, 128, m).transpose(0, 2, 1, 3).reshape(e, 128, -1)

    arrays["L0_experts"] = rows(given["L0_ffn_w_down"].transpose(0, 2, 1))
    for n, (w1, b1, w2) in {1: ("W1", "b1", "W2"), 2: ("w1", "b1", "w2"), 3: ("W1", "b1", "W2")}.items():
        w1, b1, w2 = (given[f"L{n}_ffn_{k}"] for k in (w1, b1, w2))
        arrays[f"L{n}_experts"] = _np.concatenate([w1, rows(w2), rows(b1[:, :, None])], axis=2)

    inv = (1.0 / _np.float32(10000.0) ** (_np.arange(0, 64, 2, dtype=_np.float32) / _np.float32(64))).astype(_np.float32)
    angle = (_np.arange(S, dtype=_np.float32)[:, None] * inv).astype(_np.float32).T
    sign = _np.array([-1.0, 1.0], _np.float32)[None, :, None]
    one_head = [_np.repeat(_np.cos(angle)[:, None], 2, axis=1).reshape(64, S),
                (_np.sin(angle)[:, None] * sign).reshape(64, S)]
    arrays["rope_cos"], arrays["rope_sin"] = (_np.tile(a, (2, 1)).astype(_np.float32) for a in one_head)

    nc = _bacc.Bacc("TRN2", target_bir_lowering=False, num_devices=1)
    aps, feed = {}, {}
    for n, a in arrays.items():
        a = _np.ascontiguousarray(a)
        feed[f"in_{n}"] = a
        aps[n] = nc.dram_tensor(f"in_{n}", a.shape, mybir.dt.from_np(a.dtype), kind="ExternalInput").ap()
    out = nc.dram_tensor("out_0", (B, S, D), F32, kind="ExternalOutput").ap()
    build(nc, aps, out)
    r = _run(nc, [feed], core_ids=[0])
    return r.results[0]["out_0"]
```
